# Optimizing a Trainium2 kernel written in Bass

```python
import numpy as np
import jax
import jax.numpy as jnp

def _softmax(x, axis=-1):
    return jax.nn.softmax(x, axis=axis)

def _gelu(x):
    return jax.nn.gelu(x, approximate=True)

def _silu(x):
    return jax.nn.silu(x)

def _sigmoid(x):
    return jax.nn.sigmoid(x)

def _layernorm(x, axis=-1, eps=1e-05):
    m = jnp.mean(x, axis=axis, keepdims=True)
    v = jnp.var(x, axis=axis, keepdims=True)
    return (x - m) / jnp.sqrt(v + eps)

def _scatter_add(tgt, idx, src, axis=0):
    return tgt.at[idx].add(src)

def _segment_sum(src, seg, n):
    return jax.ops.segment_sum(src, seg, n)
kernel_name = 'mk_vit_tower_postln_d1_tok_img256_r4_14af04'

def setup_inputs(seed: int=0):
    np.random.seed(seed)
    _w = jnp.asarray

    def _rec_inputs():
        import jax
        import jax.numpy as jnp
        _rk = jax.random.key(seed)
        x = -4.65018e-05 + 0.999886 * jax.random.normal(jax.random.fold_in(_rk, 1), (128, 3, 128, 128), jnp.float32)
        return x
    x = _rec_inputs()

    def _L0_tok_setup():
        import jax, jax.numpy as jnp
        import numpy as np
        B = 64
        IMG = 128
        P = 32
        DIM = 64
        DEPTH = 4
        HEADS = 4
        DH = 64
        MLP = 128
        PD = 3 * P * P
        GRID = IMG // P
        NPATCH = GRID * GRID

        def _ln(x, g, b):
            m = jnp.mean(x, -1, keepdims=True)
            v = jnp.mean((x - m) ** 2, -1, keepdims=True)
            return (x - m) * jax.lax.rsqrt(v + 1e-05) * g + b
        key = jax.random.key(seed)
        ks = jax.random.split(key, 10)

        def n(k, shape, s=0.02):
            return jax.random.normal(k, shape, jnp.float32) * s
        return {'img': jax.random.normal(ks[0], (B, 3, IMG, IMG), jnp.float32), 'ln_p1_g': jnp.ones((PD,), jnp.float32), 'ln_p1_b': jnp.zeros((PD,), jnp.float32), 'W_patch': n(ks[1], (PD, DIM)), 'b_patch': jnp.zeros((DIM,), jnp.float32), 'ln_p2_g': jnp.ones((DIM,), jnp.float32), 'ln_p2_b': jnp.zeros((DIM,), jnp.float32), 'cls': n(ks[2], (1, 1, DIM), 1.0), 'pos': n(ks[3], (1, NPATCH + 1, DIM), 1.0), 'attn_ln_g': jnp.ones((DEPTH, DIM), jnp.float32), 'attn_ln_b': jnp.zeros((DEPTH, DIM), jnp.float32), 'Wqkv': n(ks[4], (DEPTH, DIM, 3 * HEADS * DH)), 'Wo': n(ks[5], (DEPTH, HEADS * DH, DIM)), 'bo': jnp.zeros((DEPTH, DIM), jnp.float32), 'ff_ln_g': jnp.ones((DEPTH, DIM), jnp.float32), 'ff_ln_b': jnp.zeros((DEPTH, DIM), jnp.float32), 'W1': n(ks[6], (DEPTH, DIM, MLP)), 'b1': jnp.zeros((DEPTH, MLP), jnp.float32), 'W2': n(ks[7], (DEPTH, MLP, DIM)), 'b2': jnp.zeros((DEPTH, DIM), jnp.float32), 'ln_f_g': jnp.ones((DIM,), jnp.float32), 'ln_f_b': jnp.zeros((DIM,), jnp.float32)}
    _L0_tok_all = _L0_tok_setup()
    _L0_tok_in = {k: v for k, v in _L0_tok_all.items() if k in ('ln_p1_g', 'ln_p1_b', 'W_patch', 'b_patch', 'ln_p2_g', 'ln_p2_b', 'cls', 'pos', 'attn_ln_g', 'attn_ln_b', 'Wqkv', 'Wo', 'bo', 'ff_ln_g', 'ff_ln_b', 'W1', 'b1', 'W2', 'b2', 'ln_f_g', 'ln_f_b')}
    del _L0_tok_all

    def _L0_attn_setup():
        import jax, jax.numpy as jnp
        import numpy as np
        B, S, E, U = (4, 1024, 64, 128)
        NEG_FILL = -2.0 ** 32 + 1.0

        def _lrelu(z):
            return jnp.where(z >= 0, z, 0.2 * z)
        key = jax.random.key(seed)
        ks = jax.random.split(key, 4)
        sc_in = 1.0 / np.sqrt(E)
        return {'x': jax.random.normal(ks[0], (B, S, E), dtype=jnp.float32), 'Wq': jax.random.normal(ks[1], (E, U), dtype=jnp.float32) * sc_in, 'bq': jnp.zeros((U,), dtype=jnp.float32), 'Wk': jax.random.normal(ks[2], (E, U), dtype=jnp.float32) * sc_in, 'bk': jnp.zeros((U,), dtype=jnp.float32), 'Wv': jax.random.normal(ks[3], (E, E), dtype=jnp.float32) * sc_in, 'bv': jnp.zeros((E,), dtype=jnp.float32), 'gamma': jnp.ones((E,), dtype=jnp.float32), 'beta': jnp.zeros((E,), dtype=jnp.float32)}
    _L0_attn_all = _L0_attn_setup()
    _L0_attn_in = {k: v for k, v in _L0_attn_all.items() if k in ('Wq', 'bq', 'Wk', 'bk', 'Wv', 'bv', 'gamma', 'beta')}
    del _L0_attn_all

    def _L0_ffn_setup():
        import jax, jax.numpy as jnp
        import numpy as np
        B, S, D = (8, 1024, 64)
        H = 4 * D
        CAPACITY = 0.5
        key = jax.random.key(seed)
        ks = jax.random.split(key, 6)
        x = jax.random.normal(ks[0], (B, S, D), dtype=jnp.float32)
        attention_mask = jnp.zeros((B, 1, 1, S), dtype=jnp.float32)
        wr = jax.random.normal(ks[1], (D, 1), dtype=jnp.float32) * 0.02
        br = jnp.zeros((1,), dtype=jnp.float32)
        w1 = jax.random.normal(ks[2], (D, H), dtype=jnp.float32) * 0.02
        b1 = jnp.zeros((H,), dtype=jnp.float32)
        w2 = jax.random.normal(ks[3], (H, D), dtype=jnp.float32) * 0.02
        b2 = jnp.zeros((D,), dtype=jnp.float32)
        return {'x': x, 'attention_mask': attention_mask, 'wr': wr, 'br': br, 'w1': w1, 'b1': b1, 'w2': w2, 'b2': b2}
    _L0_ffn_all = _L0_ffn_setup()
    _L0_ffn_in = {k: v for k, v in _L0_ffn_all.items() if k in ('attention_mask', 'wr', 'br', 'w1', 'b1', 'w2', 'b2')}
    del _L0_ffn_all
    return {'x': x, 'L0_tok_ln_p1_g': _L0_tok_in['ln_p1_g'], 'L0_tok_ln_p1_b': _L0_tok_in['ln_p1_b'], 'L0_tok_W_patch': _L0_tok_in['W_patch'], 'L0_tok_b_patch': _L0_tok_in['b_patch'], 'L0_tok_ln_p2_g': _L0_tok_in['ln_p2_g'], 'L0_tok_ln_p2_b': _L0_tok_in['ln_p2_b'], 'L0_tok_cls': _L0_tok_in['cls'], 'L0_tok_pos': _L0_tok_in['pos'], 'L0_tok_attn_ln_g': _L0_tok_in['attn_ln_g'], 'L0_tok_attn_ln_b': _L0_tok_in['attn_ln_b'], 'L0_tok_Wqkv': _L0_tok_in['Wqkv'], 'L0_tok_Wo': _L0_tok_in['Wo'], 'L0_tok_bo': _L0_tok_in['bo'], 'L0_tok_ff_ln_g': _L0_tok_in['ff_ln_g'], 'L0_tok_ff_ln_b': _L0_tok_in['ff_ln_b'], 'L0_tok_W1': _L0_tok_in['W1'], 'L0_tok_b1': _L0_tok_in['b1'], 'L0_tok_W2': _L0_tok_in['W2'], 'L0_tok_b2': _L0_tok_in['b2'], 'L0_tok_ln_f_g': _L0_tok_in['ln_f_g'], 'L0_tok_ln_f_b': _L0_tok_in['ln_f_b'], 'L0_attn_Wq': _L0_attn_in['Wq'], 'L0_attn_bq': _L0_attn_in['bq'], 'L0_attn_Wk': _L0_attn_in['Wk'], 'L0_attn_bk': _L0_attn_in['bk'], 'L0_attn_Wv': _L0_attn_in['Wv'], 'L0_attn_bv': _L0_attn_in['bv'], 'L0_attn_gamma': _L0_attn_in['gamma'], 'L0_attn_beta': _L0_attn_in['beta'], 'L0_ffn_attention_mask': _L0_ffn_in['attention_mask'], 'L0_ffn_wr': _L0_ffn_in['wr'], 'L0_ffn_br': _L0_ffn_in['br'], 'L0_ffn_w1': _L0_ffn_in['w1'], 'L0_ffn_b1': _L0_ffn_in['b1'], 'L0_ffn_w2': _L0_ffn_in['w2'], 'L0_ffn_b2': _L0_ffn_in['b2']}

def reference(x, L0_tok_ln_p1_g, L0_tok_ln_p1_b, L0_tok_W_patch, L0_tok_b_patch, L0_tok_ln_p2_g, L0_tok_ln_p2_b, L0_tok_cls, L0_tok_pos, L0_tok_attn_ln_g, L0_tok_attn_ln_b, L0_tok_Wqkv, L0_tok_Wo, L0_tok_bo, L0_tok_ff_ln_g, L0_tok_ff_ln_b, L0_tok_W1, L0_tok_b1, L0_tok_W2, L0_tok_b2, L0_tok_ln_f_g, L0_tok_ln_f_b, L0_attn_Wq, L0_attn_bq, L0_attn_Wk, L0_attn_bk, L0_attn_Wv, L0_attn_bv, L0_attn_gamma, L0_attn_beta, L0_ffn_attention_mask, L0_ffn_wr, L0_ffn_br, L0_ffn_w1, L0_ffn_b1, L0_ffn_w2, L0_ffn_b2):
    import jax
    import jax.numpy as jnp

    def _L0_tok_ref(img, ln_p1_g, ln_p1_b, W_patch, b_patch, ln_p2_g, ln_p2_b, cls, pos, attn_ln_g, attn_ln_b, Wqkv, Wo, bo, ff_ln_g, ff_ln_b, W1, b1, W2, b2, ln_f_g, ln_f_b):
        import jax, jax.numpy as jnp
        import numpy as np
        B = 64
        IMG = 128
        P = 32
        DIM = 64
        DEPTH = 4
        HEADS = 4
        DH = 64
        MLP = 128
        PD = 3 * P * P
        GRID = IMG // P
        NPATCH = GRID * GRID

        def _ln(x, g, b):
            m = jnp.mean(x, -1, keepdims=True)
            v = jnp.mean((x - m) ** 2, -1, keepdims=True)
            return (x - m) * jax.lax.rsqrt(v + 1e-05) * g + b
        Bsz = img.shape[0]
        x = img.reshape(Bsz, 3, GRID, P, GRID, P)
        x = x.transpose(0, 2, 4, 1, 3, 5).reshape(Bsz, NPATCH, PD)
        x = _ln(x, ln_p1_g, ln_p1_b) @ W_patch + b_patch
        x = _ln(x, ln_p2_g, ln_p2_b)
        x = jnp.concatenate([jnp.broadcast_to(cls, (Bsz, 1, DIM)), x], axis=1) + pos
        scale = DH ** (-0.5)
        for i in range(DEPTH):
            h = _ln(x, attn_ln_g[i], attn_ln_b[i])
            qkv = h @ Wqkv[i]
            q, k, v = jnp.split(qkv, 3, axis=-1)

            def to_heads(t):
                return t.reshape(Bsz, -1, HEADS, DH).transpose(0, 2, 1, 3)
            q, k, v = (to_heads(q), to_heads(k), to_heads(v))
            a = jax.nn.softmax(jnp.einsum('bhqd,bhkd->bhqk', q, k) * scale, axis=-1)
            o = jnp.einsum('bhqk,bhkd->bhqd', a, v)
            o = o.transpose(0, 2, 1, 3).reshape(Bsz, -1, HEADS * DH)
            x = x + o @ Wo[i] + bo[i]
            h = _ln(x, ff_ln_g[i], ff_ln_b[i])
            x = x + jax.nn.gelu(h @ W1[i] + b1[i], approximate=False) @ W2[i] + b2[i]
        return _ln(x, ln_f_g, ln_f_b)

    def _L0_attn_ref(x, Wq, bq, Wk, bk, Wv, bv, gamma, beta):
        import jax, jax.numpy as jnp
        import numpy as np
        B, S, E, U = (4, 1024, 64, 128)
        NEG_FILL = -2.0 ** 32 + 1.0

        def _lrelu(z):
            return jnp.where(z >= 0, z, 0.2 * z)
        num_units = Wq.shape[-1]
        q = _lrelu(jnp.einsum('bse,eu->bsu', x, Wq) + bq)
        k = _lrelu(jnp.einsum('bse,eu->bsu', x, Wk) + bk)
        v = _lrelu(jnp.einsum('bse,ef->bsf', x, Wv) + bv)
        scores = jnp.einsum('bqu,bku->bqk', q, k) / jnp.sqrt(jnp.asarray(num_units, dtype=x.dtype))
        key_mask = jnp.sign(jnp.sum(jnp.abs(x), axis=-1))
        masked = jnp.where(key_mask[:, None, :] == 0, jnp.asarray(NEG_FILL, dtype=x.dtype), scores)
        probs = jax.nn.softmax(masked, axis=-1)
        out = jnp.einsum('bqk,bkf->bqf', probs, v) + x
        mean = jnp.mean(out, axis=-1, keepdims=True)
        var = jnp.mean(jnp.square(out - mean), axis=-1, keepdims=True)
        normalized = (out - mean) / jnp.sqrt(var + 1e-08)
        return gamma * normalized + beta

    def _L0_ffn_ref(x, attention_mask, wr, br, w1, b1, w2, b2):
        import jax, jax.numpy as jnp
        import numpy as np
        B, S, D = (8, 1024, 64)
        H = 4 * D
        CAPACITY = 0.5
        b, s, d = x.shape
        weights = (jnp.einsum('bsd,do->bso', x, wr) + br)[..., 0]
        k = max(1, int(CAPACITY * s))
        kk = k - 1 if k > 1 else 1
        _, idx = jax.lax.top_k(weights, k)
        sel_idx = idx[:, :kk]
        sel = jnp.take_along_axis(x, sel_idx[:, :, None], axis=1)
        h = jax.nn.gelu(jnp.einsum('bkd,dh->bkh', sel, w1) + b1)
        y = jnp.einsum('bkh,hd->bkd', h, w2) + b2
        w_sel = jnp.take_along_axis(weights, sel_idx, axis=1)
        y = y * w_sel[..., None]
        batch_idx = jnp.arange(b)[:, None]
        processed = jnp.zeros_like(x).at[batch_idx, sel_idx].set(y)
        return processed + x
    h = _L0_tok_ref(x, L0_tok_ln_p1_g, L0_tok_ln_p1_b, L0_tok_W_patch, L0_tok_b_patch, L0_tok_ln_p2_g, L0_tok_ln_p2_b, L0_tok_cls, L0_tok_pos, L0_tok_attn_ln_g, L0_tok_attn_ln_b, L0_tok_Wqkv, L0_tok_Wo, L0_tok_bo, L0_tok_ff_ln_g, L0_tok_ff_ln_b, L0_tok_W1, L0_tok_b1, L0_tok_W2, L0_tok_b2, L0_tok_ln_f_g, L0_tok_ln_f_b)
    h = _layernorm(h + _L0_attn_ref(h, L0_attn_Wq, L0_attn_bq, L0_attn_Wk, L0_attn_bk, L0_attn_Wv, L0_attn_bv, L0_attn_gamma, L0_attn_beta), axis=-1)
    h = _layernorm(h + _L0_ffn_ref(h, L0_ffn_attention_mask, L0_ffn_wr, L0_ffn_br, L0_ffn_w1, L0_ffn_b1, L0_ffn_w2, L0_ffn_b2), axis=-1)
    return h

_drawn_inputs = setup_inputs


def setup_inputs(seed=0):
    import zlib

    import numpy as np

    out = dict(_drawn_inputs(seed))
    spreads = {'L0_tok_ln_p1_g': (1.0, 0.2),
     'L0_tok_ln_p1_b': (0.0, 0.1),
     'L0_tok_b_patch': (0.0, 0.1),
     'L0_tok_ln_p2_g': (1.0, 0.2),
     'L0_tok_ln_p2_b': (0.0, 0.1),
     'L0_tok_attn_ln_g': (1.0, 0.6),
     'L0_tok_attn_ln_b': (0.0, 0.8),
     'L0_tok_bo': (0.0, 0.1),
     'L0_tok_ff_ln_g': (1.0, 0.6),
     'L0_tok_ff_ln_b': (0.0, 0.8),
     'L0_tok_b1': (0.0, 0.457),
     'L0_tok_b2': (0.0, 0.1),
     'L0_tok_ln_f_g': (1.0, 0.2),
     'L0_tok_ln_f_b': (0.0, 0.1),
     'L0_attn_bq': (0.0, 0.8),
     'L0_attn_bk': (0.0, 0.8),
     'L0_attn_bv': (0.0, 0.1),
     'L0_attn_gamma': (1.0, 0.2),
     'L0_attn_beta': (0.0, 0.1),
     'L0_ffn_b1': (0.0, 0.8),
     'L0_ffn_b2': (0.0, 0.8)}
    factors = {'L0_tok_Wo': 2.815, 'L0_ffn_wr': 8.0, 'L0_ffn_w1': 8.0, 'L0_ffn_w2': 8.0}
    for name, (base, spread) in spreads.items():
        noise = np.random.default_rng([zlib.crc32(name.encode()), seed]).standard_normal(out[name].shape)
        drawn = base * np.exp(spread * noise) if base else spread * noise
        out[name] = jnp.asarray(drawn.astype(out[name].dtype))
    for name, factor in factors.items():
        out[name] = (out[name] * factor).astype(out[name].dtype)
    return out
```

```python
import concourse.bass as bass
from concourse import mybir
from contextlib import ExitStack

B, CH, IMG, P = 128, 3, 128, 32
GRID = IMG // P
NP = GRID * GRID
TOK = NP + 1
DIM, DEPTH, HEADS, MLP, UNITS, HID = 64, 4, 4, 128, 128, 256
PD = CH * P * P
KP = CH * P
NPAIR = B // 2
COLS = NPAIR * TOK
NCH = 8
CP = NPAIR // NCH
CC = CP * TOK
PC = CP * NP
KSEL = int(0.5 * TOK) - 1
NEG = -2.0 ** 32 + 1.0
LOADS = 2 * CH * GRID
PAR_LOADS = 43

f32 = mybir.dt.float32
ALU = mybir.AluOpType
ACT = mybir.ActivationFunctionType
AX = mybir.AxisListType


def vit_tower(nc, a, out):
    with ExitStack() as ctx:
        def sb(name, *shape):
            return ctx.enter_context(nc.sbuf_tensor(name, list(shape), f32))

        class Signals(dict):
            def __missing__(self, name):
                self[name] = ctx.enter_context(nc.semaphore("s_" + name))
                return self[name]

        s = Signals()

        ps = ctx.enter_context(nc.psum_tensor("ps", [128, 8, 512], f32))

        ident = sb("ident", 128, 128)
        ones = sb("ones", 128, 128)
        ones_bd = sb("ones_bd", 128, 128)
        cen_bd = sb("cen_bd", 128, 128)
        ones_q = sb("ones_q", 128, 2, 32)
        eps5 = sb("eps5", 128, 1)
        eps8 = sb("eps8", 128, 1)
        col = sb("col", 128, 12)
        B_PATCH, G2, B2P, CLS, FG, FB, GAMMA, BETA, BV, FB2, WR, BR = range(12)
        posT = sb("posT", 128, TOK)
        lay = sb("lay", 128, 7, DEPTH)
        GA, BA, GF, BF, BO, B2, B1 = range(7)
        bo_c = sb("bo_c", 128, DEPTH)
        b2_c = sb("b2_c", 128, DEPTH)
        b1_f = sb("b1_f", 128, DEPTH)
        cur = sb("cur", 128, 3)
        arena = sb("arena", 128, 16384)
        xin = arena[0:KP, :].rearrange("p (u f m w) -> p u f m w", u=2, f=2, m=CP)
        o = 0

        def part(n):
            nonlocal o
            o += n
            return arena[:, o - n:o]

        U = part(HEADS * COLS).rearrange("p (h n) -> p h n", h=HEADS)
        G = part(HEADS * COLS).rearrange("p (h m t) -> p h m t", h=HEADS, m=NPAIR)
        htok = part(32 * 128).rearrange("p (i c) -> p i c", i=32)
        h = part(COLS)
        sq = part(COLS)
        arena2 = sb("arena2", 128, 8192)
        sqp = arena2[0:KP, 0:4096].rearrange("p (u n) -> p u n", u=2)
        half_sum = arena2[0:KP, 4096:6144].rearrange("p (u n) -> p u n", u=2)
        wtmp = arena2[0:KP, 6144:8192].rearrange("p (k d) -> p k d", k=P)
        ex = arena2[:, 0:2176].rearrange("p (g k) -> p g k", k=TOK)
        z = arena2[:, 2176:4352].rearrange("p (f n) -> p f n", f=2)
        lnv = arena2[:, 4352:5440]
        rstd = arena2[:, 5440:6528]
        nrm = arena2[:, 6528:7616]
        psq = sb("psq", KP, 2, 2 * PC)
        psm = sb("psm", KP, 2, 2 * PC)
        wp = sb("wp", KP, P, DIM)
        gp = sb("gp", KP, 2, P)
        wred = sb("wred", KP, 3 * DIM)
        cst = sb("cst", 128, 4)
        x0 = sb("x0", 128, NPAIR, TOK)
        x = sb("x", 128, COLS)
        pt = sb("pt", 128, 32 * HEADS, 32)
        wqkv = pt[0:64, 0:DEPTH * 24, :].rearrange("p (l g) k -> p l (g k)", l=DEPTH)
        wo = sb("wo", 128, DEPTH * 2, DIM)
        wo_r = sb("wo_r", 128, DEPTH * 2)
        w1 = sb("w1", 128, DEPTH, MLP)
        w1f = sb("w1f", 128, DEPTH, MLP)
        w2 = sb("w2", 128, DEPTH, DIM)
        w2_r = sb("w2_r", 128, DEPTH)
        wT = sb("wT", 128, 6, DIM)
        mu_all = sb("mu_all", 128, DEPTH, HEADS * 128)
        vo_all = sb("vo_all", 128, DEPTH, HEADS * 128)
        mu = sb("mu", 128, HEADS * 128)
        vo = sb("vo", 128, HEADS * 128)
        w1s = sb("w1s", 128, MLP)
        w2s = sb("w2s", 128, DIM)
        hbd = sb("hbd", 128, NPAIR, 2, 32)
        mx = sb("mx", 128, 32 * HEADS)
        sm = sb("sm", 128, 32 * HEADS)
        ri = sb("ri", 128, 32 * HEADS)
        pn = sb("pn", 128, 32 * HEADS, 32)
        yraw = pn[:, 0:32, :].rearrange("p a b -> p (a b)")
        sraw = hbd[:, 0:32, :, :].rearrange("p m f k -> p (m f k)").rearrange("p (k n) -> p k n", k=NCH)

        pm2, pvar, pln, prs = (U[:, k, 0:NPAIR * NP] for k in range(4))
        py = arena[:, HEADS * COLS:HEADS * COLS + NPAIR * NP]
        wqk = sb("wqk", 128, 2, UNITS)
        wv = sb("wv", 128, 128)
        fw1 = sb("fw1", 128, HID)
        fw2 = sb("fw2", 128, 2, DIM)
        fcol = sb("fcol", 128, 4)
        wrb = sb("wrb", 128, 128)
        tri = sb("tri", 128, TOK, TOK)
        gt = sb("gt", 128, 2, TOK, TOK)
        wimg = sb("wimg", 128, TOK)
        rank = sb("rank", 128, TOK)
        FIN_LOADS = 14
        NT = -(-COLS // 128)
        Q = arena[:, 0:2 * COLS].rearrange("p (f n) -> p f n", f=2)
        K = arena[:, 2 * COLS:4 * COLS].rearrange("p (f n) -> p f n", f=2)
        g_flat = arena[:, 4 * COLS:8 * COLS].rearrange("p (k n) -> p k n", k=4)
        nm, oo, rc, h1 = (g_flat[:, k, :] for k in range(4))
        wb = x
        selrow = z[:, 0, :]
        sel64 = z[:, 1, :]
        z2 = oo
        obuf = htok[:, 0:NT, :]

        def final_sp(sp):
            sp.wait_ge(s["ws"], NCH)
            for f in range(2):
                sp.dma_start(wimg[64 * f:64 * f + 64, :], wb[64 * f:64 * f + 1, :].rearrange("o (m t) -> o m t", t=TOK)).then_inc(s["sel_img"], 16)
            sp.wait_ge(s["selm"], 1)
            sp.wait_ge(s["sel_zero"], 1)
            for f in range(2):
                sp.dma_start(selrow[64 * f:64 * f + 1, :].rearrange("o (m t) -> o m t", t=TOK), wimg[64 * f:64 * f + 64, :]).then_inc(s["sel_row"], 16)
            rows = out.rearrange("(f m) t d -> (m t) f d", f=2)
            for t in range(NT):
                w = min(128, COLS - 128 * t)
                sp.wait_ge(s["oo"], t + 1)
                sp.dma_start(rows[128 * t:128 * t + w, :, :], obuf[0:w, t, :].rearrange("p (f d) -> p f d", f=2)).then_inc(s["out_done"], 16)
            sp.wait_ge(s["out_done"], 16 * NT)

        def ln_exp(act, c, psv, eps, var, ln, rs):
            act.wait_ge(s[var], c + 1)
            act.activation(chunk(lnv, c), psv, ACT.Ln, bias=eps).then_inc(s[ln], 1)
            act.wait_ge(s[ln], c + 1)
            act.activation(chunk(rstd, c), chunk(lnv, c), ACT.Exp, scale=-0.5).then_inc(s[rs], 1)

        def final_act(act):
            act.preload_act_table_set("natural_log_exp_and_others")
            for c in range(NCH):
                act.wait_ge(s["ff"], (DEPTH + 1) * NCH)
                act.activation(chunk(sq, c), chunk(x, c), ACT.Square).then_inc(s["dsq"], 1)
            for c in range(NCH):
                ln_exp(act, c, ps_v(c), eps5[:, :], "dvar", "dln", "drs")
            act.wait_ge(s["fin_in"], 16 * FIN_LOADS)
            for c in range(NCH):
                act.wait_ge(s["dh"], c + 1)
                act.activation(chunk(sq, c), chunk(h, c), ACT.Abs).then_inc(s["ka"], 1)
            for c in range(NCH):
                act.wait_ge(s["qps"], c + 1)
                act.activation(Q[:, :, c * CC:(c + 1) * CC], ps_g(c)[:, :, 0:CC], ACT.Identity, bias=fcol[:, 0:1]).then_inc(s["qa"], 1)
                act.activation(K[:, :, c * CC:(c + 1) * CC], ps_g(c)[:, :, CC:2 * CC], ACT.Identity, bias=fcol[:, 1:2]).then_inc(s["qa"], 1)
                act.wait_ge(s["vps"], c + 1)
                act.activation(chunk(nrm, c), ps_o(c), ACT.Identity, bias=col[:, BV:BV + 1]).then_inc(s["va"], 1)
            for c in range(NCH):
                act.wait_ge(s["vtp"], c + 1)
                act.activation(htok[:, 4 * c:4 * c + 4, :], ps_t(c).rearrange("p (i c) -> p i c", i=4), ACT.Copy).then_inc(s["vtk"], 1)
                act.wait_ge(s["dsub"], c + 1)
                act.activation(ex[:, 4 * c:4 * c + 4, :], ex[:, 4 * c:4 * c + 4, :], ACT.Exp, scale=UNITS ** -0.5).then_inc(s["dex"], 1)

            def centred(ready, copied, squared):
                for c in range(NCH):
                    act.wait_ge(s[ready], c + 1)
                    act.activation(chunk(rc, c), ps_v(c), ACT.Copy).then_inc(s[copied], 1)
                    act.activation(chunk(sq, c), ps_v(c), ACT.Square).then_inc(s[squared], 1)

            centred("oc", "ocs", "osq")
            for c in range(NCH):
                ln_exp(act, c, ps_o(c), eps8[:, :], "ovar", "oln", "ors")
            centred("rc", "rcs", "rsq")
            for c in range(NCH):
                ln_exp(act, c, ps_o(c), eps5[:, :], "rvar", "rln", "rrs")
            for c in range(NCH):
                act.wait_ge(s["fz"], c + 1)
                for g in range(2):
                    act.activation(U[:, 2 * g:2 * g + 2, c * CC:(c + 1) * CC], ps_g(c)[:, :, g * CC:(g + 1) * CC], ACT.Gelu_apprx_tanh,
                                   bias=fcol[:, 2 + g:3 + g]).then_inc(s["fg"], 1)
            act.preload_act_table_set("natural_log_exp_and_others")
            centred("zc", "zcs", "zsq")
            for c in range(NCH):
                ln_exp(act, c, ps_o(c), eps5[:, :], "zvar", "zln", "zrs")
            for t in range(NT):
                w = min(128, COLS - 128 * t)
                act.wait_ge(s["ops2"], t + 1)
                act.activation(obuf[0:w, t, :], ps[0:w, t % 4, 0:128], ACT.Copy).then_inc(s["oo"], 1)

        def final_pe(pe):
            for c in range(NCH):
                pe.wait_ge(s["dsq"], c + 1)
                if c >= 2:
                    pe.wait_ge(s["dln"], c - 1)
                pe.matmul(ps_v(c), ones_bd[:, :], chunk(sq, c), start=True, stop=True).then_inc(s["dvar"], 1)
            pe.wait_ge(s["fin_in"], 16 * FIN_LOADS)
            for c in range(NCH):
                pe.wait_ge(s["dh"], c + 1)
                if c >= 2:
                    pe.wait_ge(s["qa"], 2 * (c - 1))
                    pe.wait_ge(s["va"], (c - 1))
                for w in range(2):
                    for f in range(2):
                        r = slice(64 * f, 64 * f + 64)
                        mm = pe.matmul(ps_g(c)[:, f, w * CC:(w + 1) * CC], wqk[r, w, :], h[r, c * CC:(c + 1) * CC], start=True, stop=True)
                mm.then_inc(s["qps"], 1)
                pe.matmul(ps_o(c), wv[:, :], chunk(h, c), start=True, stop=True).then_inc(s["vps"], 1)
            for c in range(NCH):
                pe.wait_ge(s["ka"], c + 1)
                if c >= 2:
                    pe.wait_ge(s["key"], c - 1)
                else:
                    pe.wait_ge(s["dln"], NCH)
                pe.matmul(ps_v(c), ones_bd[:, :], chunk(sq, c), start=True, stop=True).then_inc(s["kps"], 1)
            pe.wait_ge(s["va"], NCH)
            for c in range(NCH):
                pe.wait_ge(s["leaky"], 4 * (c + 1))
                if c >= 2:
                    pe.wait_ge(s["vtk"], c - 1)
                for i in range(4):
                    m = c * CP + 2 * i
                    mm = pe.transpose(ps_t(c)[:, i * 128:i * 128 + 128], hbd[:, m:m + 2, :, :].rearrange("p j f k -> p (j f k)"), ident[:, :])
                mm.then_inc(s["vtp"], 1)
                pe.wait_ge(s["key"], NCH if c < 2 else c + 1)
                if c >= 2:
                    pe.wait_ge(s["dsub"], c - 1)
                for j in range(2):
                    pe.matmul(ps[64 * j:64 * j + 64, 6 + c % 2, 0:4 * TOK], ones_q[:, :, :].rearrange("p f q -> p (f q)"),
                              nm[:, :].rearrange("p (m t) -> p m t", t=TOK)[:, c * CP + j:(c + 1) * CP:2, :], start=True, stop=False,
                              skip_group_check=True)
                    for f in range(2):
                        for i in range(4):
                            m = c * CP + 2 * i + j
                            r = 64 * j + 32 * f
                            mm = pe.matmul(ps[r:r + TOK, 6 + c % 2, i * TOK:(i + 1) * TOK], Q[:, f, m * TOK:(m + 1) * TOK],
                                           K[:, f, m * TOK:(m + 1) * TOK], start=False, stop=True, skip_group_check=True)
                mm.then_inc(s["dsc"], 1)
            pe.wait_ge(s["dsub"], NCH)
            for c in range(NCH):
                pe.wait_ge(s["dpt"], c + 1)
                pe.wait_ge(s["vtk"], c + 1 if c == 0 else NCH)
                if c >= 2:
                    pe.wait_ge(s["pvs"], 4 * (c - 1))
                for i in range(4):
                    for j in range(2):
                        for f in range(2):
                            r = slice(64 * j + 32 * f, 64 * j + 32 * f + 32)
                            mm = pe.matmul(ps[64 * f:64 * f + 64, 4 * (c % 2) + 2 * j + f, i * TOK:(i + 1) * TOK],
                                           htok[r, 4 * c + i, 64 * f:64 * f + 64], pt[r, 4 * c + i, 0:TOK], start=True, stop=True)
                mm.then_inc(s["pv"], 1)

            def centre(src, ready, count, done, read, squares, var, ln):
                for c in range(NCH):
                    pe.wait_ge(s[ready], count * (c + 1))
                    if c >= 2:
                        pe.wait_ge(s[read], c - 1)
                    pe.matmul(ps_v(c), cen_bd[:, :], chunk(src, c), start=True, stop=True).then_inc(s[done], 1)
                for c in range(NCH):
                    pe.wait_ge(s[squares], c + 1)
                    if c >= 2:
                        pe.wait_ge(s[ln], c - 1)
                    pe.matmul(ps_o(c), ones_bd[:, :], chunk(sq, c), start=True, stop=True).then_inc(s[var], 1)

            pe.wait_ge(s["pvs"], 4 * NCH)
            centre(oo, "pvs", 4, "oc", "osq", "osq", "ovar", "oln")
            centre(nrm, "oa", 1, "rc", "rsq", "rsq", "rvar", "rln")
            pe.wait_ge(s["wrb"], 1)
            for c in range(NCH):
                pe.wait_ge(s["h1"], c + 1)
                if c >= 2:
                    pe.wait_ge(s["ws"], c - 1)
                pe.matmul(ps_v(c), wrb[:, :], chunk(h1, c), start=True, stop=True).then_inc(s["wps"], 1)
            for c in range(NCH):
                pe.wait_ge(s["h1"], c + 1)
                if c >= 2:
                    pe.wait_ge(s["fg"], 2 * (c - 1))
                for f in range(2):
                    r = slice(64 * f, 64 * f + 64)
                    for g in range(2):
                        mm = pe.matmul(ps_g(c)[:, f, g * CC:(g + 1) * CC], fw1[r, g * 128:g * 128 + 128], h1[r, c * CC:(c + 1) * CC],
                                       start=True, stop=True)
                mm.then_inc(s["fz"], 1)
            pe.wait_ge(s["rln"], NCH)
            for c in range(NCH):
                pe.wait_ge(s["fg"], 2 * (c + 1))
                if c >= 2:
                    pe.wait_ge(s["ysb"], c - 1)
                for f in range(2):
                    for g in range(2):
                        mm = pe.matmul(ps_o(c)[64 * f:64 * f + 64, :], fw2[:, g, :], U[:, 2 * g + f, c * CC:(c + 1) * CC],
                                       start=(g == 0), stop=(g == 1))
                mm.then_inc(s["fy"], 1)
            pe.wait_ge(s["sel_row"], 32)
            pe.wait_ge(s["ws"], NCH)
            for c in range(NCH):
                if c >= 2:
                    pe.wait_ge(s["y2"], c - 1)
                pe.matmul(ps_v(c), ones_bd[:, :], chunk(selrow, c), start=True, stop=True).then_inc(s["selps"], 1)
            pe.wait_ge(s["ysb"], NCH)
            pe.wait_ge(s["y2"], NCH)
            centre(z2, "z2", 1, "zc", "zsq", "zsq", "zvar", "zln")
            pe.wait_ge(s["fg"], 2 * NCH)
            for t in range(NT):
                w = min(128, COLS - 128 * t)
                pe.wait_ge(s["zo"], -(-(128 * t + w) // CC))
                if t >= 4:
                    pe.wait_ge(s["oo"], t - 3)
                pe.transpose(ps[0:w, t % 4, 0:128], nrm[:, 128 * t:128 * t + w], ident[:, :]).then_inc(s["ops2"], 1)

        def final_dve(dve):
            dve.wait_ge(s["par_in"], 16 * PAR_LOADS)
            dve.tensor_scalar(wrb[:, :], ones_bd[:, :], col[:, WR:WR + 1], float(DIM), ALU.mult, ALU.mult).then_inc(s["wrb"], 1)
            for c in range(NCH):
                dve.wait_ge(s["drs"], c + 1)
                dve.tensor_tensor(chunk(nrm, c), chunk(x, c), chunk(rstd, c), ALU.mult).then_inc(s["dn"], 1)
                dve.wait_ge(s["dn"], c + 1)
                dve.tensor_scalar(chunk(h, c), chunk(nrm, c), col[:, FG:FG + 1], col[:, FB:FB + 1], ALU.mult, ALU.add).then_inc(s["dh"], 1)
            for c in range(NCH):
                dve.wait_ge(s["qa"], 2 * (c + 1))
                for w in (Q, K):
                    v = w[:, :, c * CC:(c + 1) * CC]
                    dve.scalar_tensor_tensor(out=v, in0=v, scalar=0.2, in1=v, op0=ALU.mult, op1=ALU.max).then_inc(s["leaky"], 1)
                dve.wait_ge(s["va"], c + 1)
                for f in range(2):
                    v = pairs(nrm, c, slice(64 * f, 64 * f + 64))
                    dve.scalar_tensor_tensor(out=hbd[64 * f:64 * f + 64, c * CP:(c + 1) * CP, f, 0:TOK], in0=v, scalar=0.2, in1=v,
                                             op0=ALU.mult, op1=ALU.max).then_inc(s["leaky"], 1)
            for c in range(NCH):
                dve.wait_ge(s["kps"], c + 1)
                dve.tensor_scalar(chunk(nm, c), ps_v(c), 0.0, NEG * UNITS ** 0.5, ALU.is_equal, ALU.mult).then_inc(s["key"], 1)

            def sums(c):
                dve.wait_ge(s["dex"], c + 1)
                dve.tensor_reduce(sm[:, 4 * c:4 * c + 4], ex[:, 4 * c:4 * c + 4, :], axis=AX.X, op=ALU.add).then_inc(s["dsm"], 1)
                dve.wait_ge(s["dsm"], c + 1)
                dve.reciprocal(ri[:, 4 * c:4 * c + 4], sm[:, 4 * c:4 * c + 4]).then_inc(s["dri"], 1)
                dve.wait_ge(s["dri"], c + 1)
                dve.tensor_tensor(pn[:, 4 * c:4 * c + 4, 0:TOK], ex[:, 4 * c:4 * c + 4, :], ri[:, 4 * c:4 * c + 4, None].to_broadcast([128, 4, TOK]),
                                  ALU.mult).then_inc(s["dpn"], 1)
                dve.wait_ge(s["dpn"], c + 1)
                dve.transpose(pt[:, 4 * c:4 * c + 4, :].rearrange("p g k -> p (g k)"),
                              pn[:, 4 * c:4 * c + 4, :].rearrange("p g k -> p (g k)")).then_inc(s["dpt"], 1)

            for c in range(NCH):
                sc = ps[:, 6 + c % 2, 0:4 * TOK].rearrange("p (g k) -> p g k", k=TOK)
                dve.wait_ge(s["dsc"], c + 1)
                dve.tensor_reduce(mx[:, 4 * c:4 * c + 4], sc, axis=AX.X, op=ALU.max).then_inc(s["dmx"], 1)
                dve.wait_ge(s["dmx"], c + 1)
                dve.tensor_tensor(ex[:, 4 * c:4 * c + 4, :], sc, mx[:, 4 * c:4 * c + 4, None].to_broadcast([128, 4, TOK]), ALU.subtract).then_inc(s["dsub"], 1)
                if c:
                    sums(c - 1)
            sums(NCH - 1)
            for c in range(NCH):
                dve.wait_ge(s["pv"], c + 1)
                for j in range(2):
                    for f in range(2):
                        r = slice(64 * f, 64 * f + 64)
                        dve.tensor_tensor(pairs(oo, c, r)[:, j::2, :],
                                          ps[r, 4 * (c % 2) + 2 * j + f, 0:4 * TOK].rearrange("p (i t) -> p i t", t=TOK),
                                          pairs(h, c, r)[:, j::2, :], ALU.add).then_inc(s["pvs"], 1)
            for c in range(NCH):
                dve.wait_ge(s["ors"], c + 1)
                dve.wait_ge(s["ocs"], c + 1)
                dve.tensor_tensor(chunk(nrm, c), chunk(rc, c), chunk(rstd, c), ALU.mult).then_inc(s["on"], 1)
                dve.wait_ge(s["on"], 2 * c + 1)
                dve.scalar_tensor_tensor(out=chunk(nrm, c), in0=chunk(nrm, c), scalar=col[:, GAMMA:GAMMA + 1], in1=chunk(h, c),
                                         op0=ALU.mult, op1=ALU.add).then_inc(s["on"], 1)
                dve.wait_ge(s["on"], 2 * c + 2)
                dve.tensor_scalar(chunk(nrm, c), chunk(nrm, c), col[:, BETA:BETA + 1], None, ALU.add).then_inc(s["oa"], 1)
            for c in range(NCH):
                dve.wait_ge(s["rrs"], c + 1)
                dve.wait_ge(s["rcs"], c + 1)
                dve.tensor_tensor(chunk(h1, c), chunk(rc, c), chunk(rstd, c), ALU.mult).then_inc(s["h1"], 1)
            for c in range(NCH):
                dve.wait_ge(s["wps"], c + 1)
                dve.tensor_scalar(chunk(wb, c), ps_v(c), col[:, BR:BR + 1], None, ALU.add).then_inc(s["ws"], 1)
            dve.wait_ge(s["sel_img"], 32)
            heavier, same = gt[:, 0, :, :], gt[:, 1, :, :]
            mine, other = wimg[:, :, None].to_broadcast([128, TOK, TOK]), wimg[:, None, :].to_broadcast([128, TOK, TOK])
            dve.tensor_tensor(heavier, other, mine, ALU.is_gt).then_inc(s["compared"], 1)
            dve.tensor_tensor(same, other, mine, ALU.is_equal).then_inc(s["compared"], 1)
            dve.wait_ge(s["compared"], 2)
            dve.wait_ge(s["tri"], 2)
            dve.tensor_tensor(same, same, tri[:, :, :], ALU.mult).then_inc(s["compared"], 1)
            dve.wait_ge(s["compared"], 3)
            dve.tensor_tensor(heavier, heavier, same, ALU.add).then_inc(s["compared"], 1)
            dve.wait_ge(s["compared"], 4)
            dve.tensor_reduce(rank[:, :], heavier, axis=AX.X, op=ALU.add).then_inc(s["compared"], 1)
            dve.wait_ge(s["compared"], 5)
            dve.scalar_tensor_tensor(out=wimg[:, :], in0=rank[:, :], scalar=float(KSEL), in1=wimg[:, :], op0=ALU.is_lt, op1=ALU.mult).then_inc(s["selm"], 1)
            for c in range(NCH):
                dve.wait_ge(s["fy"], c + 1)
                dve.tensor_scalar(chunk(sel64, c), ps_o(c), col[:, FB2:FB2 + 1], float(DIM), ALU.add, ALU.mult).then_inc(s["ysb"], 1)
            for c in range(NCH):
                dve.wait_ge(s["ysb"], c + 1)
                dve.wait_ge(s["selps"], c + 1)
                dve.tensor_tensor(chunk(sel64, c), ps_v(c), chunk(sel64, c), ALU.mult).then_inc(s["y2"], 1)
                dve.wait_ge(s["y2"], c + 1)
                dve.scalar_tensor_tensor(out=chunk(z2, c), in0=chunk(h1, c), scalar=2.0, in1=chunk(sel64, c), op0=ALU.mult, op1=ALU.add).then_inc(s["z2"], 1)
            for c in range(NCH):
                dve.wait_ge(s["zrs"], c + 1)
                dve.wait_ge(s["zcs"], c + 1)
                dve.tensor_tensor(chunk(nrm, c), chunk(rc, c), chunk(rstd, c), ALU.mult).then_inc(s["zo"], 1)

        def final_pool(pool):
            pool.wait_ge(s["z"], DEPTH * NCH)
            pool.wait_ge(s["yps"], DEPTH * NCH)
            pool.memset(selrow, 0.0).then_inc(s["sel_zero"], 1)

        block = ctx.enter_context(nc.Block())

        def after(eng, signal, count):
            if not isinstance(count, int) or count > 0:
                eng.wait_ge(s[signal], count)

        def chunk(t, c):
            return t[:, c * CC:(c + 1) * CC]

        def pairs(t, c, r=slice(0, 128)):
            return t[r, c * CC:(c + 1) * CC].rearrange("p (m t) -> p m t", t=TOK)

        def softmax_sum(dve, n, c):
            g = slice(16 * c, 16 * c + 16)
            dve.wait_ge(s["ex"], n(c + 1))
            dve.tensor_reduce(sm[:, g], ex[:, g, :], axis=AX.X, op=ALU.add).then_inc(s["sm"], 1)
            dve.wait_ge(s["sm"], n(c + 1))
            dve.reciprocal(ri[:, g], sm[:, g]).then_inc(s["ri"], 1)

        def transposed(dve, n, c):
            g = slice(16 * c, 16 * c + 16)
            dve.wait_ge(s["pn"], n(c + 1))
            dve.transpose(pt[:, g, :].rearrange("p g k -> p (g k)"), pn[:, g, :].rearrange("p g k -> p (g k)")).then_inc(s["pt"], 1)

        def ps_u(c):
            return ps[:, 2 * (c % 2):2 * (c % 2) + 2, 0:2 * CC]

        def ps_t(c):
            return ps[:, 4 + c % 2, :]

        def ps_s(c):
            return ps[:, 6 + c % 2, 0:4 * HEADS * TOK]

        def ps_g(c):
            return ps[:, 2 * (c % 2):2 * (c % 2) + 2, :]

        def ps_v(c):
            return ps[:, 6 + c % 2, 0:CC]

        def ps_o(c):
            return ps[:, 4 + c % 2, 0:CC]

        @block.sync
        def _(sp):
            sp.dma_start(wp[:, :, :], a["W_patch"].rearrange("(q k) d -> q k d", q=KP)).then_inc(s["w_in"], 16)
            sp.dma_start(gp[:, 0, :], a["ln_p1_g"].rearrange("(q k) -> q k", q=KP)).then_inc(s["w_in"], 16)
            sp.dma_start(gp[:, 1, :], a["ln_p1_b"].rearrange("(q k) -> q k", q=KP)).then_inc(s["w_in"], 16)

            def load(u, first):
                for f in range(2):
                    for c in range(CH):
                        for g in range(GRID):
                            img = a["x"][bass.ds(first + f * NPAIR, CP), c, g * P:(g + 1) * P, :]
                            sp.dma_start(xin[c * P:(c + 1) * P, u, f, :, g * IMG:(g + 1) * IMG],
                                         img.rearrange("b r w -> r b w")).then_inc(s[f"x_in{u}"], 16)

            for u in range(2):
                load(u, u * CP)
            with sp.Fori(1, NCH // 2) as i:
                for u in range(2):
                    first, products, parts = sp.snap(i * (2 * CP) + u * CP), sp.snap(i * 2 + (u - 1)), sp.snap(i * 8 + 4 * (u - 1))
                    sp.wait_ge(s["patch_mm"], products)
                    sp.wait_ge(s["squares"], parts)
                    sp.wait_ge(s["halves"], parts)
                    load(u, first)
            sp.wait_ge(s["wv_zero"], 1)
            for f in range(2):
                r = slice(64 * f, 64 * f + 64)
                sp.dma_start(wqk[r, 0, :], a["Wq"]).then_inc(s["fin_in"], 16)
                sp.dma_start(wqk[r, 1, :], a["Wk"]).then_inc(s["fin_in"], 16)
                sp.dma_start(wv[r, r], a["Wv"]).then_inc(s["fin_in"], 16)
                sp.dma_start(fw1[r, :], a["fw1"]).then_inc(s["fin_in"], 16)
                sp.dma_start(fcol[:, 2 + f:3 + f], a["fb1"][f * 128:f * 128 + 128].rearrange("(d o) -> d o", o=1)).then_inc(s["fin_in"], 16)
                sp.dma_start(fw2[:, f, :], a["fw2"][f * 128:f * 128 + 128, :]).then_inc(s["fin_in"], 16)
            sp.dma_start(fcol[:, 0:1], a["bq"].rearrange("(d o) -> d o", o=1)).then_inc(s["fin_in"], 16)
            sp.dma_start(fcol[:, 1:2], a["bk"].rearrange("(d o) -> d o", o=1)).then_inc(s["fin_in"], 16)
            sp.wait_ge(s["prep_ready"], 3)
            for l in range(DEPTH):
                for slot, bank, free in (("slot_mu", mu_all, "ups"), ("slot_vo", vo_all, "ops"), ("slot_w1", w1f, "zps"), ("slot_w2", w2, "yps")):
                    to = {"slot_mu": mu, "slot_vo": vo, "slot_w1": w1s, "slot_w2": w2s}[slot]
                    sp.wait_ge(s[free], l * NCH)
                    sp.dma_start(to[:, :], bank[:, l, :]).then_inc(s[slot], 16)
            final_sp(sp)

        @block.scalar
        def _(act):
            for f in range(2):
                r = slice(64 * f, 64 * f + 64)
                for n, j in (("b_patch", B_PATCH), ("ln_p2_g", G2), ("ln_p2_b", B2P), ("ln_f_g", FG), ("ln_f_b", FB),
                             ("gamma", GAMMA), ("beta", BETA), ("bv", BV), ("fb2", FB2)):
                    act.dma_start(col[r, j:j + 1], a[n].rearrange("(d o) -> d o", o=1)).then_inc(s["par_in"], 16)
                act.dma_start(col[r, CLS:CLS + 1], a["cls"].rearrange("a b d -> d (a b)"), allow_slow_non_contiguous=True).then_inc(s["par_in"], 16)
                act.dma_start(col[r, WR:WR + 1], a["wr"]).then_inc(s["par_in"], 16)
                act.dma_start(col[r, BR:BR + 1], a["br"].rearrange("(o b) -> o b", o=1).to_broadcast([64, 1])).then_inc(s["par_in"], 16)
                act.dma_start(posT[r, :], a["pos"].rearrange("a t d -> d (a t)"), allow_slow_non_contiguous=True).then_inc(s["par_in"], 16)
                for n, j in (("attn_ln_g", GA), ("attn_ln_b", BA), ("ff_ln_g", GF), ("ff_ln_b", BF), ("bo", BO), ("b2", B2)):
                    act.dma_start(lay[r, j, :], a[n].rearrange("l d -> d l"), allow_slow_non_contiguous=True).then_inc(s["par_in"], 16)
                act.dma_start(w1[r, :, :], a["W1"].rearrange("l c d -> c l d")).then_inc(s["par_in"], 16)
            act.dma_start(lay[:, B1, :], a["b1"].rearrange("l d -> d l"), allow_slow_non_contiguous=True).then_inc(s["par_in"], 16)
            act.dma_start(w2[:, :, :], a["W2"].rearrange("l c d -> c l d")).then_inc(s["par_in"], 16)
            act.dma_start(wqkv, a["Wqkv"].rearrange("l c d -> c l d")).then_inc(s["wq_in"], 16)
            act.dma_start(wo[:, :, :], a["Wo"].rearrange("l (g q) d -> q (l g) d", q=128)).then_inc(s["par_in"], 16)
            for l in range(DEPTH):
                act.wait_ge(s["qt"], l + 1)
                if l:
                    act.wait_ge(s["vops"], l)
                act.activation(wT[:, :, :], ps[:, 4, 0:384].rearrange("p (g c) -> p g c", g=6), ACT.Copy).then_inc(s["qt_sb"], 1)
                act.wait_ge(s["mups"], l + 1)
                if l == 0:
                    act.wait_ge(s["cst_pool"], 6)
                for f in range(2):
                    r = slice(64 * f, 64 * f + 64)
                    act.activation(mu_all[r, l, :].rearrange("p (a b c) -> p b a c", b=2, c=128)[:, :, :, r], ps[r, 5:7, 0:128].rearrange("p b (a c) -> p b a c", a=2), ACT.Copy,
                                   scale=DIM ** -0.5).then_inc(s["mu_sb"], 1)
                act.wait_ge(s["vops"], l + 1)
                for f in range(2):
                    r = slice(64 * f, 64 * f + 64)
                    act.activation(vo_all[r, l, :].rearrange("p (a b c) -> p b a c", b=2, c=128)[:, :, :, r], ps[r, 0:2, 0:128].rearrange("p b (a c) -> p b a c", a=2), ACT.Copy).then_inc(s["mu_sb"], 1)
            act.wait_ge(s["mu_sb"], 4 * DEPTH)
            act.activation(eps8[:, :], eps8[:, :], ACT.Copy).then_inc(s["prep_ready"], 1)
            def two_chunks(i):
                for u in range(2):
                    act.wait_ge(s[f"x_in{u}"], i * (16 * LOADS) + 16 * LOADS)
                    for q in range(4):
                        after(act, "sq_red", i * 8 + (4 * u + q - 1))
                        act.activation(sqp[:, q % 2, :].rearrange("p (m w) -> p m w", m=4),
                                       xin[:, u, q // 2, 4 * (q % 2):4 * (q % 2) + 4, :], ACT.Square).then_inc(s["squares"], 1)

            two_chunks(0)
            with act.Fori(1, NCH // 2) as i:
                two_chunks(i)
            act.wait_ge(s["patch_out"], 2 * NCH)
            act.preload_act_table_set("natural_log_exp_and_others")
            act.activation(pm2.rearrange("p (k n) -> p k n", k=NCH), sraw[:, :, 0:PC], ACT.Square).then_inc(s["p_m2"], 1)
            act.wait_ge(s["p_var"], 1)
            act.activation(pln, pvar, ACT.Ln, bias=eps5[:, :]).then_inc(s["p_ln"], 1)
            act.wait_ge(s["p_ln"], 1)
            act.activation(prs, pln, ACT.Exp, scale=-0.5).then_inc(s["p_rs"], 1)
            act.wait_ge(s["p_yc"], 1)
            act.activation(pm2, py, ACT.Square).then_inc(s["p_sq"], 1)
            for c in range(2):
                act.wait_ge(s["p_v2"], c + 1)
                act.activation(pln[:, 512 * c:512 * c + 512], ps[:, c, :], ACT.Ln, bias=eps5[:, :]).then_inc(s["p_ln2"], 1)
            act.wait_ge(s["p_ln2"], 2)
            act.activation(prs, pln, ACT.Exp, scale=-0.5).then_inc(s["p_rs2"], 1)
            for c in range(NCH):
                act.wait_ge(s["cen"], c + 1)
                act.activation(chunk(x, c), ps[:, 2 + c % 2, 0:CC], ACT.Copy).then_inc(s["ff"], 1)

            act.wait_ge(s["prep_ready"], 3)
            with act.Fori(0, DEPTH) as l:
                def n(k):
                    return l * NCH + k
                act.preload_act_table_set("natural_log_exp_and_others")
                act.activation(cur[:, 0:2], lay[:, GA:BA + 1, bass.ds(l, 1)].rearrange("p a o -> p (a o)"), ACT.Copy).then_inc(s["cur"], 1)
                act.activation(cur[:, 2:3], b1_f[:, bass.ds(l, 1)], ACT.Copy).then_inc(s["cur"], 1)
                for c in range(NCH):
                    act.wait_ge(s["ff"], n(c + 1))
                    act.activation(chunk(sq, c), chunk(x, c), ACT.Square).then_inc(s["sq"], 1)
                for c in range(NCH):
                    act.wait_ge(s["var"], n(c + 1))
                    act.activation(chunk(lnv, c), ps_v(c), ACT.Ln, bias=eps5[:, :]).then_inc(s["lnv"], 1)
                    act.wait_ge(s["lnv"], n(c + 1))
                    act.activation(chunk(rstd, c), chunk(lnv, c), ACT.Exp, scale=-0.5).then_inc(s["rstd"], 1)
                    if c == 0:
                        act.wait_ge(s["cur"], l * 2 + 2)
                        act.wait_ge(s["pads"], 2)
                    act.wait_ge(s["nrm"], n(c + 1))
                    act.activation(hbd[0:64, c * CP:(c + 1) * CP, 0, 0:TOK], pairs(nrm, c, slice(0, 64)), ACT.Identity,
                                   bias=cur[0:64, 1:2], scale=cur[0:64, 0:1]).then_inc(s["ha"], 1)
                for c in range(NCH):
                    act.wait_ge(s["ups"], n(c + 1))
                    act.activation(U[:, :, c * CC:(c + 1) * CC].rearrange("p (a b) n -> p a b n", a=2),
                                   ps_u(c).rearrange("p a (b n) -> p a b n", b=2), ACT.Copy).then_inc(s["u"], 1)
                    act.wait_ge(s["tps"], n(c + 1))
                    act.activation(htok[:, 4 * c:4 * c + 4, :], ps_t(c).rearrange("p (i c) -> p i c", i=4), ACT.Copy).then_inc(s["tk"], 1)
                for c in range(NCH):
                    act.wait_ge(s["sub"], n(c + 1))
                    act.activation(ex[:, 16 * c:16 * c + 16, :], ex[:, 16 * c:16 * c + 16, :], ACT.Exp).then_inc(s["ex"], 1)
                for c in range(NCH):
                    act.wait_ge(s["gps"], n(c + 1))
                    act.activation(G[:, :, c * CP:(c + 1) * CP:2, :].rearrange("p h i q -> p i h q"),
                                   ps_g(c)[:, 0, :].rearrange("p (i h q) -> p i h q", i=4, h=HEADS)[:, :, :, 0:TOK],
                                   ACT.Copy).then_inc(s["ga"], 1)
                for c in range(NCH + 2):
                    if c < NCH:
                        act.wait_ge(s["att"], n(c + 1))
                        act.activation(chunk(sq, c), chunk(x, c), ACT.Square).then_inc(s["fsq"], 1)
                    if c >= 2:
                        act.wait_ge(s["fvar"], n(c - 1))
                        act.activation(chunk(lnv, c - 2), ps_v(c - 2), ACT.Ln, bias=eps5[:, :]).then_inc(s["fln"], 1)
                        act.wait_ge(s["fln"], n(c - 1))
                        act.activation(chunk(rstd, c - 2), chunk(lnv, c - 2), ACT.Exp, scale=-0.5).then_inc(s["frs"], 1)
                for c in range(NCH):
                    act.wait_ge(s["zps"], n(c + 1))
                    act.activation(z[:, :, c * CC:(c + 1) * CC], ps_g(c)[:, :, 0:CC], ACT.Gelu,
                                   bias=cur[:, 2:3]).then_inc(s["z"], 1)
                act.wait_ge(s["z"], n(NCH))
            final_act(act)

        @block.tensor
        def _(pe):
            pe.wait_ge(s["ones_ok"], 2)
            pe.wait_ge(s["wp_c"], 1)
            pe.matmul(ps[0:KP, 7, 0:DIM], ones[0:KP, 0:KP], wred[:, 0:DIM], start=True, stop=True).then_inc(s["colmean"], 1)
            for f in range(2):
                mm = pe.matmul(ps[64 * f:64 * f + 64, 3, 64:65], wred[:, 2 * DIM:3 * DIM], ones[0:KP, 0:1], start=True, stop=True)
            mm.then_inc(s["cst_ps"], 1)
            pe.wait_ge(s["ident_ok"], 1)
            pe.wait_ge(s["wq_in"], 16)
            for l in range(DEPTH):
                if l:
                    pe.wait_ge(s["qt_sb"], l)
                for g in range(6):
                    mm = pe.transpose(ps[:, 4, g * 64:g * 64 + 64], wqkv[:, l, g * 128:g * 128 + 128], ident[0:64, 0:64])
                mm.then_inc(s["qt"], 1)
                pe.wait_ge(s["qt_sb"], l + 1)
                if l:
                    pe.wait_ge(s["mu_sb"], 4 * l)
                for hd in range(HEADS):
                    r = slice(64 * (hd % 2), 64 * (hd % 2) + 64)
                    for f in range(2):
                        mm = pe.matmul(ps[64 * f:64 * f + 64, 5 + hd % 2, hd // 2 * 64:hd // 2 * 64 + 64], wT[r, 2 + hd // 2, :], wT[r, hd // 2, :],
                                       start=True, stop=True)
                mm.then_inc(s["mups"], 1)
                if l == 0:
                    pe.wait_ge(s["wo_c"], 1)
                for hd in range(HEADS):
                    r = slice(64 * (hd % 2), 64 * (hd % 2) + 64)
                    for f in range(2):
                        mm = pe.matmul(ps[64 * f:64 * f + 64, hd % 2, hd // 2 * 64:hd // 2 * 64 + 64], wT[r, 4 + hd // 2, :], wo[r, 2 * l + hd // 2, :],
                                       start=True, stop=True)
                mm.then_inc(s["vops"], 1)
            pe.wait_ge(s["par_in"], 16 * PAR_LOADS)
            pe.wait_ge(s["cst_a"], 1)
            pe.matmul(ps[:, 7, 80:81], cen_bd[:, :], cst[:, 0:1], start=True, stop=True)
            pe.matmul(ps[:, 7, 84:84 + DEPTH], cen_bd[:, :], lay[:, BO, :], start=True, stop=True)
            pe.matmul(ps[:, 7, 88:88 + DEPTH], cen_bd[:, :], lay[:, B2, :], start=True, stop=True)
            for l in range(DEPTH):
                mm = pe.matmul(ps[:, 7, 92 + l:93 + l], w1[0:64, l, :], lay[0:64, BF, l:l + 1], start=True, stop=True)
            mm.then_inc(s["bias_ps"], 1)
            pe.wait_ge(s["wp_ready"], 1)
            pe.wait_ge(s["mu_sb"], 4 * DEPTH)
            def two_chunks(i):
                for u in range(2):
                    pe.wait_ge(s[f"x_in{u}"], i * (16 * LOADS) + 16 * LOADS)
                    after(pe, "patch_out", i * 4 + (2 * u - 3))
                    for k in range(P):
                        for f in range(2):
                            mm = pe.matmul(ps[64 * f:64 * f + 64, u, 0:PC], wp[:, k, :],
                                           xin[:, u, f, :, :].rearrange("p m (g k) -> p (m g) k", k=P)[:, :, k],
                                           start=(k == 0), stop=(k == P - 1))
                    mm.then_inc(s["patch_mm"], 1)
                    after(pe, "patch_out", i * 4 + (2 * u - 2))
                    pe.wait_ge(s["sq_red"], i * 8 + 4 * (u + 1))
                    pe.wait_ge(s["sum_red"], i * 8 + 4 * (u + 1))
                    for f in range(2):
                        pe.matmul(ps[64 * f:64 * f + 64, 2 + u, 0:PC], ones[0:KP, 0:64], psm[:, u, f * PC:(f + 1) * PC], start=True, stop=True)
                        mm = pe.matmul(ps[64 * f:64 * f + 64, 2 + u, PC:2 * PC], ones[0:KP, 0:64], psq[:, u, f * PC:(f + 1) * PC], start=True, stop=True)
                    mm.then_inc(s["patch_st"], 1)

            two_chunks(0)
            with pe.Fori(1, NCH // 2) as i:
                two_chunks(i)
            pe.wait_ge(s["p_sq"], 1)
            for c in range(2):
                pe.matmul(ps[:, c, :], ones_bd[:, :], pm2[:, 512 * c:512 * c + 512], start=True, stop=True).then_inc(s["p_v2"], 1)
            pe.wait_ge(s["x0"], 1)
            for c in range(NCH):
                if c >= 2:
                    pe.wait_ge(s["ff"], c - 1)
                pe.matmul(ps[:, 2 + c % 2, 0:CC], cen_bd[:, :], x0[:, c * CP:(c + 1) * CP, :].rearrange("p m t -> p (m t)"),
                          start=True, stop=True).then_inc(s["cen"], 1)

            with pe.Fori(0, DEPTH) as l:
                def n(k):
                    return l * NCH + k

                def variance(c, squares, last, done):
                    pe.wait_ge(s[squares], n(c + 1))
                    if c >= 2:
                        pe.wait_ge(s[last], n(c - 1))
                    pe.matmul(ps_v(c), ones_bd[:, :], chunk(sq, c), start=True, stop=True).then_inc(s[done], 1)

                for c in range(NCH):
                    variance(c, "sq", "lnv", "var")
                pe.wait_ge(s["slot_mu"], l * 16 + 16)
                for c in range(NCH):
                    pe.wait_ge(s["h"], n(c + 1))
                    if c >= 2:
                        pe.wait_ge(s["u"], n(c - 1))
                    for hd in range(HEADS):
                        mm = pe.matmul(ps_u(c)[:, hd // 2, hd % 2 * CC:(hd % 2 + 1) * CC], mu[:, hd * 128:hd * 128 + 128], chunk(h, c), start=True, stop=True)
                    mm.then_inc(s["ups"], 1)
                    pe.wait_ge(s["ha"], n(c + 1))
                    pe.wait_ge(s["hb"], n(c + 1))
                    if c >= 2:
                        pe.wait_ge(s["tk"], n(c - 1))
                    for i in range(4):
                        m = c * CP + 2 * i
                        mm = pe.transpose(ps_t(c)[:, i * 128:i * 128 + 128], hbd[:, m:m + 2, :, :].rearrange("p j f k -> p (j f k)"), ident[:, :])
                    mm.then_inc(s["tps"], 1)
                for c in range(NCH):
                    pe.wait_ge(s["u"], n(c + 1))
                    if c >= 2:
                        pe.wait_ge(s["sub"], n(c - 1))
                    if c < 2:
                        pe.wait_ge(s["lnv"], n(NCH))
                    for j in range(2):
                        for i in range(4):
                            m = c * CP + 2 * i + j
                            mm = pe.matmul(ps_s(c)[64 * j:64 * j + 64, i * HEADS * TOK:(i + 1) * HEADS * TOK], hbd[:, m, :, :].rearrange("p f k -> p (f k)"),
                                           U[:, :, m * TOK:(m + 1) * TOK], start=True, stop=True)
                    mm.then_inc(s["sc"], 1)
                for c in range(NCH):
                    pe.wait_ge(s["pt"], n(c + 1))
                    pe.wait_ge(s["tk"], n(c + 1))
                    if c >= 2:
                        pe.wait_ge(s["ga"], n(c - 1))
                    if c >= 2:
                        pe.wait_ge(s["gd"], n(c - 1))
                    for i in range(4):
                        for j in range(2):
                            r = slice(64 * j, 64 * j + 64)
                            mm = pe.matmul(ps_g(c)[:, j, i * 128:i * 128 + 128], htok[r, 4 * c + i, :],
                                           pt[r, 16 * c + 4 * i:16 * c + 4 * i + 4, :], start=True, stop=True)
                    mm.then_inc(s["gps"], 1)
                pe.wait_ge(s["slot_vo"], l * 16 + 16)
                for c in range(NCH):
                    pe.wait_ge(s["ga"], n(c + 1))
                    pe.wait_ge(s["gd"], n(c + 1))
                    if c >= 2:
                        pe.wait_ge(s["att"], n(c - 1))
                    for hd in range(HEADS):
                        mm = pe.matmul(ps_o(c), vo[:, hd * 128:hd * 128 + 128], G[:, hd, c * CP:(c + 1) * CP, :].rearrange("p m t -> p (m t)"),
                                       start=(hd == 0), stop=(hd == HEADS - 1))
                    mm.then_inc(s["ops"], 1)
                    if c >= 2:
                        variance(c - 2, "fsq", "fln", "fvar")
                for c in range(NCH - 2, NCH):
                    variance(c, "fsq", "fln", "fvar")
                pe.wait_ge(s["slot_w1"], l * 16 + 16)
                for c in range(NCH):
                    pe.wait_ge(s["fn"], n(c + 1))
                    if c >= 2:
                        pe.wait_ge(s["z"], n(c - 1))
                    for f in range(2):
                        r = slice(64 * f, 64 * f + 64)
                        mm = pe.matmul(ps_g(c)[:, f, 0:CC], w1s[r, :], nrm[r, c * CC:(c + 1) * CC], start=True, stop=True)
                    mm.then_inc(s["zps"], 1)
                pe.wait_ge(s["slot_w2"], l * 16 + 16)
                for c in range(NCH):
                    pe.wait_ge(s["z"], n(c + 1))
                    if c >= 2:
                        pe.wait_ge(s["ff"], n(NCH + c - 1))
                    else:
                        pe.wait_ge(s["att"], n(NCH))
                    for f in range(2):
                        mm = pe.matmul(ps_o(c)[64 * f:64 * f + 64, :], w2s[:, :], z[:, f, c * CC:(c + 1) * CC], start=True, stop=True)
                    mm.then_inc(s["yps"], 1)
            final_pe(pe)

        @block.vector
        def _(dve):
            dve.wait_ge(s["w_in"], 48)
            dve.tensor_tensor(wtmp, wp[:, :, :], gp[:, 1, :, None].to_broadcast([KP, P, DIM]), ALU.mult).then_inc(s["wp_a"], 1)
            dve.wait_ge(s["wp_a"], 1)
            dve.tensor_reduce(wred[:, 2 * DIM:3 * DIM], wtmp.rearrange("p k d -> p d k"), axis=AX.X, op=ALU.add).then_inc(s["wp_a"], 1)
            dve.tensor_tensor(wp[:, :, :], wp[:, :, :], gp[:, 0, :, None].to_broadcast([KP, P, DIM]), ALU.mult).then_inc(s["wp_a"], 1)
            dve.wait_ge(s["wp_a"], 3)
            dve.tensor_reduce(gp[:, 1, :], wp[:, :, :], axis=AX.X, op=ALU.add).then_inc(s["wp_a"], 1)
            dve.wait_ge(s["wp_a"], 4)
            dve.tensor_scalar(gp[:, 1, :], gp[:, 1, :], 1.0 / DIM, None, ALU.mult).then_inc(s["wp_a"], 1)
            dve.wait_ge(s["wp_a"], 5)
            dve.tensor_tensor(wp[:, :, :], wp[:, :, :], gp[:, 1, :, None].to_broadcast([KP, P, DIM]), ALU.subtract).then_inc(s["wp_a"], 1)
            dve.wait_ge(s["wp_a"], 6)
            dve.tensor_reduce(wred[:, 0:DIM], wp[:, :, :].rearrange("p k d -> p d k"), axis=AX.X, op=ALU.add).then_inc(s["wp_c"], 1)
            dve.wait_ge(s["colmean"], 1)
            dve.tensor_scalar(wred[:, DIM:2 * DIM], ps[0:KP, 7, 0:DIM], 1.0 / PD, None, ALU.mult).then_inc(s["wp_a"], 1)
            dve.wait_ge(s["wp_a"], 7)
            dve.tensor_tensor(wp[:, :, :], wp[:, :, :], wred[:, None, DIM:2 * DIM].to_broadcast([KP, P, DIM]), ALU.subtract).then_inc(s["wp_ready"], 1)
            dve.wait_ge(s["par_in"], 16 * PAR_LOADS)
            dve.tensor_reduce(wo_r[:, :], wo[:, :, :], axis=AX.X, op=ALU.add).then_inc(s["wp_b"], 1)
            dve.tensor_reduce(w2_r[:, :], w2[:, :, :], axis=AX.X, op=ALU.add).then_inc(s["wp_b"], 1)
            dve.wait_ge(s["wp_b"], 2)
            dve.tensor_scalar(wo_r[:, :], wo_r[:, :], 1.0 / DIM, None, ALU.mult).then_inc(s["wp_b"], 1)
            dve.tensor_scalar(w2_r[:, :], w2_r[:, :], 1.0 / DIM, None, ALU.mult).then_inc(s["wp_b"], 1)
            dve.wait_ge(s["wp_b"], 4)
            dve.tensor_tensor(wo[:, :, :], wo[:, :, :], wo_r[:, :, None].to_broadcast([128, 2 * DEPTH, DIM]), ALU.subtract).then_inc(s["wo_c"], 1)
            dve.tensor_tensor(w2[:, :, :], w2[:, :, :], w2_r[:, :, None].to_broadcast([128, DEPTH, DIM]), ALU.subtract).then_inc(s["wp_b"], 1)
            dve.tensor_tensor(w1f[:, :, :], w1[:, :, :], lay[:, GF, :, None].to_broadcast([128, DEPTH, MLP]), ALU.mult).then_inc(s["wp_b"], 1)
            dve.wait_ge(s["wp_b"], 6)
            dve.tensor_copy(wo_r[:, :], wo_r[:, :]).then_inc(s["prep_ready"], 1)
            dve.wait_ge(s["cst_ps"], 1)
            dve.tensor_tensor(cst[:, 0:1], ps[:, 3, 64:65], col[:, B_PATCH:B_PATCH + 1], ALU.add).then_inc(s["cst_a"], 1)
            dve.wait_ge(s["bias_ps"], 1)
            dve.tensor_copy(cst[:, 1:2], ps[:, 7, 80:81]).then_inc(s["cst_b"], 1)
            dve.tensor_copy(bo_c[:, :], ps[:, 7, 84:84 + DEPTH]).then_inc(s["cst_b"], 1)
            dve.tensor_copy(b2_c[:, :], ps[:, 7, 88:88 + DEPTH]).then_inc(s["cst_b"], 1)
            dve.tensor_tensor(b1_f[:, :], ps[:, 7, 92:92 + DEPTH], lay[:, B1, :], ALU.add).then_inc(s["prep_ready"], 1)
            def two_chunks(i):
                for u in range(2):
                    after(dve, "patch_st", i * 2 + (u - 1))
                    for q in range(4):
                        w = 4 * u + q + 1
                        dve.wait_ge(s["squares"], i * 8 + w)
                        dve.tensor_reduce(psq[:, u, q * 64:q * 64 + 64], sqp[:, q % 2, :].rearrange("p (n k) -> p n k", k=P),
                                          axis=AX.X, op=ALU.add).then_inc(s["sq_red"], 1)
                        dve.wait_ge(s["halves"], i * 8 + w)
                        dve.tensor_reduce(psm[:, u, q * 64:q * 64 + 64], half_sum[:, q % 2, :].rearrange("p (n k) -> p n k", k=P // 2),
                                          axis=AX.X, op=ALU.add).then_inc(s["sum_red"], 1)
                    dve.wait_ge(s["patch_mm"], i * 2 + (u + 1))
                    dve.tensor_scalar(yraw[:, bass.ds(i * (2 * PC) + u * PC, PC)], ps[:, u, 0:PC], 1.0, None, ALU.mult).then_inc(s["patch_out"], 1)
                    dve.wait_ge(s["patch_st"], i * 2 + (u + 1))
                    dve.tensor_scalar(sraw[:, bass.ds(i * 2 + u, 1), :].rearrange("p o n -> p (o n)"), ps[:, 2 + u, 0:2 * PC], 1.0 / PD,
                                      None, ALU.mult).then_inc(s["patch_out"], 1)

            two_chunks(0)
            with dve.Fori(1, NCH // 2) as i:
                two_chunks(i)
            dve.wait_ge(s["p_m2"], 1)
            dve.tensor_tensor(pvar.rearrange("p (k n) -> p k n", k=NCH), sraw[:, :, PC:2 * PC],
                              pm2.rearrange("p (k n) -> p k n", k=NCH), ALU.subtract).then_inc(s["p_var"], 1)
            dve.wait_ge(s["p_rs"], 1)
            dve.tensor_tensor(py, yraw, prs, ALU.mult).then_inc(s["p_y"], 1)
            dve.wait_ge(s["p_y"], 1)
            dve.wait_ge(s["cst_b"], 3)
            dve.tensor_scalar(py, py, cst[:, 1:2], None, ALU.add).then_inc(s["p_yc"], 1)
            dve.wait_ge(s["p_rs2"], 1)
            dve.tensor_tensor(py, py, prs, ALU.mult).then_inc(s["p_y"], 1)
            dve.wait_ge(s["p_y"], 2)
            dve.tensor_scalar(py, py, col[:, G2:G2 + 1], col[:, B2P:B2P + 1], ALU.mult, ALU.add).then_inc(s["p_y"], 1)
            dve.tensor_tensor(cst[:, 2:3], posT[:, 0:1], col[:, CLS:CLS + 1], ALU.add).then_inc(s["cls"], 1)
            dve.wait_ge(s["cls"], 1)
            dve.tensor_copy(x0[:, :, 0:1], cst[:, None, 2:3].to_broadcast([128, NPAIR, 1])).then_inc(s["cls"], 1)
            dve.wait_ge(s["p_y"], 3)
            dve.wait_ge(s["cls"], 2)
            dve.tensor_tensor(x0[:, :, 1:TOK], py.rearrange("p (m t) -> p m t", m=NPAIR),
                              posT[:, None, 1:TOK].to_broadcast([128, NPAIR, NP]), ALU.add).then_inc(s["x0"], 1)

            with dve.Fori(0, DEPTH) as l:
                def n(k):
                    return l * NCH + k
                for c in range(NCH):
                    dve.wait_ge(s["rstd"], n(c + 1))
                    dve.tensor_tensor(chunk(nrm, c), chunk(x, c), chunk(rstd, c), ALU.mult).then_inc(s["nrm"], 1)
                    dve.wait_ge(s["nrm"], n(c + 1))
                    dve.tensor_scalar(chunk(h, c), chunk(nrm, c), lay[:, GA, bass.ds(l, 1)], lay[:, BA, bass.ds(l, 1)],
                                      ALU.mult, ALU.add).then_inc(s["h"], 1)
                    dve.wait_ge(s["h"], n(c + 1))
                    if c == 0:
                        dve.wait_ge(s["pads"], 2)
                    dve.tensor_copy(hbd[64:128, c * CP:(c + 1) * CP, 1, 0:TOK], pairs(h, c, slice(64, 128))).then_inc(s["hb"], 1)
                for c in range(NCH):
                    g = slice(16 * c, 16 * c + 16)
                    sc = ps_s(c).rearrange("p (g k) -> p g k", k=TOK)
                    dve.wait_ge(s["sc"], n(c + 1))
                    dve.tensor_reduce(mx[:, g], sc, axis=AX.X, op=ALU.max).then_inc(s["mx"], 1)
                    dve.wait_ge(s["mx"], n(c + 1))
                    dve.tensor_tensor(ex[:, g, :], sc, mx[:, g, None].to_broadcast([128, 16, TOK]), ALU.subtract).then_inc(s["sub"], 1)
                    if c:
                        softmax_sum(dve, n, c - 1)
                    if c >= 2:
                        transposed(dve, n, c - 2)
                softmax_sum(dve, n, NCH - 1)
                transposed(dve, n, NCH - 2)
                transposed(dve, n, NCH - 1)
                for c in range(NCH):
                    dve.wait_ge(s["gps"], n(c + 1))
                    dve.tensor_copy(G[:, :, c * CP + 1:(c + 1) * CP:2, :].rearrange("p h i q -> p i h q"),
                                    ps_g(c)[:, 1, :].rearrange("p (i h q) -> p i h q", i=4, h=HEADS)[:, :, :, 0:TOK]).then_inc(s["gd"], 1)
                for c in range(NCH):
                    dve.wait_ge(s["ops"], n(c + 1))
                    dve.scalar_tensor_tensor(out=chunk(x, c), in0=ps_o(c), scalar=bo_c[:, bass.ds(l, 1)], in1=chunk(x, c),
                                             op0=ALU.add, op1=ALU.add).then_inc(s["att"], 1)
                for c in range(NCH):
                    dve.wait_ge(s["frs"], n(c + 1))
                    dve.tensor_tensor(chunk(nrm, c), chunk(x, c), chunk(rstd, c), ALU.mult).then_inc(s["fn"], 1)
                for c in range(NCH):
                    dve.wait_ge(s["yps"], n(c + 1))
                    dve.scalar_tensor_tensor(out=chunk(x, c), in0=ps_o(c), scalar=b2_c[:, bass.ds(l, 1)], in1=chunk(x, c),
                                             op0=ALU.add, op1=ALU.add).then_inc(s["ff"], 1)
            final_dve(dve)

        @block.gpsimd
        def _(pool):
            pool.memset(ident[:, :], 0.0).then_inc(s["cst_pool"], 1)
            pool.memset(ones[:, :], 1.0).then_inc(s["ones_ok"], 1)
            pool.memset(ones_bd[:, :], 0.0).then_inc(s["cst_pool"], 1)
            pool.memset(eps5[:, :], 1e-5).then_inc(s["cst_pool"], 1)
            pool.memset(eps8[:, :], 1e-8).then_inc(s["cst_pool"], 1)
            pool.memset(mu_all[:, :, :], 0.0).then_inc(s["cst_pool"], 1)
            pool.memset(vo_all[:, :, :], 0.0).then_inc(s["cst_pool"], 1)
            pool.wait_ge(s["cst_pool"], 4)
            pool.affine_select(out=ident[:, :], in_=ident[:, :], compare_op=ALU.not_equal, fill=1.0, base=0,
                               pattern=[[-1, 128]], channel_multiplier=1).then_inc(s["ident_ok"], 1)
            done = 0
            for f in range(2):
                r = slice(64 * f, 64 * f + 64)
                for part_, value in ((ones_bd[r, r], 1.0 / DIM), (ones_q[r, f, :], 1.0 / DIM), (ones_q[r, 1 - f, :], 0.0)):
                    if done:
                        pool.wait_ge(s["cst_c"], done)
                    else:
                        pool.wait_ge(s["ident_ok"], 1)
                    pool.memset(part_, value).then_inc(s["cst_c"], 1)
                    done += 1
            pool.wait_ge(s["cst_c"], done)
            pool.tensor_tensor(cen_bd[:, :], ident[:, :], ones_bd[:, :], ALU.subtract).then_inc(s["ones_ok"], 1)
            pool.memset(wv[:, :], 0.0).then_inc(s["wv_zero"], 1)
            pool.memset(tri[:, :, :], 1.0).then_inc(s["tri"], 1)
            pool.wait_ge(s["tri"], 1)
            pool.affine_select(out=tri[:, :, :], in_=tri[:, :, :], compare_op=ALU.is_gt, fill=0.0, base=0,
                               pattern=[[1, TOK], [-1, TOK]], channel_multiplier=0).then_inc(s["tri"], 1)
            def two_chunks(i):
                for u in range(2):
                    pool.wait_ge(s[f"x_in{u}"], i * (16 * LOADS) + 16 * LOADS)
                    for q in range(4):
                        after(pool, "sum_red", i * 8 + (4 * u + q - 1))
                        v = xin[:, u, q // 2, 4 * (q % 2):4 * (q % 2) + 4, :].rearrange("p m (g k) -> p (m g) k", k=P)
                        pool.tensor_tensor(half_sum[:, q % 2, :].rearrange("p (n k) -> p n k", k=P // 2), v[:, :, 0:P // 2],
                                           v[:, :, P // 2:P], ALU.add).then_inc(s["halves"], 1)

            two_chunks(0)
            with pool.Fori(1, NCH // 2) as i:
                two_chunks(i)
            pool.wait_ge(s["p_y"], 1)
            pool.memset(hbd[:, :, :, :], 0.0).then_inc(s["pads"], 1)
            pool.memset(pn[:, :, :], 0.0).then_inc(s["pads"], 1)
            with pool.Fori(0, DEPTH) as l:
                for c in range(NCH):
                    g = slice(16 * c, 16 * c + 16)
                    pool.wait_ge(s["ri"], l * NCH + (c + 1))
                    if c == 0:
                        pool.wait_ge(s["pads"], 2)
                    pool.tensor_tensor(pn[:, g, 0:TOK], ex[:, g, :], ri[:, g, None].to_broadcast([128, 16, TOK]), ALU.mult).then_inc(s["pn"], 1)
            final_pool(pool)


_NAMES = {"x": "x", **{n: "L0_tok_" + n for n in ("ln_p1_g ln_p1_b W_patch b_patch ln_p2_g ln_p2_b cls pos attn_ln_g attn_ln_b Wqkv Wo "
                                               "bo ff_ln_g ff_ln_b W1 b1 W2 b2 ln_f_g ln_f_b").split()},
          **{n: "L0_attn_" + n for n in "Wq bq Wk bk Wv bv gamma beta".split()},
          "wr": "L0_ffn_wr", "br": "L0_ffn_br", "fw1": "L0_ffn_w1", "fb1": "L0_ffn_b1", "fw2": "L0_ffn_w2", "fb2": "L0_ffn_b2"}


def kernel(**inputs):
    import numpy as np
    import concourse.bacc as bacc
    from concourse.bass_utils import run_bass_kernel_spmd

    nc = bacc.Bacc("TRN2", target_bir_lowering=False, num_devices=1)
    arrays, args = {}, {}
    for short, name in _NAMES.items():
        v = np.ascontiguousarray(inputs[name])
        arrays["in_" + short] = v
        args[short] = nc.dram_tensor("in_" + short, v.shape, mybir.dt.from_np(v.dtype), kind="ExternalInput").ap()
    out = nc.dram_tensor("out", (B, TOK, DIM), f32, kind="ExternalOutput").ap()
    vit_tower(nc, args, out)
    return run_bass_kernel_spmd(nc, [arrays], core_ids=[0]).results[0]["out"]
```

```python
import concourse.bass as bass
from concourse import mybir
from contextlib import ExitStack

B, CH, IMG, P = 128, 3, 128, 32
GRID = IMG // P
NP = GRID * GRID
TOK = NP + 1
DIM, DEPTH, HEADS, MLP, UNITS, HID = 64, 4, 4, 128, 128, 256
PD = CH * P * P
KP = CH * P
NPAIR = B // 2
COLS = NPAIR * TOK
NCH = 8
CP = NPAIR // NCH
CC = CP * TOK
PC = CP * NP
KSEL = int(0.5 * TOK) - 1
NEG = -2.0 ** 32 + 1.0
LOADS = 2 * CH * GRID
PAR_LOADS = 43

f32 = mybir.dt.float32
ALU = mybir.AluOpType
ACT = mybir.ActivationFunctionType
AX = mybir.AxisListType


def vit_tower(nc, a, out):
    with ExitStack() as ctx:
        def sb(name, *shape):
            return ctx.enter_context(nc.sbuf_tensor(name, list(shape), f32))

        class Signals(dict):
            def __missing__(self, name):
                self[name] = ctx.enter_context(nc.semaphore("s_" + name))
                return self[name]

        s = Signals()

        ps = ctx.enter_context(nc.psum_tensor("ps", [128, 8, 512], f32))

        ident = sb("ident", 128, 128)
        ones = sb("ones", 128, 128)
        ones_bd = sb("ones_bd", 128, 128)
        cen_bd = sb("cen_bd", 128, 128)
        ones_q = sb("ones_q", 128, 2, 32)
        eps5 = sb("eps5", 128, 1)
        eps8 = sb("eps8", 128, 1)
        col = sb("col", 128, 12)
        B_PATCH, G2, B2P, CLS, FG, FB, GAMMA, BETA, BV, FB2, WR, BR = range(12)
        posT = sb("posT", 128, TOK)
        lay = sb("lay", 128, 7, DEPTH)
        GA, BA, GF, BF, BO, B2, B1 = range(7)
        bo_c = sb("bo_c", 128, DEPTH)
        b2_c = sb("b2_c", 128, DEPTH)
        b1_f = sb("b1_f", 128, DEPTH)
        cur = sb("cur", 128, 3)
        arena = sb("arena", 128, 16384)
        xin = arena[0:KP, :].rearrange("p (u f m w) -> p u f m w", u=2, f=2, m=CP)
        o = 0

        def part(n):
            nonlocal o
            o += n
            return arena[:, o - n:o]

        U = part(HEADS * COLS).rearrange("p (h n) -> p h n", h=HEADS)
        G = part(HEADS * COLS).rearrange("p (h m t) -> p h m t", h=HEADS, m=NPAIR)
        htok = part(32 * 128).rearrange("p (i c) -> p i c", i=32)
        h = part(COLS)
        sq = part(COLS)
        arena2 = sb("arena2", 128, 8192)
        sqp = arena2[0:KP, 0:4096].rearrange("p (u n) -> p u n", u=2)
        half_sum = arena2[0:KP, 4096:6144].rearrange("p (u n) -> p u n", u=2)
        wtmp = arena2[0:KP, 6144:8192].rearrange("p (k d) -> p k d", k=P)
        ex = arena2[:, 0:2176].rearrange("p (g k) -> p g k", k=TOK)
        z = arena2[:, 2176:4352].rearrange("p (f n) -> p f n", f=2)
        x0 = z[:, 0, :].rearrange("p (m t) -> p m t", t=TOK)
        lnv = arena2[:, 4352:5440]
        rstd = arena2[:, 5440:6528]
        nrm = arena2[:, 6528:7616]
        wp = sb("wp", KP, P, DIM)
        gp = sb("gp", KP, 2, P)
        wred = sb("wred", KP, 3 * DIM)
        cst = sb("cst", 128, 4)
        x = sb("x", 128, COLS)
        pt = sb("pt", 128, 32, 2, HEADS * 32)
        pt_flat = pt[:, :, :, :].rearrange("p i j q -> p (i j q)")
        wqkv = pt_flat[0:64, 0:DEPTH * 768].rearrange("p (l g) -> p l g", l=DEPTH)
        wT = pt_flat[:, 3072:4608].rearrange("p (l g c) -> p l g c", l=DEPTH, g=6)
        wo = pt_flat[:, 4608:5120].rearrange("p (g d) -> p g d", d=DIM)
        w1 = pt_flat[:, 5120:5632].rearrange("p (l c) -> p l c", l=DEPTH)
        wo_r = sb("wo_r", 128, DEPTH * 2)
        w1f = sb("w1f", 128, DEPTH, MLP)
        w2 = sb("w2", 128, DEPTH, DIM)
        w2_r = sb("w2_r", 128, DEPTH)
        mu_all = sb("mu_all", 128, DEPTH, HEADS * 128)
        vo_all = sb("vo_all", 128, DEPTH, HEADS * 128)
        mu = sb("mu", 128, HEADS * 128)
        vo = sb("vo", 128, HEADS * 128)
        w1s = sb("w1s", 128, MLP)
        w2s = sb("w2s", 128, DIM)
        hbd = sb("hbd", 128, NPAIR, 2, 32)
        mx = sb("mx", 128, 32 * HEADS)
        sm = sb("sm", 128, 32 * HEADS)
        ri = sb("ri", 128, 32 * HEADS)
        pn = sb("pn", 128, 32 * HEADS, 32)
        pn_flat = pn[:, :, :].rearrange("p a b -> p (a b)")
        yraw = pn_flat[:, 0:NCH * PC]
        sraw = pn_flat[:, NCH * PC:3 * NCH * PC].rearrange("p (k n) -> p k n", k=NCH)
        psq, psm = (pn_flat[0:KP, (3 + k // 2) * 1024 + k % 2 * 512:(3 + k // 2) * 1024 + k % 2 * 512 + 512].rearrange("p (u n) -> p u n", u=2)
                    for k in range(2))
        pm2, pvar, pln, prs, py = (pt_flat[:, 3072 + 1024 * k:4096 + 1024 * k] for k in range(5))
        wqk = sb("wqk", 128, 2, UNITS)
        wv = sb("wv", 128, 128)
        fw1 = sb("fw1", 128, HID)
        fw2 = sb("fw2", 128, 2, DIM)
        fw2_r = sb("fw2_r", 128, 2)
        fcol = sb("fcol", 128, 4)
        wrb = sb("wrb", 128, 128)
        gt = arena2[:, 576:576 + 2 * TOK * TOK].rearrange("p (w t o) -> p w t o", w=2, t=TOK)
        tri = arena2[:, 1216:1216 + TOK * TOK].rearrange("p (t o) -> p t o", t=TOK)
        wimg = sb("wimg", 128, TOK)
        rank = sb("rank", 128, TOK)
        FIN_LOADS = 14
        NT = -(-COLS // 128)
        Q = arena[:, 0:2 * COLS].rearrange("p (f n) -> p f n", f=2)
        K = arena[:, 2 * COLS:4 * COLS].rearrange("p (f n) -> p f n", f=2)
        g_flat = arena[:, 4 * COLS:8 * COLS].rearrange("p (k n) -> p k n", k=4)
        nm, oo, hb, h1 = (g_flat[:, k, :] for k in range(4))
        wb = x
        selrow = z[:, 0, :]
        y_sel = z[:, 1, :]
        z2 = oo
        obuf = htok[:, 0:NT, :]

        def after(eng, signal, count):
            if not isinstance(count, int) or count > 0:
                eng.wait_ge(s[signal], count)

        def chunk(t, c):
            return t[:, c * CC:(c + 1) * CC]

        def pairs(t, c, r=slice(0, 128)):
            return t[r, c * CC:(c + 1) * CC].rearrange("p (m t) -> p m t", t=TOK)

        ps_u = ps[:, 0:2, 0:2 * CC]
        ps_t = ps[:, 2, :]
        ps_s = ps[:, 3, 0:4 * HEADS * TOK]
        ps_g = ps[:, 4:6, 0:4 * HEADS * TOK]
        ps_o = ps[:, 6, 0:CC]
        ps_v = ps[:, 7, 0:CC]

        def two_banks(c):
            return ps[:, 2 * (c % 2):2 * (c % 2) + 2, :]

        def ps_y(c):
            return ps[:, 4 + c % 2, 0:CC]

        def ps_w(c):
            return ps[:, 6 + c % 2, 0:CC]

        def diagonal(*stages):
            for t in range(NCH + max(lag for lag, _ in stages)):
                for lag, stage in sorted(stages, key=lambda x: -x[0]):
                    if 0 <= t - lag < NCH:
                        stage(t - lag)

        ps_qk = ps[:, 0:2, 0:2 * CC]
        ps_pv = ps[:, 4, :]
        ps_val = ps[:, 5, 0:CC]
        ps_key = ps[:, 6, 0:CC]
        score_cols = 4 * TOK

        def ps_oc(c):
            return ps[:, c % 2, 0:CC]

        def ps_ov(c):
            return ps[:, 2 + c % 2, 0:CC]

        def third(c):
            return ps[:, c // 3, c % 3 * CC:(c % 3 + 1) * CC]

        def tile_bank(t):
            return (0, 1, 2, 4, 5, 6)[t % 6]

        NT_BANKS = 6

        def final_sp(sp):
            sp.wait_ge(s["ws"], NCH)
            for f in range(2):
                sp.dma_start(wimg[64 * f:64 * f + 64, :], wb[64 * f:64 * f + 1, :].rearrange("o (m t) -> o m t", t=TOK)).then_inc(s["sel_img"], 16)
            sp.wait_ge(s["selm"], 1)
            sp.wait_ge(s["sel_zero"], 1)
            for f in range(2):
                sp.dma_start(selrow[64 * f:64 * f + 1, :].rearrange("o (m t) -> o m t", t=TOK), wimg[64 * f:64 * f + 64, :]).then_inc(s["sel_row"], 16)
            rows = out.rearrange("(f m) t d -> (m t) f d", f=2)
            for t in range(NT):
                w = min(128, COLS - 128 * t)
                sp.wait_ge(s["oo"], t + 1)
                sp.dma_start(rows[128 * t:128 * t + w, :, :], obuf[0:w, t, :].rearrange("p (f d) -> p f d", f=2)).then_inc(s["out_done"], 16)
            sp.wait_ge(s["out_done"], 16 * NT)

        def final_act(act):
            act.wait_ge(s["fin_in"], 16 * FIN_LOADS)

            def magnitude(c):
                act.wait_ge(s["dh"], c + 1)
                act.activation(chunk(sq, c), chunk(h, c), ACT.Abs).then_inc(s["ka"], 1)

            def biased(c):
                act.wait_ge(s["qps"], c + 1)
                act.activation(Q[:, :, c * CC:(c + 1) * CC], ps_qk[:, :, 0:CC], ACT.Identity, bias=fcol[:, 0:1]).then_inc(s["qa"], 1)
                act.activation(K[:, :, c * CC:(c + 1) * CC], ps_qk[:, :, CC:2 * CC], ACT.Identity, bias=fcol[:, 1:2]).then_inc(s["qa"], 1)
                act.wait_ge(s["vps"], c + 1)
                act.activation(chunk(nrm, c), ps_val, ACT.Identity, bias=col[:, BV:BV + 1]).then_inc(s["va"], 1)

            def values_out(c):
                act.wait_ge(s["vtp"], c + 1)
                act.activation(htok[:, 4 * c:4 * c + 4, :], ps_t.rearrange("p (i c) -> p i c", i=4), ACT.Copy).then_inc(s["vtk"], 1)

            def exponential(c):
                act.wait_ge(s["dsub"], c + 1)
                act.activation(ex[:, 4 * c:4 * c + 4, :], ex[:, 4 * c:4 * c + 4, :], ACT.Exp, scale=UNITS ** -0.5).then_inc(s["dex"], 1)

            diagonal((0, magnitude), (1, biased), (3, values_out), (3, exponential))

            def square(c, place, ready, squared):
                act.wait_ge(s[ready], c + 1)
                act.activation(chunk(sq, c), place(c), ACT.Square).then_inc(s[squared], 1)

            def rstd_of(c, place, eps, var, ln, rs):
                act.wait_ge(s[var], c + 1)
                act.activation(chunk(lnv, c), place(c), ACT.Ln, bias=eps).then_inc(s[ln], 1)
                act.wait_ge(s[ln], c + 1)
                act.activation(chunk(rstd, c), chunk(lnv, c), ACT.Exp, scale=-0.5).then_inc(s[rs], 1)

            diagonal((0, lambda c: square(c, ps_oc, "oc", "osq")), (1, lambda c: rstd_of(c, ps_ov, eps8[:, :], "ovar", "oln", "ors")),
                     (3, lambda c: square(c, ps_y, "rc", "rsq")), (4, lambda c: rstd_of(c, lambda c: ps[:, 6, 0:CC], eps5[:, :], "rvar", "rln", "rrs")))

            def hidden(c):
                act.wait_ge(s["fz"], c + 1)
                for g in range(2):
                    act.activation(U[:, 2 * g:2 * g + 2, c * CC:(c + 1) * CC], two_banks(c)[:, :, g * CC:(g + 1) * CC], ACT.Gelu_apprx_tanh,
                                   bias=fcol[:, 2 + g:3 + g]).then_inc(s["fg"], 1)

            def mlp_out(c):
                act.wait_ge(s["fy"], c + 1)
                act.activation(chunk(y_sel, c), ps_y(c), ACT.Identity, bias=cst[:, 1:2]).then_inc(s["ysb"], 1)

            diagonal((0, hidden), (2, mlp_out))
            act.preload_act_table_set("natural_log_exp_and_others")

            def routed_square(c):
                act.wait_ge(s["z2"], c + 1)
                act.activation(chunk(sq, c), chunk(z2, c), ACT.Square).then_inc(s["zsq"], 1)

            def tile_out(t):
                w = min(128, COLS - 128 * t)
                act.wait_ge(s["ops2"], t + 1)
                act.activation(obuf[0:w, t, :], ps[0:w, tile_bank(t), 0:128], ACT.Copy).then_inc(s["oo"], 1)

            diagonal((0, routed_square), (1, lambda c: rstd_of(c, lambda c: ps[:, 3 + c % 2 * 4, 0:CC], eps5[:, :], "zvar", "zln", "zrs")),
                     (4, tile_out))
            for t in range(NCH, NT):
                tile_out(t)

        def final_pe(pe):
            pe.wait_ge(s["fin_in"], 16 * FIN_LOADS)

            def free(signal, c, each=1, places=1):
                if c >= places:
                    pe.wait_ge(s[signal], each * (c - places + 1))

            def project(c):
                pe.wait_ge(s["dh"], c + 1)
                free("qa", c, 2)
                for f in range(2):
                    for w in range(2):
                        r = slice(64 * f, 64 * f + 64)
                        mm = pe.matmul(ps_qk[:, f, w * CC:(w + 1) * CC], wqk[r, w, :], h[r, c * CC:(c + 1) * CC], start=True, stop=True)
                mm.then_inc(s["qps"], 1)
                free("va", c)
                pe.matmul(ps_val, wv[:, :], chunk(h, c), start=True, stop=True).then_inc(s["vps"], 1)
                pe.wait_ge(s["ka"], c + 1)
                free("key", c)
                pe.matmul(ps_key, ones_bd[:, :], chunk(sq, c), start=True, stop=True).then_inc(s["kps"], 1)

            def attend(c):
                pe.wait_ge(s["leaky"], 4 * (c + 1))
                free("vtk", c)
                for i in range(4):
                    m = c * CP + 2 * i
                    mm = pe.transpose(ps_t[:, i * 128:i * 128 + 128], hbd[:, m:m + 2, :, :].rearrange("p j f k -> p (j f k)"), ident[:, :])
                mm.then_inc(s["vtp"], 1)
                pe.wait_ge(s["key"], c + 1)
                free("dsub", c)
                for j in range(2):
                    pe.matmul(ps[64 * j:64 * j + 64, 3, 0:score_cols], ones_q[:, :, :].rearrange("p f q -> p (f q)"),
                              nm[:, :].rearrange("p (m t) -> p m t", t=TOK)[:, c * CP + j:(c + 1) * CP:2, :], start=True, stop=False,
                              skip_group_check=True)
                    for f in range(2):
                        for i in range(4):
                            m = c * CP + 2 * i + j
                            r = 64 * j + 32 * f
                            mm = pe.matmul(ps[r:r + TOK, 3, i * TOK:(i + 1) * TOK], Q[:, f, m * TOK:(m + 1) * TOK],
                                           K[:, f, m * TOK:(m + 1) * TOK], start=False, stop=True, skip_group_check=True)
                mm.then_inc(s["dsc"], 1)

            def probabilities_by_values(c):
                pe.wait_ge(s["dpt"], 2 * (c + 1))
                pe.wait_ge(s["vtk"], c + 1)
                free("pvs", c)
                for i in range(4):
                    mm = pe.matmul(ps_pv[:, i * 128:i * 128 + 128], htok[:, 4 * c + i, :], pt[:, 4 * c + i, :, 0:64], start=True, stop=True)
                mm.then_inc(s["pv"], 1)

            diagonal((1, project), (3, attend), (6, probabilities_by_values))

            def centre_attended(c):
                pe.wait_ge(s["pvs"], c + 1)
                free("on", c, places=2)
                pe.matmul(ps_oc(c), cen_bd[:, :], chunk(oo, c), start=True, stop=True).then_inc(s["oc"], 1)

            def variance_attended(c):
                pe.wait_ge(s["osq"], c + 1)
                free("oln", c, places=2)
                pe.matmul(ps_ov(c), ones_bd[:, :], chunk(sq, c), start=True, stop=True).then_inc(s["ovar"], 1)

            def centre_sum(c):
                pe.wait_ge(s["on"], c + 1)
                pe.wait_ge(s["hb"], NCH)
                free("h1", c, places=2)
                pe.matmul(ps_y(c), cen_bd[:, :], chunk(nrm, c), start=True, stop=False)
                pe.matmul(ps_y(c), cen_bd[:, :], chunk(hb, c), start=False, stop=True).then_inc(s["rc"], 1)

            def variance_sum(c):
                pe.wait_ge(s["rsq"], c + 1)
                free("rln", c)
                pe.matmul(ps[:, 6, 0:CC], ones_bd[:, :], chunk(sq, c), start=True, stop=True).then_inc(s["rvar"], 1)

            def routing_weight(c):
                pe.wait_ge(s["h1"], c + 1)
                if c == 0:
                    pe.wait_ge(s["wrb"], 1)
                free("ws", c)
                pe.matmul(ps[:, 7, 0:CC], wrb[:, :], chunk(h1, c), start=True, stop=True).then_inc(s["wps"], 1)

            diagonal((0, centre_attended), (1, variance_attended), (3, centre_sum), (4, variance_sum), (6, routing_weight))

            def hidden(c):
                free("fg", c, 2, places=2)
                for f in range(2):
                    r = slice(64 * f, 64 * f + 64)
                    for g in range(2):
                        mm = pe.matmul(two_banks(c)[:, f, g * CC:(g + 1) * CC], fw1[r, g * 128:g * 128 + 128], h1[r, c * CC:(c + 1) * CC],
                                       start=True, stop=True)
                mm.then_inc(s["fz"], 1)

            def mlp_out(c):
                if c == 0:
                    pe.wait_ge(s["fw2_c"], 3)
                pe.wait_ge(s["fg"], 2 * (c + 1))
                free("ysb", c, places=2)
                for f in range(2):
                    for g in range(2):
                        mm = pe.matmul(ps_y(c)[64 * f:64 * f + 64, :], fw2[:, g, :], U[:, 2 * g + f, c * CC:(c + 1) * CC],
                                       start=(g == 0), stop=(g == 1))
                mm.then_inc(s["fy"], 1)

            diagonal((0, hidden), (1, mlp_out))
            pe.wait_ge(s["sel_row"], 32)
            pe.wait_ge(s["ws"], NCH)
            for k in range(3):
                w = slice(3 * k * CC, min(3 * (k + 1), NCH) * CC)
                pe.matmul(ps[:, k, 0:w.stop - w.start], ones_bd[:, :], selrow[:, w], start=True, stop=True).then_inc(s["selps"], 1)

            def variance_routed(c):
                pe.wait_ge(s["zsq"], c + 1)
                free("zln", c, places=2)
                pe.matmul(ps[:, 3 + c % 2 * 4, 0:CC], ones_bd[:, :], chunk(sq, c), start=True, stop=True).then_inc(s["zvar"], 1)

            def tile(t):
                w = min(128, COLS - 128 * t)
                pe.wait_ge(s["zo"], min(t + 1, NCH))
                pe.wait_ge(s["y2"], NCH)
                free("oo", t, places=NT_BANKS)
                pe.transpose(ps[0:w, tile_bank(t), 0:128], nrm[:, 128 * t:128 * t + w], ident[:, :]).then_inc(s["ops2"], 1)

            diagonal((1, variance_routed), (4, tile))
            for t in range(NCH, NT):
                tile(t)

        def final_dve(dve):
            dve.wait_ge(s["par_in"], 16 * PAR_LOADS)
            dve.tensor_scalar(wrb[:, :], ones_bd[:, :], col[:, WR:WR + 1], float(DIM), ALU.mult, ALU.mult).then_inc(s["wrb"], 1)

            def normalised(c):
                dve.wait_ge(s["rstd"], (DEPTH * NCH) + c + 1)
                dve.tensor_tensor(chunk(nrm, c), chunk(x, c), chunk(rstd, c), ALU.mult).then_inc(s["dn"], 1)
                dve.wait_ge(s["dn"], c + 1)
                dve.tensor_scalar(chunk(h, c), chunk(nrm, c), col[:, FG:FG + 1], col[:, FB:FB + 1], ALU.mult, ALU.add).then_inc(s["dh"], 1)

            def keys(c):
                dve.wait_ge(s["kps"], c + 1)
                dve.tensor_scalar(chunk(nm, c), ps_key, 0.0, NEG * UNITS ** 0.5, ALU.is_equal, ALU.mult).then_inc(s["key"], 1)

            def leaky(c):
                dve.wait_ge(s["qa"], 2 * (c + 1))
                for w in (Q, K):
                    v = w[:, :, c * CC:(c + 1) * CC]
                    dve.scalar_tensor_tensor(out=v, in0=v, scalar=0.2, in1=v, op0=ALU.mult, op1=ALU.max).then_inc(s["leaky"], 1)
                dve.wait_ge(s["va"], c + 1)
                for f in range(2):
                    v = pairs(nrm, c, slice(64 * f, 64 * f + 64))
                    dve.scalar_tensor_tensor(out=hbd[64 * f:64 * f + 64, c * CP:(c + 1) * CP, f, 0:TOK], in0=v, scalar=0.2, in1=v,
                                             op0=ALU.mult, op1=ALU.max).then_inc(s["leaky"], 1)

            def less_maximum(c):
                g = slice(4 * c, 4 * c + 4)
                sc = ps[:, 3, 0:score_cols].rearrange("p (g k) -> p g k", k=TOK)
                dve.wait_ge(s["dsc"], c + 1)
                dve.tensor_reduce(mx[:, g], sc, axis=AX.X, op=ALU.max).then_inc(s["dmx"], 1)
                dve.wait_ge(s["dmx"], c + 1)
                dve.tensor_tensor(ex[:, g, :], sc, mx[:, g, None].to_broadcast([128, 4, TOK]), ALU.subtract).then_inc(s["dsub"], 1)

            def softmax_sum(c):
                g = slice(4 * c, 4 * c + 4)
                dve.wait_ge(s["dex"], c + 1)
                dve.tensor_reduce(sm[:, g], ex[:, g, :], axis=AX.X, op=ALU.add).then_inc(s["dsm"], 1)
                dve.wait_ge(s["dsm"], c + 1)
                dve.reciprocal(ri[:, g], sm[:, g]).then_inc(s["dri"], 1)

            def transposed(c):
                dve.wait_ge(s["dpn"], c + 1)
                for j in range(2):
                    r = slice(64 * j, 64 * j + 64)
                    dve.transpose(pt[r, 4 * c:4 * c + 4, j, 0:32], pn[r, 4 * c:4 * c + 4, :]).then_inc(s["dpt"], 1)

            def attended(c):
                dve.wait_ge(s["pv"], c + 1)
                dve.tensor_tensor(pairs(oo, c), ps_pv.rearrange("p (m q) -> p m q", q=64)[:, :, 0:TOK], pairs(h, c), ALU.add).then_inc(s["pvs"], 1)

            diagonal((0, normalised), (1, keys), (2, leaky), (3, less_maximum), (4, softmax_sum), (5, transposed), (7, attended))

            def scaled(c):
                dve.wait_ge(s["ors"], c + 1)
                dve.scalar_tensor_tensor(out=chunk(nrm, c), in0=ps_oc(c), scalar=col[:, GAMMA:GAMMA + 1], in1=chunk(rstd, c),
                                         op0=ALU.mult, op1=ALU.mult).then_inc(s["on"], 1)

            def renormalised(c):
                dve.wait_ge(s["rrs"], c + 1)
                dve.tensor_tensor(chunk(h1, c), ps_y(c), chunk(rstd, c), ALU.mult).then_inc(s["h1"], 1)

            def weight_out(c):
                dve.wait_ge(s["wps"], c + 1)
                dve.tensor_scalar(chunk(wb, c), ps[:, 7, 0:CC], col[:, BR:BR + 1], float(DIM), ALU.add, ALU.mult).then_inc(s["ws"], 1)

            diagonal((2, scaled), (5, renormalised), (6, weight_out))
            dve.tensor_reduce(fw2_r[:, :], fw2[:, :, :], axis=AX.X, op=ALU.add).then_inc(s["fw2_c"], 1)
            dve.wait_ge(s["fw2_c"], 1)
            dve.tensor_scalar(fw2_r[:, :], fw2_r[:, :], 1.0 / DIM, None, ALU.mult).then_inc(s["fw2_c"], 1)
            dve.wait_ge(s["fw2_c"], 2)
            dve.tensor_tensor(fw2[:, :, :], fw2[:, :, :], fw2_r[:, :, None].to_broadcast([128, 2, DIM]), ALU.subtract).then_inc(s["fw2_c"], 1)
            dve.wait_ge(s["sel_img"], 32)
            heavier, same = gt[:, 0, :, :], gt[:, 1, :, :]
            mine, other = wimg[:, :, None].to_broadcast([128, TOK, TOK]), wimg[:, None, :].to_broadcast([128, TOK, TOK])
            dve.tensor_tensor(heavier, other, mine, ALU.is_gt).then_inc(s["compared"], 1)
            dve.tensor_tensor(same, other, mine, ALU.is_equal).then_inc(s["compared"], 1)
            dve.wait_ge(s["compared"], 2)
            dve.wait_ge(s["tri"], 2)
            dve.tensor_tensor(same, same, tri[:, :, :], ALU.mult).then_inc(s["compared"], 1)
            dve.wait_ge(s["compared"], 3)
            dve.tensor_tensor(heavier, heavier, same, ALU.add).then_inc(s["compared"], 1)
            dve.wait_ge(s["compared"], 4)
            dve.tensor_reduce(rank[:, :], heavier, axis=AX.X, op=ALU.add).then_inc(s["compared"], 1)
            dve.wait_ge(s["compared"], 5)
            dve.scalar_tensor_tensor(out=wimg[:, :], in0=rank[:, :], scalar=float(KSEL), in1=wimg[:, :], op0=ALU.is_lt, op1=ALU.mult).then_inc(s["selm"], 1)

            def routed(c):
                dve.wait_ge(s["selps"], c // 3 + 1)
                dve.wait_ge(s["ysb"], c + 1)
                dve.tensor_tensor(chunk(y_sel, c), third(c), chunk(y_sel, c), ALU.mult).then_inc(s["y2"], 1)
                dve.wait_ge(s["y2"], c + 1)
                dve.scalar_tensor_tensor(out=chunk(z2, c), in0=chunk(h1, c), scalar=2.0, in1=chunk(y_sel, c), op0=ALU.mult, op1=ALU.add).then_inc(s["z2"], 1)

            def output(c):
                dve.wait_ge(s["zrs"], c + 1)
                dve.tensor_tensor(chunk(nrm, c), chunk(z2, c), chunk(rstd, c), ALU.mult).then_inc(s["zo"], 1)

            for c in range(NCH):
                routed(c)
            for c in range(NCH):
                output(c)

        def final_pool(pool):
            pool.memset(tri[:, :, :], 1.0).then_inc(s["tri"], 1)
            pool.wait_ge(s["tri"], 1)
            pool.affine_select(out=tri[:, :, :], in_=tri[:, :, :], compare_op=ALU.is_gt, fill=0.0, base=0,
                               pattern=[[1, TOK], [-1, TOK]], channel_multiplier=0).then_inc(s["tri"], 1)
            for c in range(NCH):
                pool.wait_ge(s["dri"], c + 1)
                g = slice(4 * c, 4 * c + 4)
                pool.tensor_tensor(pn[:, g, 0:TOK], ex[:, g, :], ri[:, g, None].to_broadcast([128, 4, TOK]), ALU.mult).then_inc(s["dpn"], 1)
            for c in range(NCH):
                pool.wait_ge(s["dh"], c + 1)
                pool.tensor_scalar(chunk(hb, c), chunk(h, c), col[:, BETA:BETA + 1], None, ALU.add).then_inc(s["hb"], 1)
            pool.memset(selrow, 0.0).then_inc(s["sel_zero"], 1)

        block = ctx.enter_context(nc.Block())

        @block.sync
        def _(sp):
            sp.dma_start(wp[:, :, :], a["W_patch"].rearrange("(q k) d -> q k d", q=KP)).then_inc(s["w_in"], 16)
            sp.dma_start(gp[:, 0, :], a["ln_p1_g"].rearrange("(q k) -> q k", q=KP)).then_inc(s["w_in"], 16)
            sp.dma_start(gp[:, 1, :], a["ln_p1_b"].rearrange("(q k) -> q k", q=KP)).then_inc(s["w_in"], 16)

            def load(u, first):
                for f in range(2):
                    for c in range(CH):
                        for g in range(GRID):
                            img = a["x"][bass.ds(first + f * NPAIR, CP), c, g * P:(g + 1) * P, :]
                            sp.dma_start(xin[c * P:(c + 1) * P, u, f, :, g * IMG:(g + 1) * IMG],
                                         img.rearrange("b r w -> r b w")).then_inc(s[f"x_in{u}"], 16)

            for u in range(2):
                load(u, u * CP)
            with sp.Fori(1, NCH // 2) as i:
                for u in range(2):
                    first, products, parts = sp.snap(i * (2 * CP) + u * CP), sp.snap(i * 2 + (u - 1)), sp.snap(i * 8 + 4 * (u - 1))
                    sp.wait_ge(s["patch_mm"], products)
                    sp.wait_ge(s["squares"], parts)
                    sp.wait_ge(s["halves"], parts)
                    load(u, first)
            sp.wait_ge(s["wv_zero"], 1)
            for f in range(2):
                r = slice(64 * f, 64 * f + 64)
                sp.dma_start(wqk[r, 0, :], a["Wq"]).then_inc(s["fin_in"], 16)
                sp.dma_start(wqk[r, 1, :], a["Wk"]).then_inc(s["fin_in"], 16)
                sp.dma_start(wv[r, r], a["Wv"]).then_inc(s["fin_in"], 16)
                sp.dma_start(fw1[r, :], a["fw1"]).then_inc(s["fin_in"], 16)
                sp.dma_start(fcol[:, 2 + f:3 + f], a["fb1"][f * 128:f * 128 + 128].rearrange("(d o) -> d o", o=1)).then_inc(s["fin_in"], 16)
                sp.dma_start(fw2[:, f, :], a["fw2"][f * 128:f * 128 + 128, :]).then_inc(s["fin_in"], 16)
            sp.dma_start(fcol[:, 0:1], a["bq"].rearrange("(d o) -> d o", o=1)).then_inc(s["fin_in"], 16)
            sp.dma_start(fcol[:, 1:2], a["bk"].rearrange("(d o) -> d o", o=1)).then_inc(s["fin_in"], 16)
            sp.wait_ge(s["prep_ready"], 3)
            for l in range(DEPTH):
                for slot, bank, free in (("slot_mu", mu_all, "ups"), ("slot_vo", vo_all, "ops"), ("slot_w1", w1f, "zps"), ("slot_w2", w2, "yps")):
                    to = {"slot_mu": mu, "slot_vo": vo, "slot_w1": w1s, "slot_w2": w2s}[slot]
                    sp.wait_ge(s[free], l * NCH)
                    sp.dma_start(to[:, :], bank[:, l, :]).then_inc(s[slot], 16)
            final_sp(sp)

        @block.scalar
        def _(act):
            for f in range(2):
                r = slice(64 * f, 64 * f + 64)
                for n, j in (("b_patch", B_PATCH), ("ln_p2_g", G2), ("ln_p2_b", B2P), ("ln_f_g", FG), ("ln_f_b", FB),
                             ("gamma", GAMMA), ("beta", BETA), ("bv", BV), ("fb2", FB2)):
                    act.dma_start(col[r, j:j + 1], a[n].rearrange("(d o) -> d o", o=1)).then_inc(s["par_in"], 16)
                act.dma_start(col[r, CLS:CLS + 1], a["cls"].rearrange("a b d -> d (a b)"), allow_slow_non_contiguous=True).then_inc(s["par_in"], 16)
                act.dma_start(col[r, WR:WR + 1], a["wr"]).then_inc(s["par_in"], 16)
                act.dma_start(col[r, BR:BR + 1], a["br"].rearrange("(o b) -> o b", o=1).to_broadcast([64, 1])).then_inc(s["par_in"], 16)
                act.dma_start(posT[r, :], a["pos"].rearrange("a t d -> d (a t)"), allow_slow_non_contiguous=True).then_inc(s["par_in"], 16)
                for n, j in (("attn_ln_g", GA), ("attn_ln_b", BA), ("ff_ln_g", GF), ("ff_ln_b", BF), ("bo", BO), ("b2", B2)):
                    act.dma_start(lay[r, j, :], a[n].rearrange("l d -> d l"), allow_slow_non_contiguous=True).then_inc(s["par_in"], 16)
                act.dma_start(w1[r, :, :], a["W1"].rearrange("l c d -> c l d")).then_inc(s["par_in"], 16)
            act.dma_start(lay[:, B1, :], a["b1"].rearrange("l d -> d l"), allow_slow_non_contiguous=True).then_inc(s["par_in"], 16)
            act.dma_start(w2[:, :, :], a["W2"].rearrange("l c d -> c l d")).then_inc(s["par_in"], 16)
            act.dma_start(wqkv, a["Wqkv"].rearrange("l c d -> c l d")).then_inc(s["wq_in"], 16)
            act.dma_start(wo, a["Wo"].rearrange("l (g q) d -> q (l g) d", q=128)).then_inc(s["par_in"], 16)

            def squares(i, u):
                act.wait_ge(s[f"x_in{u}"], i * (16 * LOADS) + 16 * LOADS)
                for q in range(4):
                    after(act, "sq_red", i * 8 + (4 * u + q - 1))
                    act.activation(sqp[:, q % 2, :].rearrange("p (m w) -> p m w", m=4),
                                   xin[:, u, q // 2, 4 * (q % 2):4 * (q % 2) + 4, :], ACT.Square).then_inc(s["squares"], 1)

            squares(0, 0)
            squares(0, 1)
            for l in range(DEPTH):
                act.wait_ge(s["qt"], l + 1)
                act.activation(wT[:, l, :, :], ps[:, 4 + l % 2, 0:384].rearrange("p (g c) -> p g c", g=6), ACT.Copy).then_inc(s["qt_sb"], 1)
            act.wait_ge(s["cst_pool"], 6)
            for l in range(DEPTH):
                for bank, to, signal, scale in ((6, mu_all, "mups", DIM ** -0.5), (4, vo_all, "vops", 1.0)):
                    act.wait_ge(s[signal], l + 1)
                    for f in range(2):
                        r = slice(64 * f, 64 * f + 64)
                        act.activation(to[r, l, :].rearrange("p (a b c) -> p b a c", b=2, c=128)[:, :, :, r],
                                       ps[r, bank:bank + 2, 0:128].rearrange("p b (a c) -> p b a c", a=2), ACT.Copy,
                                       scale=scale).then_inc(s["mu_sb"], 1)
            act.wait_ge(s["mu_sb"], 4 * DEPTH)
            act.activation(eps8[:, :], eps8[:, :], ACT.Copy).then_inc(s["prep_ready"], 1)
            with act.Fori(1, NCH // 2) as i:
                squares(i, 0)
                squares(i, 1)
            act.preload_act_table_set("natural_log_exp_and_others")

            def rstd_of(half, var, ready, ln, rs):
                w = slice(512 * half, 512 * half + 512)
                act.wait_ge(s[ready], half + 1)
                act.activation(pln[:, w], var, ACT.Ln, bias=eps5[:, :]).then_inc(s[ln], 1)
                act.wait_ge(s[ln], half + 1)
                act.activation(prs[:, w], pln[:, w], ACT.Exp, scale=-0.5).then_inc(s[rs], 1)

            for half in range(2):
                w = slice(512 * half, 512 * half + 512)
                act.wait_ge(s["st_out"], 4 * half + 4)
                act.activation(pm2[:, w].rearrange("p (k n) -> p k n", k=4), sraw[:, 4 * half:4 * half + 4, 0:PC], ACT.Square).then_inc(s["p_m2"], 1)
                rstd_of(half, pvar[:, w], "p_var", "p_ln", "p_rs")
            for half in range(2):
                w = slice(512 * half, 512 * half + 512)
                act.wait_ge(s["p_cen"], half + 1)
                act.activation(pm2[:, w], ps[:, half, :], ACT.Square).then_inc(s["p_sq"], 1)
                act.activation(py[:, w], ps[:, half, :], ACT.Copy).then_inc(s["p_yc"], 1)
            for half in range(2):
                rstd_of(half, ps[:, 2 + half, :], "p_v2", "p_ln2", "p_rs2")

            def stream_square(c, count):
                act.wait_ge(s["ff"], count + (c + 1))
                act.activation(chunk(sq, c), chunk(x, c), ACT.Square).then_inc(s["sq"], 1)

            def stream_rstd(c, count):
                act.wait_ge(s["var"], count + (c + 1))
                act.activation(chunk(lnv, c), ps_w(c), ACT.Ln, bias=eps5[:, :]).then_inc(s["lnv"], 1)
                act.wait_ge(s["lnv"], count + (c + 1))
                act.activation(chunk(rstd, c), chunk(lnv, c), ACT.Exp, scale=-0.5).then_inc(s["rstd"], 1)

            def embedded(c):
                act.wait_ge(s["cen"], c + 1)
                act.activation(chunk(x, c), ps_y(c), ACT.Copy).then_inc(s["ff"], 1)

            diagonal((0, embedded), (0, lambda c: stream_square(c, 0)), (2, lambda c: stream_rstd(c, 0)))
            act.wait_ge(s["prep_ready"], 3)
            with act.Fori(0, DEPTH) as l:
                def n(k):
                    return l * NCH + k

                act.activation(cur[:, 0:2], lay[:, GA:BA + 1, bass.ds(l, 1)].rearrange("p a o -> p (a o)"), ACT.Copy).then_inc(s["cur"], 1)
                act.activation(cur[:, 2:3], b1_f[:, bass.ds(l, 1)], ACT.Copy).then_inc(s["cur"], 1)

                def own_half(c):
                    act.wait_ge(s["nrm"], n(c + 1))
                    if c == 0:
                        act.wait_ge(s["cur"], l * 2 + 2)
                        act.wait_ge(s["pads"], 1)
                    for f in range(2):
                        r = slice(64 * f, 64 * f + 64)
                        act.activation(hbd[r, c * CP:(c + 1) * CP, f, 0:TOK], pairs(nrm, c, r), ACT.Identity,
                                       bias=cur[r, 1:2], scale=cur[r, 0:1]).then_inc(s["ha"], 1)

                def u_out(c):
                    act.wait_ge(s["ups"], n(c + 1))
                    act.activation(U[:, :, c * CC:(c + 1) * CC].rearrange("p (a b) n -> p a b n", a=2),
                                   ps_u.rearrange("p a (b n) -> p a b n", b=2), ACT.Copy).then_inc(s["u"], 1)

                def tokens_out(c):
                    act.wait_ge(s["tps"], n(c + 1))
                    act.activation(htok[:, 4 * c:4 * c + 4, :], ps_t.rearrange("p (i c) -> p i c", i=4), ACT.Copy).then_inc(s["tk"], 1)

                def exponential(c):
                    act.wait_ge(s["sub"], n(c + 1))
                    act.activation(ex[:, 16 * c:16 * c + 16, :], ex[:, 16 * c:16 * c + 16, :], ACT.Exp).then_inc(s["ex"], 1)

                def g_out(c):
                    act.wait_ge(s["gps"], n(c + 1))
                    for b in range(2):
                        m = c * CP + 4 * b
                        act.activation(G[:, :, m:m + 4, :].rearrange("p h m q -> p m h q"),
                                       ps_g[:, b, :].rearrange("p (m h q) -> p m h q", m=4, h=HEADS), ACT.Copy).then_inc(s["ga"], 1)

                def mlp_square(c):
                    act.wait_ge(s["att"], n(c + 1))
                    act.activation(chunk(sq, c), chunk(x, c), ACT.Square).then_inc(s["fsq"], 1)

                def mlp_rstd(c):
                    act.wait_ge(s["fvar"], n(c + 1))
                    act.activation(chunk(lnv, c), ps_v, ACT.Ln, bias=eps5[:, :]).then_inc(s["fln"], 1)
                    act.wait_ge(s["fln"], n(c + 1))
                    act.activation(chunk(rstd, c), chunk(lnv, c), ACT.Exp, scale=-0.5).then_inc(s["frs"], 1)

                diagonal((0, own_half), (1, u_out), (1, tokens_out), (2, exponential), (5, g_out), (6, mlp_square), (7, mlp_rstd))
                for c in range(NCH):
                    act.wait_ge(s["zps"], n(c + 1))
                    act.activation(z[:, :, c * CC:(c + 1) * CC], two_banks(c)[:, :, 0:CC], ACT.Gelu, bias=cur[:, 2:3]).then_inc(s["z"], 1)
                act.preload_act_table_set("natural_log_exp_and_others")
                diagonal((0, lambda c: stream_square(c, n(NCH))), (2, lambda c: stream_rstd(c, n(NCH))))
                act.wait_ge(s["z"], n(NCH))
            final_act(act)

        @block.tensor
        def _(pe):
            pe.wait_ge(s["ones_ok"], 2)
            pe.wait_ge(s["wp_c"], 1)
            pe.matmul(ps[0:KP, 7, 0:DIM], ones[0:KP, 0:KP], wred[:, 0:DIM], start=True, stop=True).then_inc(s["colmean"], 1)

            def products(i, u, between=None):
                pe.wait_ge(s[f"x_in{u}"], i * (16 * LOADS) + 16 * LOADS)
                after(pe, "y_out", i * 2 + (u - 1))
                for k in range(P):
                    if between and k == P // 2:
                        between()
                    for f in range(2):
                        mm = pe.matmul(ps[64 * f:64 * f + 64, u, 0:PC], wp[:, k, :],
                                       xin[:, u, f, :, :].rearrange("p m (g k) -> p (m g) k", k=P)[:, :, k],
                                       start=(k == 0), stop=(k == P - 1))
                mm.then_inc(s["patch_mm"], 1)

            def statistics(i, u):
                pe.wait_ge(s["sq_red"], i * 8 + 4 * (u + 1))
                pe.wait_ge(s["sum_red"], i * 8 + 4 * (u + 1))
                after(pe, "st_out", i * 2 + (u - 1))
                for f in range(2):
                    for w, part_sums in ((0, psm), (1, psq)):
                        mm = pe.matmul(ps[64 * f:64 * f + 64, 2 + u % 2, w * PC:(w + 1) * PC], ones[0:KP, 0:64],
                                       part_sums[:, u % 2, f * PC:(f + 1) * PC], start=True, stop=True)
                mm.then_inc(s["patch_st"], 1)

            pe.wait_ge(s["wp_ready"], 1)
            products(0, 0)
            products(0, 1, lambda: statistics(0, 0))
            pe.wait_ge(s["ident_ok"], 1)
            pe.wait_ge(s["wq_in"], 16)
            for l in range(DEPTH):
                if l >= 2:
                    pe.wait_ge(s["qt_sb"], l - 1)
                for g in range(6):
                    mm = pe.transpose(ps[:, 4 + l % 2, g * 64:g * 64 + 64], wqkv[:, l, g * 128:g * 128 + 128], ident[0:64, 0:64])
                mm.then_inc(s["qt"], 1)
            pe.wait_ge(s["qt_sb"], DEPTH)
            pe.wait_ge(s["wo_c"], 1)
            for l in range(DEPTH):
                for bank, g, signal in ((6, 2, "mups"), (4, 4, "vops")):
                    if l:
                        pe.wait_ge(s["mu_sb"], 4 * l - (2 if g == 2 else 0))
                    for hd in range(HEADS):
                        r = slice(64 * (hd % 2), 64 * (hd % 2) + 64)
                        right = wT[r, l, hd // 2, :] if g == 2 else wo[r, 2 * l + hd // 2, :]
                        for f in range(2):
                            mm = pe.matmul(ps[64 * f:64 * f + 64, bank + hd % 2, hd // 2 * 64:hd // 2 * 64 + 64], wT[r, l, g + hd // 2, :],
                                           right, start=True, stop=True)
                    mm.then_inc(s[signal], 1)
            pe.wait_ge(s["mu_sb"], 4 * DEPTH)
            pe.wait_ge(s["par_in"], 16 * PAR_LOADS)
            pe.wait_ge(s["wp_b"], 1)
            for f in range(2):
                pe.matmul(ps[64 * f:64 * f + 64, 7, 64:65], wred[:, 2 * DIM:3 * DIM], ones[0:KP, 0:1], start=True, stop=True)
            pe.matmul(ps[:, 7, 84:84 + DEPTH], cen_bd[:, :], lay[:, BO, :], start=True, stop=True)
            pe.matmul(ps[:, 7, 88:88 + DEPTH], cen_bd[:, :], lay[:, B2, :], start=True, stop=True)
            pe.matmul(ps[:, 7, 96:97], cen_bd[:, :], col[:, FB2:FB2 + 1], start=True, stop=True)
            for l in range(DEPTH):
                mm = pe.matmul(ps[:, 7, 92 + l:93 + l], w1[0:64, l, :], lay[0:64, BF, l:l + 1], start=True, stop=True)
            mm.then_inc(s["bias_ps"], 1)
            with pe.Fori(1, NCH // 2) as i:
                products(i, 0, lambda: statistics(i, -1))
                products(i, 1, lambda: statistics(i, 0))
            statistics(NCH // 2 - 1, 1)
            for half in range(2):
                pe.wait_ge(s["p_yb"], half + 1)
                pe.wait_ge(s["y_out"], NCH)
                pe.matmul(ps[:, half, :], cen_bd[:, :], py[:, 512 * half:512 * half + 512], start=True, stop=True).then_inc(s["p_cen"], 1)
            for half in range(2):
                pe.wait_ge(s["p_sq"], half + 1)
                pe.wait_ge(s["st_out"], NCH)
                pe.matmul(ps[:, 2 + half, :], ones_bd[:, :], pm2[:, 512 * half:512 * half + 512], start=True, stop=True).then_inc(s["p_v2"], 1)

            def centre_tokens(c):
                pe.wait_ge(s["x0"], c // 4 + 1)
                if c >= 2:
                    pe.wait_ge(s["ff"], c - 1)
                pe.matmul(ps_y(c), cen_bd[:, :], x0[:, c * CP:(c + 1) * CP, :].rearrange("p m t -> p (m t)"),
                          start=True, stop=True).then_inc(s["cen"], 1)

            def stream_variance(c, count):
                pe.wait_ge(s["sq"], count + (c + 1))
                if c >= 2:
                    pe.wait_ge(s["lnv"], count + (c - 1))
                pe.matmul(ps_w(c), ones_bd[:, :], chunk(sq, c), start=True, stop=True).then_inc(s["var"], 1)

            diagonal((0, centre_tokens), (2, lambda c: stream_variance(c, 0)))
            with pe.Fori(0, DEPTH) as l:
                def n(k):
                    return l * NCH + k

                def free(signal, c, each=1):
                    if c:
                        pe.wait_ge(s[signal], l * (NCH * each) + c * each)

                def keys(c):
                    pe.wait_ge(s["h"], n(c + 1))
                    if c == 0:
                        pe.wait_ge(s["slot_mu"], l * 16 + 16)
                    free("u", c)
                    for hd in range(HEADS):
                        mm = pe.matmul(ps_u[:, hd // 2, hd % 2 * CC:(hd % 2 + 1) * CC], mu[:, hd * 128:hd * 128 + 128], chunk(h, c),
                                       start=True, stop=True)
                    mm.then_inc(s["ups"], 1)

                def tokens(c):
                    pe.wait_ge(s["ha"], l * (2 * NCH) + 2 * (c + 1))
                    free("tk", c)
                    for i in range(4):
                        m = c * CP + 2 * i
                        mm = pe.transpose(ps_t[:, i * 128:i * 128 + 128], hbd[:, m:m + 2, :, :].rearrange("p j f k -> p (j f k)"), ident[:, :])
                    mm.then_inc(s["tps"], 1)

                def scores(c):
                    pe.wait_ge(s["u"], n(c + 1))
                    free("sub", c)
                    for j in range(2):
                        for i in range(4):
                            m = c * CP + 2 * i + j
                            mm = pe.matmul(ps_s[64 * j:64 * j + 64, i * HEADS * TOK:(i + 1) * HEADS * TOK],
                                           hbd[:, m, :, :].rearrange("p f k -> p (f k)"), U[:, :, m * TOK:(m + 1) * TOK], start=True, stop=True)
                    mm.then_inc(s["sc"], 1)

                def mixed(c):
                    pe.wait_ge(s["pt"], l * (2 * NCH) + 2 * (c + 1))
                    pe.wait_ge(s["tk"], n(c + 1))
                    free("ga", c, 2)
                    for i in range(4):
                        w = 2 * HEADS * TOK
                        mm = pe.matmul(ps_g[:, i // 2, i % 2 * w:(i % 2 + 1) * w], htok[:, 4 * c + i, :],
                                       pt[:, 4 * c + i, :, :].rearrange("p j (h q) -> p (j h) q", q=32)[:, :, 0:TOK], start=True, stop=True)
                    mm.then_inc(s["gps"], 1)

                def attention_out(c):
                    pe.wait_ge(s["ga"], l * (2 * NCH) + 2 * (c + 1))
                    if c == 0:
                        pe.wait_ge(s["slot_vo"], l * 16 + 16)
                    free("att", c)
                    for hd in range(HEADS):
                        mm = pe.matmul(ps_o, vo[:, hd * 128:hd * 128 + 128], G[:, hd, c * CP:(c + 1) * CP, :].rearrange("p m t -> p (m t)"),
                                       start=(hd == 0), stop=(hd == HEADS - 1))
                    mm.then_inc(s["ops"], 1)

                def mlp_variance(c):
                    pe.wait_ge(s["fsq"], n(c + 1))
                    free("fln", c)
                    pe.matmul(ps_v, ones_bd[:, :], chunk(sq, c), start=True, stop=True).then_inc(s["fvar"], 1)

                diagonal((1, keys), (1, tokens), (2, scores), (5, mixed), (6, attention_out), (7, mlp_variance))
                pe.wait_ge(s["slot_w1"], l * 16 + 16)
                for c in range(NCH):
                    pe.wait_ge(s["fn"], n(c + 1))
                    if c >= 2:
                        pe.wait_ge(s["z"], n(c - 1))
                    for f in range(2):
                        r = slice(64 * f, 64 * f + 64)
                        mm = pe.matmul(two_banks(c)[:, f, 0:CC], w1s[r, :], nrm[r, c * CC:(c + 1) * CC], start=True, stop=True)
                    mm.then_inc(s["zps"], 1)
                pe.wait_ge(s["slot_w2"], l * 16 + 16)

                def mlp_out(c):
                    pe.wait_ge(s["z"], n(c + 1))
                    if c >= 2:
                        pe.wait_ge(s["ff"], n(NCH + c - 1))
                    for f in range(2):
                        mm = pe.matmul(ps_y(c)[64 * f:64 * f + 64, :], w2s[:, :], z[:, f, c * CC:(c + 1) * CC], start=True, stop=True)
                    mm.then_inc(s["yps"], 1)

                diagonal((0, mlp_out), (2, lambda c: stream_variance(c, n(NCH))))
            final_pe(pe)

        @block.vector
        def _(dve):
            dve.wait_ge(s["w_in"], 48)
            dve.wait_ge(s["wp_bias"], 1)
            dve.tensor_tensor(wp[:, :, :], wp[:, :, :], gp[:, 0, :, None].to_broadcast([KP, P, DIM]), ALU.mult).then_inc(s["wp_a"], 1)
            dve.wait_ge(s["wp_a"], 1)
            dve.tensor_reduce(wred[:, 0:DIM], wp[:, :, :].rearrange("p k d -> p d k"), axis=AX.X, op=ALU.add).then_inc(s["wp_c"], 1)
            dve.wait_ge(s["colmean"], 1)
            dve.tensor_scalar(wred[:, DIM:2 * DIM], ps[0:KP, 7, 0:DIM], 1.0 / PD, None, ALU.mult).then_inc(s["wp_a"], 1)
            dve.wait_ge(s["wp_a"], 2)
            dve.tensor_tensor(wp[:, :, :], wp[:, :, :], wred[:, None, DIM:2 * DIM].to_broadcast([KP, P, DIM]), ALU.subtract).then_inc(s["wp_ready"], 1)

            def sums(i, u, between=None):
                after(dve, "patch_st", i * 2 + (u - 1))
                for q in range(4):
                    if between and q == 2:
                        between()
                    w = 4 * u + q + 1
                    dve.wait_ge(s["squares"], i * 8 + w)
                    dve.tensor_reduce(psq[:, u, q * 64:q * 64 + 64], sqp[:, q % 2, :].rearrange("p (n k) -> p n k", k=P),
                                      axis=AX.X, op=ALU.add).then_inc(s["sq_red"], 1)
                    dve.wait_ge(s["halves"], i * 8 + w)
                    dve.tensor_reduce(psm[:, u, q * 64:q * 64 + 64], half_sum[:, q % 2, :].rearrange("p (n k) -> p n k", k=P // 2),
                                      axis=AX.X, op=ALU.add).then_inc(s["sum_red"], 1)

            def leave_psum(i, u):
                dve.wait_ge(s["patch_mm"], i * 2 + (u + 1))
                dve.tensor_scalar(yraw[:, bass.ds(i * (2 * PC) + u * PC, PC)], ps[:, u % 2, 0:PC], 1.0, None, ALU.mult).then_inc(s["y_out"], 1)
                dve.wait_ge(s["patch_st"], i * 2 + (u + 1))
                dve.tensor_scalar(sraw[:, bass.ds(i * 2 + u, 1), :].rearrange("p o n -> p (o n)"), ps[:, 2 + u % 2, 0:2 * PC], 1.0 / PD,
                                  None, ALU.mult).then_inc(s["st_out"], 1)

            sums(0, 0)
            sums(0, 1, lambda: leave_psum(0, 0))
            dve.tensor_reduce(wred[:, 2 * DIM:3 * DIM], wtmp.rearrange("p k d -> p d k"), axis=AX.X, op=ALU.add).then_inc(s["wp_b"], 1)
            dve.wait_ge(s["par_in"], 16 * PAR_LOADS)
            dve.tensor_reduce(wo_r[:, :], wo, axis=AX.X, op=ALU.add).then_inc(s["wp_b"], 1)
            dve.tensor_reduce(w2_r[:, :], w2[:, :, :], axis=AX.X, op=ALU.add).then_inc(s["wp_b"], 1)
            dve.wait_ge(s["wp_b"], 3)
            dve.tensor_scalar(wo_r[:, :], wo_r[:, :], 1.0 / DIM, None, ALU.mult).then_inc(s["wp_b"], 1)
            dve.tensor_scalar(w2_r[:, :], w2_r[:, :], 1.0 / DIM, None, ALU.mult).then_inc(s["wp_b"], 1)
            dve.wait_ge(s["wp_b"], 5)
            dve.tensor_tensor(wo, wo, wo_r[:, :, None].to_broadcast([128, 2 * DEPTH, DIM]), ALU.subtract).then_inc(s["wo_c"], 1)
            dve.tensor_tensor(w2[:, :, :], w2[:, :, :], w2_r[:, :, None].to_broadcast([128, DEPTH, DIM]), ALU.subtract).then_inc(s["wp_b"], 1)
            dve.tensor_tensor(w1f[:, :, :], w1, lay[:, GF, :, None].to_broadcast([128, DEPTH, MLP]), ALU.mult).then_inc(s["wp_b"], 1)
            dve.wait_ge(s["wp_b"], 7)
            dve.tensor_copy(wo_r[:, :], wo_r[:, :]).then_inc(s["prep_ready"], 1)
            dve.wait_ge(s["bias_ps"], 1)
            dve.tensor_tensor(cst[:, 0:1], ps[:, 7, 64:65], col[:, B_PATCH:B_PATCH + 1], ALU.add).then_inc(s["cst_b"], 1)
            dve.tensor_copy(cst[:, 1:2], ps[:, 7, 96:97]).then_inc(s["cst_b"], 1)
            dve.tensor_copy(bo_c[:, :], ps[:, 7, 84:84 + DEPTH]).then_inc(s["cst_b"], 1)
            dve.tensor_copy(b2_c[:, :], ps[:, 7, 88:88 + DEPTH]).then_inc(s["cst_b"], 1)
            dve.tensor_tensor(b1_f[:, :], ps[:, 7, 92:92 + DEPTH], lay[:, B1, :], ALU.add).then_inc(s["prep_ready"], 1)
            dve.tensor_tensor(cst[:, 2:3], posT[:, 0:1], col[:, CLS:CLS + 1], ALU.add).then_inc(s["cls"], 1)
            with dve.Fori(1, NCH // 2) as i:
                sums(i, 0, lambda: leave_psum(i, -1))
                sums(i, 1, lambda: leave_psum(i, 0))
            dve.wait_ge(s["sum_red"], 4 * NCH)
            dve.wait_ge(s["cls"], 1)
            dve.tensor_copy(x0[:, :, 0:1], cst[:, None, 2:3].to_broadcast([128, NPAIR, 1])).then_inc(s["cls"], 1)
            dve.wait_ge(s["cst_b"], 4)
            for half in range(2):
                w = slice(512 * half, 512 * half + 512)
                if half:
                    leave_psum(NCH // 2 - 1, 1)
                dve.wait_ge(s["p_m2"], half + 1)
                dve.tensor_tensor(pvar[:, w].rearrange("p (k n) -> p k n", k=4), sraw[:, 4 * half:4 * half + 4, PC:2 * PC],
                                  pm2[:, w].rearrange("p (k n) -> p k n", k=4), ALU.subtract).then_inc(s["p_var"], 1)
                dve.wait_ge(s["p_rs"], half + 1)
                dve.tensor_tensor(py[:, w], yraw[:, w], prs[:, w], ALU.mult).then_inc(s["p_y"], 1)
                dve.wait_ge(s["p_y"], half + 1)
                dve.tensor_scalar(py[:, w], py[:, w], cst[:, 0:1], None, ALU.add).then_inc(s["p_yb"], 1)
            for half in range(2):
                w = slice(512 * half, 512 * half + 512)
                m = slice(32 * half, 32 * half + 32)
                dve.wait_ge(s["p_yc"], half + 1)
                dve.wait_ge(s["p_rs2"], half + 1)
                dve.tensor_tensor(py[:, w], py[:, w], prs[:, w], ALU.mult).then_inc(s["p_y"], 1)
                dve.wait_ge(s["p_y"], 2 * half + 3)
                dve.tensor_scalar(py[:, w], py[:, w], col[:, G2:G2 + 1], col[:, B2P:B2P + 1], ALU.mult, ALU.add).then_inc(s["p_y"], 1)
                dve.wait_ge(s["p_y"], 2 * half + 4)
                dve.wait_ge(s["cls"], 2)
                dve.tensor_tensor(x0[:, m, 1:TOK], py[:, w].rearrange("p (m t) -> p m t", m=32),
                                  posT[:, None, 1:TOK].to_broadcast([128, 32, NP]), ALU.add).then_inc(s["x0"], 1)

            with dve.Fori(0, DEPTH) as l:
                def n(k):
                    return l * NCH + k

                def normalised(c):
                    dve.wait_ge(s["rstd"], n(c + 1))
                    dve.tensor_tensor(chunk(nrm, c), chunk(x, c), chunk(rstd, c), ALU.mult).then_inc(s["nrm"], 1)
                    dve.wait_ge(s["nrm"], n(c + 1))
                    dve.tensor_scalar(chunk(h, c), chunk(nrm, c), lay[:, GA, bass.ds(l, 1)], lay[:, BA, bass.ds(l, 1)],
                                      ALU.mult, ALU.add).then_inc(s["h"], 1)

                def less_maximum(c):
                    g = slice(16 * c, 16 * c + 16)
                    sc = ps_s.rearrange("p (g k) -> p g k", k=TOK)
                    dve.wait_ge(s["sc"], n(c + 1))
                    dve.tensor_reduce(mx[:, g], sc, axis=AX.X, op=ALU.max).then_inc(s["mx"], 1)
                    dve.wait_ge(s["mx"], n(c + 1))
                    dve.tensor_tensor(ex[:, g, :], sc, mx[:, g, None].to_broadcast([128, 16, TOK]), ALU.subtract).then_inc(s["sub"], 1)

                def softmax_sum(c):
                    g = slice(16 * c, 16 * c + 16)
                    dve.wait_ge(s["ex"], n(c + 1))
                    dve.tensor_reduce(sm[:, g], ex[:, g, :], axis=AX.X, op=ALU.add).then_inc(s["sm"], 1)
                    dve.wait_ge(s["sm"], n(c + 1))
                    dve.reciprocal(ri[:, g], sm[:, g]).then_inc(s["ri"], 1)

                def transposed(c):
                    dve.wait_ge(s["pn"], n(c + 1))
                    if c == 0:
                        dve.wait_ge(s["pads"], 4)
                    for j in range(2):
                        r = slice(64 * j, 64 * j + 64)
                        dve.transpose(pt[r, 4 * c:4 * c + 4, j, :], pn[r, 16 * c:16 * c + 16, :].rearrange("p (i g) k -> p i (g k)", i=4)).then_inc(s["pt"], 1)

                def stream_attention(c):
                    dve.wait_ge(s["ops"], n(c + 1))
                    dve.scalar_tensor_tensor(out=chunk(x, c), in0=ps_o, scalar=bo_c[:, bass.ds(l, 1)], in1=chunk(x, c),
                                             op0=ALU.add, op1=ALU.add).then_inc(s["att"], 1)

                def mlp_normalised(c):
                    dve.wait_ge(s["frs"], n(c + 1))
                    dve.tensor_tensor(chunk(nrm, c), chunk(x, c), chunk(rstd, c), ALU.mult).then_inc(s["fn"], 1)

                diagonal((0, normalised), (2, less_maximum), (3, softmax_sum), (4, transposed), (6, stream_attention), (8, mlp_normalised))
                for c in range(NCH):
                    dve.wait_ge(s["yps"], n(c + 1))
                    dve.scalar_tensor_tensor(out=chunk(x, c), in0=ps_y(c), scalar=b2_c[:, bass.ds(l, 1)], in1=chunk(x, c),
                                             op0=ALU.add, op1=ALU.add).then_inc(s["ff"], 1)
            final_dve(dve)

        @block.gpsimd
        def _(pool):
            pool.memset(ident[:, :], 0.0).then_inc(s["cst_pool"], 1)
            pool.wait_ge(s["w_in"], 48)
            pool.tensor_tensor(wtmp, wp[:, :, :], gp[:, 1, :, None].to_broadcast([KP, P, DIM]), ALU.mult).then_inc(s["wp_bias"], 1)
            pool.memset(ones[:, :], 1.0).then_inc(s["ones_ok"], 1)
            pool.memset(ones_bd[:, :], 0.0).then_inc(s["cst_pool"], 1)
            pool.memset(eps5[:, :], 1e-5).then_inc(s["cst_pool"], 1)
            pool.memset(eps8[:, :], 1e-8).then_inc(s["cst_pool"], 1)
            pool.memset(mu_all[:, :, :], 0.0).then_inc(s["cst_pool"], 1)
            pool.memset(vo_all[:, :, :], 0.0).then_inc(s["cst_pool"], 1)
            pool.wait_ge(s["cst_pool"], 4)
            pool.affine_select(out=ident[:, :], in_=ident[:, :], compare_op=ALU.not_equal, fill=1.0, base=0,
                               pattern=[[-1, 128]], channel_multiplier=1).then_inc(s["ident_ok"], 1)
            done = 0
            for f in range(2):
                r = slice(64 * f, 64 * f + 64)
                for part_, value in ((ones_bd[r, r], 1.0 / DIM), (ones_q[r, f, :], 1.0 / DIM), (ones_q[r, 1 - f, :], 0.0)):
                    if done:
                        pool.wait_ge(s["cst_c"], done)
                    else:
                        pool.wait_ge(s["ident_ok"], 1)
                    pool.memset(part_, value).then_inc(s["cst_c"], 1)
                    done += 1
            pool.wait_ge(s["cst_c"], done)
            pool.tensor_tensor(cen_bd[:, :], ident[:, :], ones_bd[:, :], ALU.subtract).then_inc(s["ones_ok"], 1)
            pool.memset(wv[:, :], 0.0).then_inc(s["wv_zero"], 1)

            def two_chunks(i):
                for u in range(2):
                    pool.wait_ge(s[f"x_in{u}"], i * (16 * LOADS) + 16 * LOADS)
                    for q in range(4):
                        after(pool, "sum_red", i * 8 + (4 * u + q - 1))
                        v = xin[:, u, q // 2, 4 * (q % 2):4 * (q % 2) + 4, :].rearrange("p m (g k) -> p (m g) k", k=P)
                        pool.tensor_tensor(half_sum[:, q % 2, :].rearrange("p (n k) -> p n k", k=P // 2), v[:, :, 0:P // 2],
                                           v[:, :, P // 2:P], ALU.add).then_inc(s["halves"], 1)

            two_chunks(0)
            with pool.Fori(1, NCH // 2) as i:
                two_chunks(i)
            pool.memset(hbd[:, :, :, :], 0.0).then_inc(s["pads"], 1)
            pool.wait_ge(s["p_yb"], 2)
            pool.memset(pn[:, :, TOK:32], 0.0).then_inc(s["pads"], 1)
            pool.wait_ge(s["x0"], 2)
            for j in range(2):
                pool.wait_ge(s["pads"], 2 + j)
                pool.memset(pt[64 * j:64 * j + 64, :, 1 - j, :], 0.0).then_inc(s["pads"], 1)
            pool.wait_ge(s["pads"], 4)
            with pool.Fori(0, DEPTH) as l:
                for c in range(NCH):
                    g = slice(16 * c, 16 * c + 16)
                    pool.wait_ge(s["ri"], l * NCH + (c + 1))
                    pool.tensor_tensor(pn[:, g, 0:TOK], ex[:, g, :], ri[:, g, None].to_broadcast([128, 16, TOK]), ALU.mult).then_inc(s["pn"], 1)
            final_pool(pool)


_NAMES = {"x": "x", **{n: "L0_tok_" + n for n in ("ln_p1_g ln_p1_b W_patch b_patch ln_p2_g ln_p2_b cls pos attn_ln_g attn_ln_b Wqkv Wo "
                                               "bo ff_ln_g ff_ln_b W1 b1 W2 b2 ln_f_g ln_f_b").split()},
          **{n: "L0_attn_" + n for n in "Wq bq Wk bk Wv bv gamma beta".split()},
          "wr": "L0_ffn_wr", "br": "L0_ffn_br", "fw1": "L0_ffn_w1", "fb1": "L0_ffn_b1", "fw2": "L0_ffn_w2", "fb2": "L0_ffn_b2"}


def kernel(**inputs):
    import numpy as np
    import concourse.bacc as bacc
    from concourse.bass_utils import run_bass_kernel_spmd

    nc = bacc.Bacc("TRN2", target_bir_lowering=False, num_devices=1)
    arrays, args = {}, {}
    for short, name in _NAMES.items():
        v = np.ascontiguousarray(inputs[name])
        arrays["in_" + short] = v
        args[short] = nc.dram_tensor("in_" + short, v.shape, mybir.dt.from_np(v.dtype), kind="ExternalInput").ap()
    out = nc.dram_tensor("out", (B, TOK, DIM), f32, kind="ExternalOutput").ap()
    vit_tower(nc, args, out)
    return run_bass_kernel_spmd(nc, [arrays], core_ids=[0]).results[0]["out"]
```

```python
import concourse.bass as bass
from concourse import mybir
from contextlib import ExitStack

B, CH, IMG, P = 128, 3, 128, 32
GRID = IMG // P
NP = GRID * GRID
TOK = NP + 1
DIM, DEPTH, HEADS, MLP, UNITS, HID = 64, 4, 4, 128, 128, 256
PD = CH * P * P
KP = CH * P
NPAIR = B // 2
COLS = NPAIR * TOK
NCH = 8
CP = NPAIR // NCH
CC = CP * TOK
PC = CP * NP
KSEL = int(0.5 * TOK) - 1
NEG = -2.0 ** 32 + 1.0
LOADS = CH * GRID
FOLDED_ONCE = 1
PAR_LOADS = 30

f32 = mybir.dt.float32
ALU = mybir.AluOpType
ACT = mybir.ActivationFunctionType
AX = mybir.AxisListType


def vit_tower(nc, a, out):
    with ExitStack() as ctx:
        def sb(name, *shape):
            return ctx.enter_context(nc.sbuf_tensor(name, list(shape), f32))

        class Signals(dict):
            def __missing__(self, name):
                self[name] = ctx.enter_context(nc.semaphore("s_" + name))
                return self[name]

        s = Signals()

        ps = ctx.enter_context(nc.psum_tensor("ps", [128, 8, 512], f32))

        ident = sb("ident", 128, 128)
        ones = sb("ones", 128, 128)
        ones_bd = sb("ones_bd", 128, 128)
        cen_bd = sb("cen_bd", 128, 128)
        ones_q = sb("ones_q", 128, 2, 32)
        eps5 = sb("eps5", 128, 1)
        eps8 = sb("eps8", 128, 1)
        col = sb("col", 128, 12)
        B_PATCH, G2, B2P, CLS, FG, FB, GAMMA, BETA, BV, FB2, WR, BR = range(12)
        posT = sb("posT", 128, TOK)
        lay = sb("lay", 128, 7, DEPTH)
        GA, BA, GF, BF, BO, B2, B1 = range(7)
        bo_c = sb("bo_c", 128, DEPTH)
        b2_c = sb("b2_c", 128, DEPTH)
        b1_f = sb("b1_f", 128, DEPTH)
        cur = sb("cur", 128, 3)
        arena = sb("arena", 128, 16384)
        xin = arena[0:KP, :].rearrange("p (u f m w) -> p u f m w", u=2, f=2, m=CP)
        o = 0

        def part(n):
            nonlocal o
            o += n
            return arena[:, o - n:o]

        U = part(HEADS * COLS).rearrange("p (h n) -> p h n", h=HEADS)
        G = part(HEADS * COLS).rearrange("p (h m t) -> p h m t", h=HEADS, m=NPAIR)
        htok = part(32 * 128).rearrange("p (i c) -> p i c", i=32)
        h = part(COLS)
        sq = part(COLS)
        arena2 = sb("arena2", 128, 8192)
        sqp = arena2[0:KP, 0:4096].rearrange("p (u n) -> p u n", u=2)
        half_sum = arena2[0:KP, 4096:6144].rearrange("p (u n) -> p u n", u=2)
        wtmp = arena2[0:KP, 6144:8192].rearrange("p (k d) -> p k d", k=P)
        wgain = arena2[0:KP, 0:2048].rearrange("p (k d) -> p k d", k=P)
        ex = arena2[:, 0:2176].rearrange("p (g k) -> p g k", k=TOK)
        z = arena2[:, 2176:4352].rearrange("p (f n) -> p f n", f=2)
        x0 = z[:, 0, :].rearrange("p (m t) -> p m t", t=TOK)
        lnv = arena2[:, 4352:5440]
        rstd = arena2[:, 5440:6528]
        nrm = arena2[:, 6528:7616]
        wp = sb("wp", KP, P, DIM)
        gp = sb("gp", KP, 2, P)
        wred = sb("wred", KP, 3 * DIM)
        cst = sb("cst", 128, 4)
        x = sb("x", 128, COLS)
        pt = sb("pt", 128, 32, 2, HEADS * 32)
        pt_flat = pt[:, :, :, :].rearrange("p i j q -> p (i j q)")
        wqkv = pt_flat[0:64, 0:DEPTH * 768].rearrange("p (l g) -> p l g", l=DEPTH)
        wT = pt_flat[:, 3072:4608].rearrange("p (l g c) -> p l g c", l=DEPTH, g=6)
        wo = pt_flat[:, 4608:5120].rearrange("p (g d) -> p g d", d=DIM)
        w1 = pt_flat[:, 5120:5632].rearrange("p (l c) -> p l c", l=DEPTH)
        wo_r = sb("wo_r", 128, DEPTH * 2)
        w1f = sb("w1f", 128, DEPTH, MLP)
        w2 = sb("w2", 128, DEPTH, DIM)
        w2_r = sb("w2_r", 128, DEPTH)
        mu_all = sb("mu_all", 128, DEPTH, HEADS * 128)
        vo_all = sb("vo_all", 128, DEPTH, HEADS * 128)
        mu = sb("mu", 128, HEADS * 128)
        vo = sb("vo", 128, HEADS * 128)
        w1s = sb("w1s", 128, 2, MLP)
        w2s = sb("w2s", 128, DIM)
        hbd = sb("hbd", 128, NPAIR, 2, 32)
        mx = sb("mx", 128, 32 * HEADS)
        sm = sb("sm", 128, 32 * HEADS)
        ri = sb("ri", 128, 32 * HEADS)
        pn = sb("pn", 128, 32 * HEADS, 32)
        pn_flat = pn[:, :, :].rearrange("p a b -> p (a b)")
        yraw = pn_flat[:, 0:NCH * PC]
        sraw = pn_flat[:, NCH * PC:3 * NCH * PC].rearrange("p (k n) -> p k n", k=NCH)
        psq, psm = (pn_flat[0:KP, (3 + k // 2) * 1024 + k % 2 * 512:(3 + k // 2) * 1024 + k % 2 * 512 + 512].rearrange("p (u n) -> p u n", u=2)
                    for k in range(2))
        pm2, pvar, pln, prs, py = (pt_flat[:, 3072 + 1024 * k:4096 + 1024 * k] for k in range(5))
        wqk = sb("wqk", 128, 2, 2, UNITS)
        wv = sb("wv", 128, 128)
        fw1 = sb("fw1", 128, 2, HID)
        fw2 = sb("fw2", 128, 2, DIM)
        fw2_r = sb("fw2_r", 128, 2)
        fcol = sb("fcol", 128, 4)
        wrb = sb("wrb", 128, 128)
        gt = arena2[:, 576:576 + 2 * TOK * TOK].rearrange("p (w t o) -> p w t o", w=2, t=TOK)
        tri = arena2[:, 1216:1216 + TOK * TOK].rearrange("p (t o) -> p t o", t=TOK)
        wimg = sb("wimg", 128, TOK)
        rank = sb("rank", 128, TOK)
        FIN_LOADS = 14
        QC = CC // 2
        Q = arena[:, 0:2 * COLS].rearrange("p (f n) -> p f n", f=2)
        K = arena[:, 2 * COLS:4 * COLS].rearrange("p (f n) -> p f n", f=2)
        g_flat = arena[:, 4 * COLS:8 * COLS].rearrange("p (k n) -> p k n", k=4)
        nm, oo, hb, h1 = (g_flat[:, k, :] for k in range(4))
        wb = x
        selrow = z[:, 0, :]
        y_sel = z[:, 1, :]
        z2 = oo
        obuf = htok[0:QC, :, :].rearrange("p i c -> p (i c)")[:, 0:NCH * 256].rearrange("p (k n) -> p k n", k=NCH)

        def after(eng, signal, count):
            if not isinstance(count, int) or count > 0:
                eng.wait_ge(s[signal], count)

        def chunk(t, c):
            return t[:, c * CC:(c + 1) * CC]

        def pairs(t, c, r=slice(0, 128)):
            return t[r, c * CC:(c + 1) * CC].rearrange("p (m t) -> p m t", t=TOK)

        LAST = NCH // 2 - 1

        def ps_centred(half):
            return ps[:, (4, 0)[half], :]

        def ps_spread(half):
            return ps[:, (5, 1)[half], :]

        ps_u = ps[:, 0:2, 0:2 * CC]
        ps_t = ps[:, 2, :]
        ps_s = ps[:, 3, 0:4 * HEADS * TOK]
        ps_g = ps[:, 4:6, 0:4 * HEADS * TOK]
        ps_o = ps[:, 6, 0:CC]
        ps_v = ps[:, 7, 0:CC]

        def ps_z(c):
            return ps[:, c % 3, 0:2 * CC]

        THIRDS = -(-NCH // 3)

        def ps_var(c):
            return ps[:, (3, 6, 7)[c // 3], c % 3 * CC:(c % 3 + 1) * CC]

        def third(t, k):
            return t[:, 3 * k * CC:min(3 * (k + 1), NCH) * CC]

        def ps_third(k):
            return ps[:, (3, 6, 7)[k], 0:(min(3 * (k + 1), NCH) - 3 * k) * CC]

        def two_banks(c):
            return ps[:, 2 * (c % 2):2 * (c % 2) + 2, :]

        def ps_y(c):
            return ps[:, 4 + c % 2, 0:CC]

        def diagonal(*stages, steps=NCH):
            for t in range(steps + max(lag for lag, _ in stages)):
                for lag, stage in sorted(stages, key=lambda x: -x[0]):
                    if 0 <= t - lag < steps:
                        stage(t - lag)

        ps_qk = ps[:, 0:2, 0:2 * CC]
        ps_pv = ps[:, 4, :]
        ps_val = ps[:, 5, 0:CC]
        ps_key = ps[:, 6, 0:CC]
        score_cols = 4 * TOK

        WIDE = 2 * CC
        NW = NCH // 2

        def wide(t, g):
            return t[:, g * WIDE:(g + 1) * WIDE]

        def ps_oc(g):
            return ps[:, g % 2, 0:WIDE]

        def ps_ov(g):
            return ps[:, 2 + g % 2, 0:WIDE]

        def ps_rc(g):
            return ps[:, 4 + g % 2, 0:WIDE]

        ps_rv = ps[:, 6, 0:WIDE]
        ps_rw = ps[:, 7, 0:WIDE]

        def spread(c):
            return ps[:, c // 3, c % 3 * CC:(c % 3 + 1) * CC]

        def ps_zv(c):
            return ps[:, (3, 7, 6)[c // 3], c % 3 * CC:(c % 3 + 1) * CC]

        def ps_zv_third(k):
            return ps[:, (3, 7, 6)[k], 0:(min(3 * (k + 1), NCH) - 3 * k) * CC]

        ROW_BANKS = 5

        def row_bank(c):
            return (0, 1, 2, 4, 5)[c % ROW_BANKS]

        def final_sp(sp):
            sp.wait_ge(s["ws"], NW)
            for f in range(2):
                sp.dma_start(wimg[64 * f:64 * f + 64, :], wb[64 * f:64 * f + 1, :].rearrange("o (m t) -> o m t", t=TOK)).then_inc(s["sel_img"], 16)
            sp.wait_ge(s["selm"], 1)
            sp.wait_ge(s["sel_zero"], 1)
            for f in range(2):
                sp.dma_start(selrow[64 * f:64 * f + 1, :].rearrange("o (m t) -> o m t", t=TOK), wimg[64 * f:64 * f + 64, :]).then_inc(s["sel_row"], 16)
            for c in range(NCH):
                sp.wait_ge(s["oo"], c + 1)
                sp.dma_start(out[2 * CP * c:2 * CP * (c + 1), :, :].rearrange("(g m) t d -> (m t) g d", g=4),
                             obuf[:, c, :].rearrange("p (g d) -> p g d", g=4)).then_inc(s["out_done"], 16)
            sp.wait_ge(s["out_done"], 16 * NCH)

        def final_act(act):
            act.wait_ge(s["fin_in"], 16 * FIN_LOADS)

            def magnitude(c):
                act.wait_ge(s["dh"], c + 1)
                act.activation(chunk(sq, c), chunk(h, c), ACT.Abs).then_inc(s["ka"], 1)

            def biased(c):
                act.wait_ge(s["qps"], c + 1)
                act.activation(Q[:, :, c * CC:(c + 1) * CC], ps_qk[:, :, 0:CC], ACT.Identity, bias=fcol[:, 0:1]).then_inc(s["qa"], 1)
                act.activation(K[:, :, c * CC:(c + 1) * CC], ps_qk[:, :, CC:2 * CC], ACT.Identity, bias=fcol[:, 1:2]).then_inc(s["qa"], 1)
                act.wait_ge(s["vps"], c + 1)
                act.activation(chunk(nrm, c), ps_val, ACT.Identity, bias=col[:, BV:BV + 1]).then_inc(s["va"], 1)

            def values_out(c):
                act.wait_ge(s["vtp"], c + 1)
                act.activation(htok[:, 4 * c:4 * c + 4, :], ps_t.rearrange("p (i c) -> p i c", i=4), ACT.Copy).then_inc(s["vtk"], 1)

            def exponential(c):
                act.wait_ge(s["dsub"], c + 1)
                act.activation(ex[:, 4 * c:4 * c + 4, :], ex[:, 4 * c:4 * c + 4, :], ACT.Exp, scale=UNITS ** -0.5).then_inc(s["dex"], 1)

            diagonal((0, magnitude), (1, biased), (3, values_out), (3, exponential))

            def square(g, place, ready, squared):
                act.wait_ge(s[ready], g + 1)
                act.activation(wide(sq, g), place, ACT.Square).then_inc(s[squared], 1)

            def rstd_of(g, place, eps, var, ln, rs):
                act.wait_ge(s[var], g + 1)
                act.activation(wide(lnv, g), place, ACT.Ln, bias=eps).then_inc(s[ln], 1)
                act.wait_ge(s[ln], g + 1)
                act.activation(wide(rstd, g), wide(lnv, g), ACT.Exp, scale=-0.5).then_inc(s[rs], 1)

            diagonal((0, lambda g: square(g, ps_oc(g), "oc", "osq")), (1, lambda g: rstd_of(g, ps_ov(g), eps8[:, :], "ovar", "oln", "ors")),
                     (3, lambda g: square(g, ps_rc(g), "rc", "rsq")), (4, lambda g: rstd_of(g, ps_rv, eps5[:, :], "rvar", "rln", "rrs")),
                     steps=NW)

            def hidden(c):
                act.wait_ge(s["fz"], c + 1)
                for g in range(2):
                    act.activation(U[:, 2 * g:2 * g + 2, c * CC:(c + 1) * CC], two_banks(c)[:, :, g * CC:(g + 1) * CC], ACT.Gelu_apprx_tanh,
                                   bias=fcol[:, 2 + g:3 + g]).then_inc(s["fg"], 1)

            def mlp_out(c):
                act.wait_ge(s["fy"], c + 1)
                act.activation(chunk(y_sel, c), ps_y(c), ACT.Identity, bias=cst[:, 1:2]).then_inc(s["ysb"], 1)

            diagonal((0, hidden), (3, mlp_out))
            act.preload_act_table_set("natural_log_exp_and_others")

            def routed_square(c):
                act.wait_ge(s["z2"], c + 1)
                act.activation(chunk(sq, c), chunk(z2, c), ACT.Square).then_inc(s["zsq"], 1)

            def routed_rstd(k):
                act.wait_ge(s["zvar"], min(3 * (k + 1), NCH))
                act.activation(third(lnv, k), ps_zv_third(k), ACT.Ln, bias=eps5[:, :]).then_inc(s["zln"], 1)
                act.wait_ge(s["zln"], k + 1)
                act.activation(third(rstd, k), third(lnv, k), ACT.Exp, scale=-0.5).then_inc(s["zrs"], 1)

            def rows_out(c):
                act.wait_ge(s["ops2"], c + 1)
                act.activation(obuf[:, c, :].rearrange("p (f a d) -> p a f d", f=2, a=2),
                               ps[0:QC, row_bank(c), 0:256].rearrange("p (a f d) -> p a f d", a=2, f=2), ACT.Copy).then_inc(s["oo"], 1)

            for c in range(NCH):
                routed_square(c)
                if c in (4, 7):
                    routed_rstd(c // 3 - 1)
            rows_out(0)
            rows_out(1)
            routed_rstd(THIRDS - 1)
            for c in range(2, NCH):
                rows_out(c)

        def final_pe(pe):
            pe.wait_ge(s["fin_in"], 16 * FIN_LOADS)
            pe.wait_ge(s["lnv"], (DEPTH + 1) * THIRDS)

            def free(signal, c, each=1, places=1):
                if c >= places:
                    pe.wait_ge(s[signal], each * (c - places + 1))

            def project(c):
                pe.wait_ge(s["dh"], c + 1)
                free("qa", c, 2)
                for f in range(2):
                    for w in range(2):
                        mm = pe.matmul(ps_qk[:, f, w * CC:(w + 1) * CC], wqk[:, f, w, :], chunk(h, c), start=True, stop=True)
                mm.then_inc(s["qps"], 1)
                free("va", c)
                pe.matmul(ps_val, wv[:, :], chunk(h, c), start=True, stop=True).then_inc(s["vps"], 1)
                pe.wait_ge(s["ka"], c + 1)
                free("key", c)
                pe.matmul(ps_key, ones_bd[:, :], chunk(sq, c), start=True, stop=True).then_inc(s["kps"], 1)

            def attend(c):
                pe.wait_ge(s["leaky"], 4 * (c + 1))
                free("vtk", c)
                for i in range(4):
                    m = c * CP + 2 * i
                    mm = pe.transpose(ps_t[:, i * 128:i * 128 + 128], hbd[:, m:m + 2, :, :].rearrange("p j f k -> p (j f k)"), ident[:, :])
                mm.then_inc(s["vtp"], 1)
                pe.wait_ge(s["key"], c + 1)
                free("dsub", c)
                for j in range(2):
                    pe.matmul(ps[64 * j:64 * j + 64, 3, 0:score_cols], ones_q[:, :, :].rearrange("p f q -> p (f q)"),
                              nm[:, :].rearrange("p (m t) -> p m t", t=TOK)[:, c * CP + j:(c + 1) * CP:2, :], start=True, stop=False,
                              skip_group_check=True)
                    for f in range(2):
                        for i in range(4):
                            m = c * CP + 2 * i + j
                            r = 64 * j + 32 * f
                            mm = pe.matmul(ps[r:r + TOK, 3, i * TOK:(i + 1) * TOK], Q[:, f, m * TOK:(m + 1) * TOK],
                                           K[:, f, m * TOK:(m + 1) * TOK], start=False, stop=True, skip_group_check=True)
                mm.then_inc(s["dsc"], 1)

            def probabilities_by_values(c):
                pe.wait_ge(s["dpt"], 2 * (c + 1))
                pe.wait_ge(s["vtk"], c + 1)
                free("pvs", c)
                for i in range(4):
                    mm = pe.matmul(ps_pv[:, i * 128:i * 128 + 128], htok[:, 4 * c + i, :], pt[:, 4 * c + i, :, 0:64], start=True, stop=True)
                mm.then_inc(s["pv"], 1)

            diagonal((1, project), (3, attend), (6, probabilities_by_values))

            def centre_attended(g):
                pe.wait_ge(s["pvs"], 2 * (g + 1))
                free("on", g, 2, places=2)
                pe.matmul(ps_oc(g), cen_bd[:, :], wide(oo, g), start=True, stop=True).then_inc(s["oc"], 1)

            def variance_attended(g):
                pe.wait_ge(s["osq"], g + 1)
                free("oln", g, places=2)
                pe.matmul(ps_ov(g), ones_bd[:, :], wide(sq, g), start=True, stop=True).then_inc(s["ovar"], 1)

            def centre_sum(g):
                pe.wait_ge(s["on"], 2 * (g + 1))
                free("h1", g, places=2)
                pe.matmul(ps_rc(g), cen_bd[:, :], wide(nrm, g), start=True, stop=True).then_inc(s["rc"], 1)

            def variance_sum(g):
                pe.wait_ge(s["rsq"], g + 1)
                free("rln", g)
                pe.matmul(ps_rv, ones_bd[:, :], wide(sq, g), start=True, stop=True).then_inc(s["rvar"], 1)

            def routing_weight(g):
                pe.wait_ge(s["h1"], g + 1)
                if g == 0:
                    pe.wait_ge(s["wrb"], 1)
                free("ws", g)
                pe.matmul(ps_rw, wrb[:, :], wide(h1, g), start=True, stop=True).then_inc(s["wps"], 1)

            diagonal((0, centre_attended), (1, variance_attended), (3, centre_sum), (4, variance_sum), (6, routing_weight), steps=NW)

            def hidden(c):
                free("fg", c, 2, places=2)
                for f in range(2):
                    for g in range(2):
                        mm = pe.matmul(two_banks(c)[:, f, g * CC:(g + 1) * CC], fw1[:, f, g * 128:g * 128 + 128], chunk(h1, c),
                                       start=True, stop=True)
                mm.then_inc(s["fz"], 1)

            def mlp_out(c):
                if c == 0:
                    pe.wait_ge(s["fw2_c"], 3)
                pe.wait_ge(s["fg"], 2 * (c + 1))
                free("ysb", c, places=2)
                for f in range(2):
                    for g in range(2):
                        mm = pe.matmul(ps_y(c)[64 * f:64 * f + 64, :], fw2[:, g, :], U[:, 2 * g + f, c * CC:(c + 1) * CC],
                                       start=(g == 0), stop=(g == 1))
                mm.then_inc(s["fy"], 1)

            diagonal((0, hidden), (2, mlp_out))
            pe.wait_ge(s["sel_row"], 32)
            pe.wait_ge(s["ws"], NW)
            for k in range(3):
                w = slice(3 * k * CC, min(3 * (k + 1), NCH) * CC)
                pe.matmul(ps[:, k, 0:w.stop - w.start], ones_bd[:, :], selrow[:, w], start=True, stop=True).then_inc(s["selps"], 1)

            def variance_routed(c):
                pe.wait_ge(s["zsq"], c + 1)
                pe.matmul(ps_zv(c), ones_bd[:, :], chunk(sq, c), start=True, stop=True).then_inc(s["zvar"], 1)

            def rows(c):
                pe.wait_ge(s["zo"], c + 1)
                pe.wait_ge(s["y2"], NCH)
                free("oo", c, places=ROW_BANKS)
                for w in range(2):
                    mm = pe.transpose(ps[0:QC, row_bank(c), w * 128:w * 128 + 128], chunk(nrm, c)[:, w * QC:(w + 1) * QC], ident[:, :])
                mm.then_inc(s["ops2"], 1)

            for c in range(NCH):
                variance_routed(c)
            for c in range(NCH):
                rows(c)

        def final_dve(dve):
            dve.wait_ge(s["par_in"], 16 * PAR_LOADS)
            dve.tensor_scalar(wrb[:, :], ones_bd[:, :], col[:, WR:WR + 1], float(DIM), ALU.mult, ALU.mult).then_inc(s["wrb"], 1)

            def normalised(c):
                dve.wait_ge(s["rstd"], DEPTH * THIRDS + c // 3 + 1)
                dve.tensor_tensor(chunk(nrm, c), chunk(x, c), chunk(rstd, c), ALU.mult).then_inc(s["dn"], 1)
                dve.wait_ge(s["dn"], c + 1)
                dve.tensor_scalar(chunk(h, c), chunk(nrm, c), col[:, FG:FG + 1], col[:, FB:FB + 1], ALU.mult, ALU.add).then_inc(s["dh"], 1)

            def keys(c):
                dve.wait_ge(s["kps"], c + 1)
                dve.tensor_scalar(chunk(nm, c), ps_key, 0.0, NEG * UNITS ** 0.5, ALU.is_equal, ALU.mult).then_inc(s["key"], 1)

            def leaky(c):
                dve.wait_ge(s["qa"], 2 * (c + 1))
                for w in (Q, K):
                    v = w[:, :, c * CC:(c + 1) * CC]
                    dve.scalar_tensor_tensor(out=v, in0=v, scalar=0.2, in1=v, op0=ALU.mult, op1=ALU.max).then_inc(s["leaky"], 1)
                dve.wait_ge(s["va"], c + 1)
                for f in range(2):
                    v = pairs(nrm, c, slice(64 * f, 64 * f + 64))
                    dve.scalar_tensor_tensor(out=hbd[64 * f:64 * f + 64, c * CP:(c + 1) * CP, f, 0:TOK], in0=v, scalar=0.2, in1=v,
                                             op0=ALU.mult, op1=ALU.max).then_inc(s["leaky"], 1)

            def less_maximum(c):
                g = slice(4 * c, 4 * c + 4)
                sc = ps[:, 3, 0:score_cols].rearrange("p (g k) -> p g k", k=TOK)
                dve.wait_ge(s["dsc"], c + 1)
                dve.tensor_reduce(mx[:, g], sc, axis=AX.X, op=ALU.max).then_inc(s["dmx"], 1)
                dve.wait_ge(s["dmx"], c + 1)
                dve.tensor_tensor(ex[:, g, :], sc, mx[:, g, None].to_broadcast([128, 4, TOK]), ALU.subtract).then_inc(s["dsub"], 1)

            def softmax_sum(c):
                g = slice(4 * c, 4 * c + 4)
                dve.wait_ge(s["dex"], c + 1)
                dve.tensor_reduce(sm[:, g], ex[:, g, :], axis=AX.X, op=ALU.add).then_inc(s["dsm"], 1)
                dve.wait_ge(s["dsm"], c + 1)
                dve.reciprocal(ri[:, g], sm[:, g]).then_inc(s["dri"], 1)

            def transposed(c):
                dve.wait_ge(s["dpn"], c + 1)
                for j in range(2):
                    r = slice(64 * j, 64 * j + 64)
                    dve.transpose(pt[r, 4 * c:4 * c + 4, j, 0:32], pn[r, 4 * c:4 * c + 4, :]).then_inc(s["dpt"], 1)

            def attended(c):
                dve.wait_ge(s["pv"], c + 1)
                dve.tensor_tensor(pairs(oo, c), ps_pv.rearrange("p (m q) -> p m q", q=64)[:, :, 0:TOK], pairs(h, c), ALU.add).then_inc(s["pvs"], 1)

            diagonal((0, normalised), (1, keys), (2, leaky), (3, less_maximum), (4, softmax_sum), (5, transposed), (7, attended))

            def scaled(g):
                dve.wait_ge(s["ors"], g + 1)
                dve.scalar_tensor_tensor(out=wide(nrm, g), in0=ps_oc(g), scalar=col[:, GAMMA:GAMMA + 1], in1=wide(rstd, g),
                                         op0=ALU.mult, op1=ALU.mult).then_inc(s["on"], 1)
                dve.wait_ge(s["on"], 2 * g + 1)
                dve.wait_ge(s["hb"], 2 * (g + 1))
                dve.tensor_tensor(wide(nrm, g), wide(nrm, g), wide(hb, g), ALU.add).then_inc(s["on"], 1)

            def renormalised(g):
                dve.wait_ge(s["rrs"], g + 1)
                dve.tensor_tensor(wide(h1, g), ps_rc(g), wide(rstd, g), ALU.mult).then_inc(s["h1"], 1)

            def weight_out(g):
                dve.wait_ge(s["wps"], g + 1)
                dve.tensor_scalar(wide(wb, g), ps_rw, col[:, BR:BR + 1], float(DIM), ALU.add, ALU.mult).then_inc(s["ws"], 1)

            diagonal((2, scaled), (5, renormalised), (6, weight_out), steps=NW)
            dve.tensor_reduce(fw2_r[:, :], fw2[:, :, :], axis=AX.X, op=ALU.add).then_inc(s["fw2_c"], 1)
            dve.wait_ge(s["fw2_c"], 1)
            dve.tensor_scalar(fw2_r[:, :], fw2_r[:, :], 1.0 / DIM, None, ALU.mult).then_inc(s["fw2_c"], 1)
            dve.wait_ge(s["fw2_c"], 2)
            dve.tensor_tensor(fw2[:, :, :], fw2[:, :, :], fw2_r[:, :, None].to_broadcast([128, 2, DIM]), ALU.subtract).then_inc(s["fw2_c"], 1)
            dve.wait_ge(s["sel_img"], 32)
            heavier, same = gt[:, 0, :, :], gt[:, 1, :, :]
            mine, other = wimg[:, :, None].to_broadcast([128, TOK, TOK]), wimg[:, None, :].to_broadcast([128, TOK, TOK])
            dve.tensor_tensor(heavier, other, mine, ALU.is_gt).then_inc(s["compared"], 1)
            dve.tensor_tensor(same, other, mine, ALU.is_equal).then_inc(s["compared"], 1)
            dve.wait_ge(s["compared"], 2)
            dve.wait_ge(s["tri"], 2)
            dve.tensor_tensor(same, same, tri[:, :, :], ALU.mult).then_inc(s["compared"], 1)
            dve.wait_ge(s["compared"], 3)
            dve.tensor_tensor(heavier, heavier, same, ALU.add).then_inc(s["compared"], 1)
            dve.wait_ge(s["compared"], 4)
            dve.tensor_reduce(rank[:, :], heavier, axis=AX.X, op=ALU.add).then_inc(s["compared"], 1)
            dve.wait_ge(s["compared"], 5)
            dve.scalar_tensor_tensor(out=wimg[:, :], in0=rank[:, :], scalar=float(KSEL), in1=wimg[:, :], op0=ALU.is_lt, op1=ALU.mult).then_inc(s["selm"], 1)

            def routed(c):
                dve.wait_ge(s["selps"], c // 3 + 1)
                dve.wait_ge(s["ysb"], c + 1)
                dve.tensor_tensor(chunk(y_sel, c), spread(c), chunk(y_sel, c), ALU.mult).then_inc(s["y2"], 1)
                dve.wait_ge(s["y2"], c + 1)
                dve.scalar_tensor_tensor(out=chunk(z2, c), in0=chunk(h1, c), scalar=2.0, in1=chunk(y_sel, c), op0=ALU.mult, op1=ALU.add).then_inc(s["z2"], 1)

            def output(c):
                dve.wait_ge(s["zrs"], c // 3 + 1)
                dve.tensor_tensor(chunk(nrm, c), chunk(z2, c), chunk(rstd, c), ALU.mult).then_inc(s["zo"], 1)

            for c in range(NCH):
                routed(c)
            for c in range(NCH):
                output(c)

        def final_pool(pool):
            pool.memset(tri[:, :, :], 1.0).then_inc(s["tri"], 1)
            pool.wait_ge(s["tri"], 1)
            pool.affine_select(out=tri[:, :, :], in_=tri[:, :, :], compare_op=ALU.is_gt, fill=0.0, base=0,
                               pattern=[[1, TOK], [-1, TOK]], channel_multiplier=0).then_inc(s["tri"], 1)
            for c in range(NCH):
                pool.wait_ge(s["dri"], c + 1)
                g = slice(4 * c, 4 * c + 4)
                pool.tensor_tensor(pn[:, g, 0:TOK], ex[:, g, :], ri[:, g, None].to_broadcast([128, 4, TOK]), ALU.mult).then_inc(s["dpn"], 1)
                pool.tensor_scalar(chunk(hb, c), chunk(h, c), col[:, BETA:BETA + 1], None, ALU.add).then_inc(s["hb"], 1)
            pool.memset(selrow, 0.0).then_inc(s["sel_zero"], 1)

        block = ctx.enter_context(nc.Block())

        @block.sync
        def _(sp):
            sp.dma_start(wp[:, :, :], a["W_patch"].rearrange("(q k) d -> q k d", q=KP)).then_inc(s["w_in"], 16)
            sp.dma_start(gp[:, 0, :], a["ln_p1_g"].rearrange("(q k) -> q k", q=KP)).then_inc(s["w_in"], 16)
            sp.dma_start(gp[:, 1, :], a["ln_p1_b"].rearrange("(q k) -> q k", q=KP)).then_inc(s["w_in"], 16)

            def load(u, first):
                for c in range(CH):
                    for g in range(GRID):
                        img = a["x"][bass.ds(first, 2 * CP), c, g * P:(g + 1) * P, :]
                        sp.dma_start(xin[c * P:(c + 1) * P, u, :, :, g * IMG:(g + 1) * IMG].rearrange("p f m w -> p (f m) w"),
                                     img.rearrange("b r w -> r b w")).then_inc(s[f"x_in{u}"], 16)

            for u in range(2):
                load(u, u * (2 * CP))
            def both_halves(to, source, **kw):
                sp.dma_start(to, source[None].to_broadcast([2, DIM, 1]), **kw).then_inc(s["par_in"], 16)

            for n, j in (("b_patch", B_PATCH), ("ln_p2_g", G2), ("ln_p2_b", B2P), ("ln_f_g", FG), ("ln_f_b", FB),
                         ("gamma", GAMMA), ("beta", BETA), ("bv", BV), ("fb2", FB2)):
                both_halves(col[:, j:j + 1], a[n].rearrange("(d o) -> d o", o=1))
            both_halves(col[:, CLS:CLS + 1], a["cls"].rearrange("a b d -> d (a b)"), allow_slow_non_contiguous=True)
            both_halves(col[:, WR:WR + 1], a["wr"])
            sp.dma_start(col[:, BR:BR + 1], a["br"].rearrange("(o b) -> o b", o=1).to_broadcast([128, 1])).then_inc(s["par_in"], 16)
            for f in range(2):
                r = slice(64 * f, 64 * f + 64)
                sp.dma_start(posT[r, :], a["pos"].rearrange("a t d -> d (a t)"), allow_slow_non_contiguous=True).then_inc(s["par_in"], 16)
                sp.dma_start(w1[r, :, :], a["W1"].rearrange("l c d -> c l d")).then_inc(s["par_in"], 16)
                for n, j in (("attn_ln_g", GA), ("attn_ln_b", BA), ("ff_ln_g", GF), ("ff_ln_b", BF), ("bo", BO), ("b2", B2)):
                    sp.dma_start(lay[r, j, :], a[n].rearrange("l d -> d l"), allow_slow_non_contiguous=True).then_inc(s["par_in"], 16)
            sp.dma_start(lay[:, B1, :], a["b1"].rearrange("l d -> d l"), allow_slow_non_contiguous=True).then_inc(s["par_in"], 16)
            sp.dma_start(w2[:, :, :], a["W2"].rearrange("l c d -> c l d")).then_inc(s["par_in"], 16)
            with sp.Fori(1, NCH // 2) as i:
                for u in range(2):
                    first, products, parts = sp.snap(i * (4 * CP) + u * (2 * CP)), sp.snap(i * 2 + (u - 1)), sp.snap(i * 8 + 4 * (u - 1))
                    sp.wait_ge(s["patch_mm"], products)
                    sp.wait_ge(s["squares"], parts)
                    sp.wait_ge(s["halves"], parts)
                    load(u, first)
            sp.wait_ge(s["w_zero"], 4)
            for f in range(2):
                r = slice(64 * f, 64 * f + 64)
                sp.dma_start(wqk[r, f, 0, :], a["Wq"]).then_inc(s["fin_in"], 16)
                sp.dma_start(wqk[r, f, 1, :], a["Wk"]).then_inc(s["fin_in"], 16)
                sp.dma_start(wv[r, r], a["Wv"]).then_inc(s["fin_in"], 16)
                sp.dma_start(fw1[r, f, :], a["fw1"]).then_inc(s["fin_in"], 16)
                sp.dma_start(fcol[:, 2 + f:3 + f], a["fb1"][f * 128:f * 128 + 128].rearrange("(d o) -> d o", o=1)).then_inc(s["fin_in"], 16)
                sp.dma_start(fw2[:, f, :], a["fw2"][f * 128:f * 128 + 128, :]).then_inc(s["fin_in"], 16)
            sp.dma_start(fcol[:, 0:1], a["bq"].rearrange("(d o) -> d o", o=1)).then_inc(s["fin_in"], 16)
            sp.dma_start(fcol[:, 1:2], a["bk"].rearrange("(d o) -> d o", o=1)).then_inc(s["fin_in"], 16)
            sp.wait_ge(s["prep_ready"], 3)
            for l in range(DEPTH):
                sp.wait_ge(s["ups"], l * NCH)
                sp.dma_start(mu[:, :], mu_all[:, l, :]).then_inc(s["slot_mu"], 16)
                sp.wait_ge(s["ops"], l * NCH)
                sp.dma_start(vo[:, :], vo_all[:, l, :]).then_inc(s["slot_vo"], 16)
                sp.wait_ge(s["zps"], l * NCH)
                for f in range(2):
                    r = slice(64 * f, 64 * f + 64)
                    sp.dma_start(w1s[r, f, :], w1f[r, l, :]).then_inc(s["slot_w1"], 16)
                sp.wait_ge(s["yps"], l * NCH)
                sp.dma_start(w2s[:, :], w2[:, l, :]).then_inc(s["slot_w2"], 16)
            final_sp(sp)

        @block.scalar
        def _(act):
            act.dma_start(wqkv, a["Wqkv"].rearrange("l c d -> c l d")).then_inc(s["wq_in"], 16)
            act.dma_start(wo, a["Wo"].rearrange("l (g q) d -> q (l g) d", q=128)).then_inc(s["wo_in"], 16)

            def squares(i, u):
                act.wait_ge(s[f"x_in{u}"], i * (16 * LOADS) + 16 * LOADS)
                for q in range(4):
                    after(act, "sq_red", i * 8 + (4 * u + q - 1))
                    act.activation(sqp[:, q % 2, :].rearrange("p (m w) -> p m w", m=4),
                                   xin[:, u, q // 2, 4 * (q % 2):4 * (q % 2) + 4, :], ACT.Square).then_inc(s["squares"], 1)

            for l in range(DEPTH):
                act.wait_ge(s["qt"], l + 1)
                act.activation(wT[:, l, :, :], ps[:, 4 + l % 2, 0:384].rearrange("p (g c) -> p g c", g=6), ACT.Copy).then_inc(s["qt_sb"], 1)
            act.wait_ge(s["cst_pool"], 6)
            for l in range(DEPTH):
                for bank, to, signal, scale in ((6, mu_all, "mups", DIM ** -0.5), (4, vo_all, "vops", 1.0)):
                    act.wait_ge(s[signal], l + 1)
                    for f in range(2):
                        r = slice(64 * f, 64 * f + 64)
                        act.activation(to[r, l, :].rearrange("p (a b c) -> p b a c", b=2, c=128)[:, :, :, r],
                                       ps[r, bank:bank + 2, 0:128].rearrange("p b (a c) -> p b a c", a=2), ACT.Copy,
                                       scale=scale).then_inc(s["mu_sb"], 1)
            act.wait_ge(s["mu_sb"], 4 * DEPTH)
            act.activation(eps8[:, :], eps8[:, :], ACT.Copy).then_inc(s["prep_ready"], 1)
            act.wait_ge(s["wp_ready"], 1)
            squares(0, 0)
            squares(0, 1)
            with act.Fori(1, LAST) as i:
                squares(i, 0)
                squares(i, 1)
            act.preload_act_table_set("natural_log_exp_and_others")

            def half_cols(half):
                return slice(512 * half, 512 * half + 512)

            def patch_rstd(half, var, ready, ln, rs):
                w = half_cols(half)
                act.wait_ge(s[ready], half + 1)
                act.activation(pln[:, w], var, ACT.Ln, bias=eps5[:, :]).then_inc(s[ln], 1)
                act.wait_ge(s[ln], half + 1)
                act.activation(prs[:, w], pln[:, w], ACT.Exp, scale=-0.5).then_inc(s[rs], 1)

            def mean_square(half):
                act.wait_ge(s["st_out"], 4 * half + 4)
                act.activation(pm2[:, half_cols(half)].rearrange("p (k n) -> p k n", k=4), sraw[:, 4 * half:4 * half + 4, 0:PC], ACT.Square).then_inc(s["p_m2"], 1)
                patch_rstd(half, pvar[:, half_cols(half)], "p_var", "p_ln", "p_rs")

            def centred_out(half):
                act.wait_ge(s["p_cen"], half + 1)
                act.activation(pm2[:, half_cols(half)], ps_centred(half), ACT.Square).then_inc(s["p_sq"], 1)
                act.activation(py[:, half_cols(half)], ps_centred(half), ACT.Copy).then_inc(s["p_yc"], 1)

            def feature_rstd(half):
                patch_rstd(half, ps_spread(half), "p_v2", "p_ln2", "p_rs2")

            mean_square(0)
            squares(LAST, 0)
            squares(LAST, 1)
            centred_out(0)
            feature_rstd(0)

            def stream_square(c, count):
                act.wait_ge(s["ff"], count + (c + 1))
                act.activation(chunk(sq, c), chunk(x, c), ACT.Square).then_inc(s["sq"], 1)

            def stream_rstd(k, count, done):
                w = third(lnv, k)
                act.wait_ge(s["var"], count + min(3 * (k + 1), NCH))
                act.activation(w, ps_third(k), ACT.Ln, bias=eps5[:, :]).then_inc(s["lnv"], 1)
                act.wait_ge(s["lnv"], done + (k + 1))
                act.activation(third(rstd, k), w, ACT.Exp, scale=-0.5).then_inc(s["rstd"], 1)

            def embed_half(half):
                for g in range(2 * half, 2 * half + 2):
                    act.wait_ge(s["cen"], g + 1)
                    act.activation(wide(x, g), ps[:, 4 + g % 2, 0:WIDE], ACT.Copy).then_inc(s["ff"], 2)
                    act.wait_ge(s["ff"], 2 * (g + 1))
                    act.activation(wide(sq, g), wide(x, g), ACT.Square).then_inc(s["sq"], 2)

            mean_square(1)
            embed_half(0)
            centred_out(1)
            stream_rstd(0, 0, 0)
            feature_rstd(1)
            embed_half(1)
            act.wait_ge(s["prep_ready"], 3)
            with act.Fori(0, DEPTH) as l:
                def n(k):
                    return l * NCH + k

                act.activation(cur[:, 0:2], lay[:, GA:BA + 1, bass.ds(l, 1)].rearrange("p a o -> p (a o)"), ACT.Copy).then_inc(s["cur"], 1)
                act.activation(cur[:, 2:3], b1_f[:, bass.ds(l, 1)], ACT.Copy).then_inc(s["cur"], 1)

                def own_half(c):
                    act.wait_ge(s["nrm"], n(c + 1))
                    if c == 0:
                        act.wait_ge(s["cur"], l * 2 + 2)
                        act.wait_ge(s["pads"], 1)
                    for f in range(2):
                        r = slice(64 * f, 64 * f + 64)
                        act.activation(hbd[r, c * CP:(c + 1) * CP, f, 0:TOK], pairs(nrm, c, r), ACT.Identity,
                                       bias=cur[r, 1:2], scale=cur[r, 0:1]).then_inc(s["ha"], 1)
                    if c in (1, 4):
                        stream_rstd(c // 3 + 1, n(0), l * THIRDS)

                def u_out(c):
                    act.wait_ge(s["ups"], n(c + 1))
                    act.activation(U[:, :, c * CC:(c + 1) * CC].rearrange("p (a b) n -> p a b n", a=2),
                                   ps_u.rearrange("p a (b n) -> p a b n", b=2), ACT.Copy).then_inc(s["u"], 1)

                def tokens_out(c):
                    act.wait_ge(s["tps"], n(c + 1))
                    act.activation(htok[:, 4 * c:4 * c + 4, :], ps_t.rearrange("p (i c) -> p i c", i=4), ACT.Copy).then_inc(s["tk"], 1)

                def exponential(c):
                    act.wait_ge(s["sub"], n(c + 1))
                    act.activation(ex[:, 16 * c:16 * c + 16, :], ex[:, 16 * c:16 * c + 16, :], ACT.Exp).then_inc(s["ex"], 1)

                def g_out(c):
                    act.wait_ge(s["gps"], n(c + 1))
                    for b in range(2):
                        m = c * CP + 4 * b
                        act.activation(G[:, :, m:m + 4, :].rearrange("p h m q -> p m h q"),
                                       ps_g[:, b, :].rearrange("p (m h q) -> p m h q", m=4, h=HEADS), ACT.Copy).then_inc(s["ga"], 1)

                def mlp_square(c):
                    act.wait_ge(s["att"], n(c + 1))
                    act.activation(chunk(sq, c), chunk(x, c), ACT.Square).then_inc(s["fsq"], 1)

                def mlp_rstd(c):
                    act.wait_ge(s["fvar"], n(c + 1))
                    act.activation(chunk(lnv, c), ps_v, ACT.Ln, bias=eps5[:, :]).then_inc(s["fln"], 1)
                    act.wait_ge(s["fln"], n(c + 1))
                    act.activation(chunk(rstd, c), chunk(lnv, c), ACT.Exp, scale=-0.5).then_inc(s["frs"], 1)

                diagonal((0, own_half), (2, u_out), (2, tokens_out), (3, exponential), (6, g_out), (7, mlp_square), (8, mlp_rstd))

                def hidden(c):
                    act.wait_ge(s["zps"], n(c + 1))
                    act.activation(z[:, :, c * CC:(c + 1) * CC], ps_z(c).rearrange("p (f n) -> p f n", f=2), ACT.Gelu,
                                   bias=cur[:, 2:3]).then_inc(s["z"], 1)

                for c in range(NCH):
                    if c >= 4:
                        stream_square(c - 4, n(NCH))
                    hidden(c)
                act.preload_act_table_set("natural_log_exp_and_others")
                stream_rstd(0, n(NCH), l * THIRDS + THIRDS)
                for c in range(4, NCH):
                    stream_square(c, n(NCH))
                act.wait_ge(s["z"], n(NCH))
            for k in range(1, THIRDS):
                stream_rstd(k, DEPTH * NCH, DEPTH * THIRDS)
            final_act(act)

        @block.tensor
        def _(pe):
            def keep_warm(bank, steps):
                for _ in range(steps):
                    pe.matmul(ps[:, bank, 0:128], ident[:, :], ident[:, :], start=True, stop=True)

            pe.wait_ge(s["ident_ok"], 1)
            pe.wait_ge(s["wq_in"], 16)
            for l in range(DEPTH):
                if l >= 2:
                    pe.wait_ge(s["qt_sb"], l - 1)
                for g in range(6):
                    mm = pe.transpose(ps[:, 4 + l % 2, g * 64:g * 64 + 64], wqkv[:, l, g * 128:g * 128 + 128], ident[0:64, 0:64])
                mm.then_inc(s["qt"], 1)
            pe.wait_ge(s["qt_sb"], DEPTH)
            pe.wait_ge(s["wo_c"], 3)
            for l in range(DEPTH):
                for bank, g, signal in ((6, 2, "mups"), (4, 4, "vops")):
                    if l:
                        pe.wait_ge(s["mu_sb"], 4 * l - (2 if g == 2 else 0))
                    for hd in range(HEADS):
                        r = slice(64 * (hd % 2), 64 * (hd % 2) + 64)
                        right = wT[r, l, hd // 2, :] if g == 2 else wo[r, 2 * l + hd // 2, :]
                        for f in range(2):
                            mm = pe.matmul(ps[64 * f:64 * f + 64, bank + hd % 2, hd // 2 * 64:hd // 2 * 64 + 64], wT[r, l, g + hd // 2, :],
                                           right, start=True, stop=True)
                    mm.then_inc(s[signal], 1)
                if l == 1:
                    pe.wait_ge(s["ones_ok"], 2)
                    pe.wait_ge(s["wp_c"], 1)
                    pe.matmul(ps[0:KP, 0, 0:DIM], ones[0:KP, 0:KP], wred[:, 0:DIM], start=True, stop=True).then_inc(s["colmean"], 1)
            def products(i, u, between=None):
                pe.wait_ge(s[f"x_in{u}"], i * (16 * LOADS) + 16 * LOADS)
                after(pe, "y_out", i * 2 + (u - 1))
                for f in range(2):
                    if between and f == 1:
                        between()
                    for k in range(P):
                        mm = pe.matmul(ps[64 * f:64 * f + 64, u, 0:PC], wp[:, k, :],
                                       xin[:, u, f, :, :].rearrange("p m (g k) -> p (m g) k", k=P)[:, :, k],
                                       start=(k == 0), stop=(k == P - 1))
                mm.then_inc(s["patch_mm"], 1)

            def statistics(i, u):
                pe.wait_ge(s["sq_red"], i * 8 + 4 * (u + 1))
                pe.wait_ge(s["sum_red"], i * 8 + 4 * (u + 1))
                after(pe, "st_out", i * 2 + (u - 1))
                for f in range(2):
                    for w, part_sums in ((0, psm), (1, psq)):
                        mm = pe.matmul(ps[64 * f:64 * f + 64, 2 + u % 2, w * PC:(w + 1) * PC], ones[0:KP, 0:64],
                                       part_sums[:, u % 2, f * PC:(f + 1) * PC], start=True, stop=True)
                mm.then_inc(s["patch_st"], 1)

            pe.wait_ge(s["wp_ready"], 1)
            products(0, 0)
            products(0, 1, lambda: statistics(0, 0))
            with pe.Fori(1, LAST) as i:
                products(i, 0, lambda: statistics(i, -1))
                products(i, 1, lambda: statistics(i, 0))

            def centre_patches(half):
                pe.wait_ge(s["p_yb"], half + 1)
                pe.matmul(ps_centred(half), cen_bd[:, :], py[:, 512 * half:512 * half + 512], start=True, stop=True).then_inc(s["p_cen"], 1)

            def patch_variance(half):
                pe.wait_ge(s["p_sq"], half + 1)
                pe.matmul(ps_spread(half), ones_bd[:, :], pm2[:, 512 * half:512 * half + 512], start=True, stop=True).then_inc(s["p_v2"], 1)

            pe.wait_ge(s["mu_sb"], 4 * DEPTH)
            pe.wait_ge(s["par_in"], 16 * PAR_LOADS)
            pe.wait_ge(s["wp_b"], 1)
            for f in range(2):
                pe.matmul(ps[64 * f:64 * f + 64, 7, 64:65], wred[:, 2 * DIM:3 * DIM], ones[0:KP, 0:1], start=True, stop=True)
            pe.matmul(ps[:, 7, 84:84 + DEPTH], cen_bd[:, :], lay[:, BO, :], start=True, stop=True)
            pe.matmul(ps[:, 7, 88:88 + DEPTH], cen_bd[:, :], lay[:, B2, :], start=True, stop=True)
            pe.matmul(ps[:, 7, 96:97], cen_bd[:, :], col[:, FB2:FB2 + 1], start=True, stop=True)
            for l in range(DEPTH):
                mm = pe.matmul(ps[:, 7, 92 + l:93 + l], w1[0:64, l, :], lay[0:64, BF, l:l + 1], start=True, stop=True)
            mm.then_inc(s["bias_ps"], 1)
            products(LAST, 0, lambda: statistics(LAST, -1))
            centre_patches(0)
            products(LAST, 1, lambda: statistics(LAST, 0))
            patch_variance(0)
            statistics(LAST, 1)

            def centre_tokens(g):
                pe.wait_ge(s["x0"], g // 2 + 1)
                if g >= 2:
                    pe.wait_ge(s["ff"], 2 * (g - 1))
                pe.matmul(ps[:, 4 + g % 2, 0:WIDE], cen_bd[:, :], x0[:, 2 * g * CP:2 * (g + 1) * CP, :].rearrange("p m t -> p (m t)"),
                          start=True, stop=True).then_inc(s["cen"], 1)

            def stream_variance(c, count):
                pe.wait_ge(s["sq"], count + (c + 1))
                pe.matmul(ps_var(c), ones_bd[:, :], chunk(sq, c), start=True, stop=True).then_inc(s["var"], 1)

            pe.wait_ge(s["y_out"], NCH)
            pe.wait_ge(s["st_out"], NCH)
            keep_warm(0, 8)
            for g in range(NW // 2):
                centre_tokens(g)
            centre_patches(1)
            for c in range(4):
                stream_variance(c, 0)
            keep_warm(2, 4)
            patch_variance(1)
            keep_warm(2, 6)
            for g in range(NW // 2, NW):
                centre_tokens(g)
            for c in range(4, NCH):
                stream_variance(c, 0)
            with pe.Fori(0, DEPTH) as l:
                def n(k):
                    return l * NCH + k

                def free(signal, c, each=1):
                    if c:
                        pe.wait_ge(s[signal], l * (NCH * each) + c * each)

                def keys(c):
                    pe.wait_ge(s["h"], n(c + 1))
                    if c == 0:
                        pe.wait_ge(s["slot_mu"], l * 16 + 16)
                    free("u", c)
                    for hd in range(HEADS):
                        mm = pe.matmul(ps_u[:, hd // 2, hd % 2 * CC:(hd % 2 + 1) * CC], mu[:, hd * 128:hd * 128 + 128], chunk(h, c),
                                       start=True, stop=True)
                    mm.then_inc(s["ups"], 1)

                def tokens(c):
                    pe.wait_ge(s["ha"], l * (2 * NCH) + 2 * (c + 1))
                    free("tk", c)
                    for i in range(4):
                        m = c * CP + 2 * i
                        mm = pe.transpose(ps_t[:, i * 128:i * 128 + 128], hbd[:, m:m + 2, :, :].rearrange("p j f k -> p (j f k)"), ident[:, :])
                    mm.then_inc(s["tps"], 1)

                def scores(c):
                    pe.wait_ge(s["u"], n(c + 1))
                    free("sub", c)
                    for j in range(2):
                        for i in range(4):
                            m = c * CP + 2 * i + j
                            mm = pe.matmul(ps_s[64 * j:64 * j + 64, i * HEADS * TOK:(i + 1) * HEADS * TOK],
                                           hbd[:, m, :, :].rearrange("p f k -> p (f k)"), U[:, :, m * TOK:(m + 1) * TOK], start=True, stop=True)
                    mm.then_inc(s["sc"], 1)

                def mixed(c):
                    pe.wait_ge(s["pt"], l * (2 * NCH) + 2 * (c + 1))
                    pe.wait_ge(s["tk"], n(c + 1))
                    free("ga", c, 2)
                    for i in range(4):
                        w = 2 * HEADS * TOK
                        mm = pe.matmul(ps_g[:, i // 2, i % 2 * w:(i % 2 + 1) * w], htok[:, 4 * c + i, :],
                                       pt[:, 4 * c + i, :, :].rearrange("p j (h q) -> p (j h) q", q=32)[:, :, 0:TOK], start=True, stop=True)
                    mm.then_inc(s["gps"], 1)

                def attention_out(c):
                    pe.wait_ge(s["ga"], l * (2 * NCH) + 2 * (c + 1))
                    if c == 0:
                        pe.wait_ge(s["slot_vo"], l * 16 + 16)
                        pe.wait_ge(s["lnv"], l * THIRDS + 2)
                    free("att", c)
                    for hd in range(HEADS):
                        mm = pe.matmul(ps_o, vo[:, hd * 128:hd * 128 + 128], G[:, hd, c * CP:(c + 1) * CP, :].rearrange("p m t -> p (m t)"),
                                       start=(hd == 0), stop=(hd == HEADS - 1))
                    mm.then_inc(s["ops"], 1)

                def mlp_variance(c):
                    pe.wait_ge(s["fsq"], n(c + 1))
                    free("fln", c)
                    if c == 0:
                        pe.wait_ge(s["lnv"], l * THIRDS + THIRDS)
                    pe.matmul(ps_v, ones_bd[:, :], chunk(sq, c), start=True, stop=True).then_inc(s["fvar"], 1)

                def hidden(c):
                    pe.wait_ge(s["fn"], n(c + 1))
                    if c == 0:
                        pe.wait_ge(s["slot_w1"], l * 32 + 32)
                        pe.wait_ge(s["tk"], n(NCH))
                    if c >= 3:
                        pe.wait_ge(s["z"], n(c - 2))
                    for f in range(2):
                        mm = pe.matmul(ps_z(c)[:, f * CC:(f + 1) * CC], w1s[:, f, :], chunk(nrm, c), start=True, stop=True)
                    mm.then_inc(s["zps"], 1)

                def mlp_out(c):
                    if c == 0:
                        pe.wait_ge(s["slot_w2"], l * 16 + 16)
                    pe.wait_ge(s["z"], n(c + 1))
                    if c >= 2:
                        pe.wait_ge(s["ff"], n(NCH + c - 1))
                    for f in range(2):
                        mm = pe.matmul(ps_y(c)[64 * f:64 * f + 64, :], w2s[:, :], z[:, f, c * CC:(c + 1) * CC], start=True, stop=True)
                    mm.then_inc(s["yps"], 1)

                diagonal((2, keys), (2, tokens), (3, scores), (6, mixed), (7, attention_out), (8, mlp_variance),
                         (11, lambda c: hidden(c) if c < 3 else None))
                keep_warm(3, 14)
                diagonal((0, lambda c: hidden(c + 3) if c + 3 < NCH else None), (0, mlp_out), (5, lambda c: stream_variance(c, n(NCH))))
                keep_warm(0, 6)
            final_pe(pe)

        @block.vector
        def _(dve):
            dve.wait_ge(s["wo_in"], 16)
            dve.tensor_reduce(wo_r[:, :], wo, axis=AX.X, op=ALU.add).then_inc(s["wo_c"], 1)
            dve.wait_ge(s["wo_c"], 1)
            dve.tensor_scalar(wo_r[:, :], wo_r[:, :], 1.0 / DIM, None, ALU.mult).then_inc(s["wo_c"], 1)
            dve.wait_ge(s["wo_c"], 2)
            dve.tensor_tensor(wo, wo, wo_r[:, :, None].to_broadcast([128, 2 * DEPTH, DIM]), ALU.subtract).then_inc(s["wo_c"], 1)
            dve.wait_ge(s["w_in"], 48)
            dve.tensor_tensor(wgain, wp[:, :, :], gp[:, 0, :, None].to_broadcast([KP, P, DIM]), ALU.mult).then_inc(s["wp_a"], 1)
            dve.wait_ge(s["wp_a"], 1)
            dve.tensor_reduce(wred[:, 0:DIM], wgain.rearrange("p k d -> p d k"), axis=AX.X, op=ALU.add).then_inc(s["wp_c"], 1)
            dve.wait_ge(s["colmean"], 1)
            dve.tensor_scalar(wred[:, DIM:2 * DIM], ps[0:KP, 0, 0:DIM], 1.0 / PD, None, ALU.mult).then_inc(s["wp_a"], 1)
            dve.wait_ge(s["wp_a"], 2)
            dve.wait_ge(s["wp_bias"], 1)
            dve.tensor_tensor(wp[:, :, :], wgain, wred[:, None, DIM:2 * DIM].to_broadcast([KP, P, DIM]), ALU.subtract).then_inc(s["wp_ready"], 1)

            def sums(i, u, between=None):
                after(dve, "patch_st", i * 2 + (u - 1))
                for q in range(4):
                    if between and q == 2:
                        between()
                    w = 4 * u + q + 1
                    dve.wait_ge(s["squares"], i * 8 + w)
                    dve.tensor_reduce(psq[:, u, q * 64:q * 64 + 64], sqp[:, q % 2, :].rearrange("p (n k) -> p n k", k=P),
                                      axis=AX.X, op=ALU.add).then_inc(s["sq_red"], 1)
                    dve.wait_ge(s["halves"], i * 8 + w)
                    dve.tensor_reduce(psm[:, u, q * 64:q * 64 + 64],
                                      half_sum[:, q % 2, :].rearrange("p (n k) -> p n k", k=P // 2)[:, :, 0:P // 2 if q < FOLDED_ONCE else P // 4],
                                      axis=AX.X, op=ALU.add).then_inc(s["sum_red"], 1)

            def leave_psum(i, u):
                dve.wait_ge(s["patch_mm"], i * 2 + (u + 1))
                dve.tensor_scalar(yraw[:, bass.ds(i * (2 * PC) + u * PC, PC)], ps[:, u % 2, 0:PC], 1.0, None, ALU.mult).then_inc(s["y_out"], 1)
                dve.wait_ge(s["patch_st"], i * 2 + (u + 1))
                dve.tensor_scalar(sraw[:, bass.ds(i * 2 + u, 1), :].rearrange("p o n -> p (o n)"), ps[:, 2 + u % 2, 0:2 * PC], 1.0 / PD,
                                  None, ALU.mult).then_inc(s["st_out"], 1)

            sums(0, 0)
            sums(0, 1, lambda: leave_psum(0, 0))
            dve.tensor_reduce(wred[:, 2 * DIM:3 * DIM], wtmp.rearrange("p k d -> p d k"), axis=AX.X, op=ALU.add).then_inc(s["wp_b"], 1)
            dve.wait_ge(s["par_in"], 16 * PAR_LOADS)
            dve.tensor_reduce(w2_r[:, :], w2[:, :, :], axis=AX.X, op=ALU.add).then_inc(s["wp_b"], 1)
            dve.wait_ge(s["wp_b"], 2)
            dve.tensor_scalar(w2_r[:, :], w2_r[:, :], 1.0 / DIM, None, ALU.mult).then_inc(s["wp_b"], 1)
            dve.wait_ge(s["wp_b"], 3)
            dve.tensor_tensor(w2[:, :, :], w2[:, :, :], w2_r[:, :, None].to_broadcast([128, DEPTH, DIM]), ALU.subtract).then_inc(s["wp_b"], 1)
            dve.tensor_tensor(w1f[:, :, :], w1, lay[:, GF, :, None].to_broadcast([128, DEPTH, MLP]), ALU.mult).then_inc(s["wp_b"], 1)
            dve.wait_ge(s["wp_b"], 5)
            dve.tensor_copy(wo_r[:, :], wo_r[:, :]).then_inc(s["prep_ready"], 1)
            with dve.Fori(1, LAST) as i:
                sums(i, 0, lambda: leave_psum(i, -1))
                sums(i, 1, lambda: leave_psum(i, 0))

            def half_cols(half):
                return slice(512 * half, 512 * half + 512)

            def patch_variance(half):
                w = half_cols(half)
                dve.wait_ge(s["p_m2"], half + 1)
                dve.tensor_tensor(pvar[:, w].rearrange("p (k n) -> p k n", k=4), sraw[:, 4 * half:4 * half + 4, PC:2 * PC],
                                  pm2[:, w].rearrange("p (k n) -> p k n", k=4), ALU.subtract).then_inc(s["p_var"], 1)

            def patch_normalised(half):
                w = half_cols(half)
                dve.wait_ge(s["p_rs"], half + 1)
                dve.tensor_tensor(py[:, w], yraw[:, w], prs[:, w], ALU.mult).then_inc(s["p_y"], 1)
                dve.wait_ge(s["p_y"], 3 * half + 1)
                dve.tensor_scalar(py[:, w], py[:, w], cst[:, 0:1], None, ALU.add).then_inc(s["p_yb"], 1)

            def tokens_made(half):
                w = half_cols(half)
                m = slice(32 * half, 32 * half + 32)
                dve.wait_ge(s["p_yc"], half + 1)
                dve.wait_ge(s["p_rs2"], half + 1)
                dve.tensor_tensor(py[:, w], py[:, w], prs[:, w], ALU.mult).then_inc(s["p_y"], 1)
                dve.wait_ge(s["p_y"], 3 * half + 2)
                dve.tensor_scalar(py[:, w], py[:, w], col[:, G2:G2 + 1], col[:, B2P:B2P + 1], ALU.mult, ALU.add).then_inc(s["p_y"], 1)
                dve.wait_ge(s["p_y"], 3 * half + 3)
                dve.tensor_tensor(x0[:, m, 1:TOK], py[:, w].rearrange("p (m t) -> p m t", m=32),
                                  posT[:, None, 1:TOK].to_broadcast([128, 32, NP]), ALU.add).then_inc(s["x0"], 1)

            def first_between():
                leave_psum(LAST, -1)
                patch_normalised(0)

            dve.wait_ge(s["bias_ps"], 1)
            dve.tensor_tensor(cst[:, 0:1], ps[:, 7, 64:65], col[:, B_PATCH:B_PATCH + 1], ALU.add).then_inc(s["cst_b"], 1)
            dve.tensor_copy(cst[:, 1:2], ps[:, 7, 96:97]).then_inc(s["cst_b"], 1)
            dve.tensor_copy(bo_c[:, :], ps[:, 7, 84:84 + DEPTH]).then_inc(s["cst_b"], 1)
            dve.tensor_copy(b2_c[:, :], ps[:, 7, 88:88 + DEPTH]).then_inc(s["cst_b"], 1)
            dve.tensor_tensor(b1_f[:, :], ps[:, 7, 92:92 + DEPTH], lay[:, B1, :], ALU.add).then_inc(s["prep_ready"], 1)
            dve.tensor_tensor(cst[:, 2:3], posT[:, 0:1], col[:, CLS:CLS + 1], ALU.add).then_inc(s["cls"], 1)
            dve.wait_ge(s["cst_b"], 4)
            patch_variance(0)
            sums(LAST, 0, first_between)
            sums(LAST, 1, lambda: leave_psum(LAST, 0))
            dve.wait_ge(s["sum_red"], 4 * NCH)
            dve.wait_ge(s["cls"], 1)
            dve.tensor_copy(x0[:, :, 0:1], cst[:, None, 2:3].to_broadcast([128, NPAIR, 1])).then_inc(s["cls"], 1)
            dve.wait_ge(s["cls"], 2)
            leave_psum(LAST, 1)
            patch_variance(1)
            tokens_made(0)
            patch_normalised(1)
            tokens_made(1)

            with dve.Fori(0, DEPTH) as l:
                def n(k):
                    return l * NCH + k

                def normalised(c):
                    dve.wait_ge(s["rstd"], l * THIRDS + (c // 3 + 1))
                    dve.tensor_tensor(chunk(nrm, c), chunk(x, c), chunk(rstd, c), ALU.mult).then_inc(s["nrm"], 1)
                    dve.wait_ge(s["nrm"], n(c + 1))
                    dve.tensor_scalar(chunk(h, c), chunk(nrm, c), lay[:, GA, bass.ds(l, 1)], lay[:, BA, bass.ds(l, 1)],
                                      ALU.mult, ALU.add).then_inc(s["h"], 1)

                def less_maximum(c):
                    g = slice(16 * c, 16 * c + 16)
                    sc = ps_s.rearrange("p (g k) -> p g k", k=TOK)
                    dve.wait_ge(s["sc"], n(c + 1))
                    dve.tensor_reduce(mx[:, g], sc, axis=AX.X, op=ALU.max).then_inc(s["mx"], 1)
                    dve.wait_ge(s["mx"], n(c + 1))
                    dve.tensor_tensor(ex[:, g, :], sc, mx[:, g, None].to_broadcast([128, 16, TOK]), ALU.subtract).then_inc(s["sub"], 1)

                def softmax_sum(c):
                    g = slice(16 * c, 16 * c + 16)
                    dve.wait_ge(s["ex"], n(c + 1))
                    dve.tensor_reduce(sm[:, g], ex[:, g, :], axis=AX.X, op=ALU.add).then_inc(s["sm"], 1)
                    dve.wait_ge(s["sm"], n(c + 1))
                    dve.reciprocal(ri[:, g], sm[:, g]).then_inc(s["ri"], 1)

                def transposed(c):
                    dve.wait_ge(s["pn"], n(c + 1))
                    if c == 0:
                        dve.wait_ge(s["pads"], 4)
                    for j in range(2):
                        r = slice(64 * j, 64 * j + 64)
                        dve.transpose(pt[r, 4 * c:4 * c + 4, j, :], pn[r, 16 * c:16 * c + 16, :].rearrange("p (i g) k -> p i (g k)", i=4)).then_inc(s["pt"], 1)

                def stream_attention(c):
                    dve.wait_ge(s["ops"], n(c + 1))
                    dve.scalar_tensor_tensor(out=chunk(x, c), in0=ps_o, scalar=bo_c[:, bass.ds(l, 1)], in1=chunk(x, c),
                                             op0=ALU.add, op1=ALU.add).then_inc(s["att"], 1)

                def mlp_normalised(c):
                    dve.wait_ge(s["frs"], n(c + 1))
                    dve.tensor_tensor(chunk(nrm, c), chunk(x, c), chunk(rstd, c), ALU.mult).then_inc(s["fn"], 1)

                diagonal((0, normalised), (3, less_maximum), (4, softmax_sum), (5, transposed), (7, stream_attention), (9, mlp_normalised))
                for c in range(NCH):
                    dve.wait_ge(s["yps"], n(c + 1))
                    dve.scalar_tensor_tensor(out=chunk(x, c), in0=ps_y(c), scalar=b2_c[:, bass.ds(l, 1)], in1=chunk(x, c),
                                             op0=ALU.add, op1=ALU.add).then_inc(s["ff"], 1)
            final_dve(dve)

        @block.gpsimd
        def _(pool):
            pool.memset(ident[:, :], 0.0).then_inc(s["cst_pool"], 1)
            pool.memset(ones[:, :], 1.0).then_inc(s["ones_ok"], 1)
            pool.memset(ones_bd[:, :], 0.0).then_inc(s["cst_pool"], 1)
            pool.memset(eps5[:, :], 1e-5).then_inc(s["cst_pool"], 1)
            pool.memset(eps8[:, :], 1e-8).then_inc(s["cst_pool"], 1)
            pool.wait_ge(s["cst_pool"], 4)
            pool.affine_select(out=ident[:, :], in_=ident[:, :], compare_op=ALU.not_equal, fill=1.0, base=0,
                               pattern=[[-1, 128]], channel_multiplier=1).then_inc(s["ident_ok"], 1)
            pool.memset(mu_all[:, :, :], 0.0).then_inc(s["cst_pool"], 1)
            pool.memset(vo_all[:, :, :], 0.0).then_inc(s["cst_pool"], 1)
            pool.wait_ge(s["w_in"], 48)
            pool.wait_ge(s["cst_pool"], 6)
            pool.tensor_tensor(wtmp, wp[:, :, :], gp[:, 1, :, None].to_broadcast([KP, P, DIM]), ALU.mult).then_inc(s["wp_bias"], 1)
            done = 0
            for f in range(2):
                r = slice(64 * f, 64 * f + 64)
                for part_, value in ((ones_bd[r, r], 1.0 / DIM), (ones_q[r, f, :], 1.0 / DIM), (ones_q[r, 1 - f, :], 0.0)):
                    if done:
                        pool.wait_ge(s["cst_c"], done)
                    else:
                        pool.wait_ge(s["ident_ok"], 1)
                    pool.memset(part_, value).then_inc(s["cst_c"], 1)
                    done += 1
            pool.wait_ge(s["cst_c"], done)
            pool.tensor_tensor(cen_bd[:, :], ident[:, :], ones_bd[:, :], ALU.subtract).then_inc(s["ones_ok"], 1)
            for zero in (wv[:, :], wqk[:, :, :, :], fw1[:, :, :], w1s[:, :, :]):
                pool.memset(zero, 0.0).then_inc(s["w_zero"], 1)

            def two_chunks(i):
                for u in range(2):
                    pool.wait_ge(s[f"x_in{u}"], i * (16 * LOADS) + 16 * LOADS)
                    for q in range(4):
                        after(pool, "sum_red", i * 8 + (4 * u + q - 1))
                        v = xin[:, u, q // 2, 4 * (q % 2):4 * (q % 2) + 4, :].rearrange("p m (g k) -> p (m g) k", k=P)
                        sums = half_sum[:, q % 2, :].rearrange("p (n k) -> p n k", k=P // 2)
                        once = q < FOLDED_ONCE
                        pool.tensor_tensor(sums, v[:, :, 0:P // 2], v[:, :, P // 2:P], ALU.add).then_inc(s["halves" if once else "folded"], 1)
                        if not once:
                            pool.wait_ge(s["folded"], i * (2 * (4 - FOLDED_ONCE)) + ((4 - FOLDED_ONCE) * u + q - FOLDED_ONCE + 1))
                            pool.tensor_tensor(sums[:, :, 0:P // 4], sums[:, :, 0:P // 4], sums[:, :, P // 4:P // 2], ALU.add).then_inc(s["halves"], 1)

            two_chunks(0)
            with pool.Fori(1, NCH // 2) as i:
                two_chunks(i)
            pool.memset(hbd[:, :, :, :], 0.0).then_inc(s["pads"], 1)
            pool.wait_ge(s["p_yb"], 2)
            pool.memset(pn[:, :, TOK:32], 0.0).then_inc(s["pads"], 1)
            pool.wait_ge(s["x0"], 2)
            for j in range(2):
                pool.wait_ge(s["pads"], 2 + j)
                pool.memset(pt[64 * j:64 * j + 64, :, 1 - j, :], 0.0).then_inc(s["pads"], 1)
            pool.wait_ge(s["pads"], 4)
            with pool.Fori(0, DEPTH) as l:
                for c in range(NCH):
                    g = slice(16 * c, 16 * c + 16)
                    pool.wait_ge(s["ri"], l * NCH + (c + 1))
                    pool.tensor_tensor(pn[:, g, 0:TOK], ex[:, g, :], ri[:, g, None].to_broadcast([128, 16, TOK]), ALU.mult).then_inc(s["pn"], 1)
            final_pool(pool)


_NAMES = {"x": "x", **{n: "L0_tok_" + n for n in ("ln_p1_g ln_p1_b W_patch b_patch ln_p2_g ln_p2_b cls pos attn_ln_g attn_ln_b Wqkv Wo "
                                               "bo ff_ln_g ff_ln_b W1 b1 W2 b2 ln_f_g ln_f_b").split()},
          **{n: "L0_attn_" + n for n in "Wq bq Wk bk Wv bv gamma beta".split()},
          "wr": "L0_ffn_wr", "br": "L0_ffn_br", "fw1": "L0_ffn_w1", "fb1": "L0_ffn_b1", "fw2": "L0_ffn_w2", "fb2": "L0_ffn_b2"}


def kernel(**inputs):
    import numpy as np
    import concourse.bacc as bacc
    from concourse.bass_utils import run_bass_kernel_spmd

    nc = bacc.Bacc("TRN2", target_bir_lowering=False, num_devices=1)
    arrays, args = {}, {}
    for short, name in _NAMES.items():
        v = np.ascontiguousarray(inputs[name])
        arrays["in_" + short] = v
        args[short] = nc.dram_tensor("in_" + short, v.shape, mybir.dt.from_np(v.dtype), kind="ExternalInput").ap()
    out = nc.dram_tensor("out", (B, TOK, DIM), f32, kind="ExternalOutput").ap()
    vit_tower(nc, args, out)
    return run_bass_kernel_spmd(nc, [arrays], core_ids=[0]).results[0]["out"]
```
